# Optimizing a Trainium2 kernel written in Bass

```python
import numpy as np
import jax
import jax.numpy as jnp

def _softmax(x, axis=-1):
    return jax.nn.softmax(x, axis=axis)

def _gelu(x):
    return jax.nn.gelu(x, approximate=True)

def _silu(x):
    return jax.nn.silu(x)

def _sigmoid(x):
    return jax.nn.sigmoid(x)

def _layernorm(x, axis=-1, eps=1e-05):
    m = jnp.mean(x, axis=axis, keepdims=True)
    v = jnp.var(x, axis=axis, keepdims=True)
    return (x - m) / jnp.sqrt(v + eps)

def _scatter_add(tgt, idx, src, axis=0):
    return tgt.at[idx].add(src)

def _segment_sum(src, seg, n):
    return jax.ops.segment_sum(src, seg, n)
kernel_name = 'mk_decoder_preln_d2_seqx_r4_e77441'

def setup_inputs(seed: int=0):
    np.random.seed(seed)
    _w = jnp.asarray

    def _rec_inputs():
        import jax
        import jax.numpy as jnp
        _rk = jax.random.key(seed)
        x = -0.0002928 + 1 * jax.random.normal(jax.random.fold_in(_rk, 1), (8, 512, 256), jnp.float32)
        _lenS = 512 - jax.random.randint(jax.random.fold_in(_rk, 7), (8,), 0, max(1, 512 // 4) + 1, jnp.int32)
        _lenS2 = 64 - jax.random.randint(jax.random.fold_in(_rk, 8), (8,), 0, max(1, 64 // 4) + 1, jnp.int32)
        _ctx_1024P = jax.random.normal(jax.random.fold_in(_rk, 11), (8, 16, 256), jnp.float32)
        _ctx_1024c = jax.random.dirichlet(jax.random.fold_in(_rk, 511), 0.3 * jnp.ones((16,), jnp.float32), (8, 64))
        _ctx_1024t = jnp.einsum('bsk,bkd->bsd', _ctx_1024c, _ctx_1024P)
        _ctx_1024t = _ctx_1024t * jax.lax.rsqrt(jnp.mean(jnp.square(_ctx_1024t)) + 1e-12) * 0.953939
        ctx_1024 = -1.39393e-06 + 0.999914 * (_ctx_1024t + 0.3 * jax.random.normal(jax.random.fold_in(_rk, 611), (8, 64, 256), jnp.float32))
        _validS = jnp.arange(512)[None, :] < _lenS[:, None]
        _validS2 = jnp.arange(64)[None, :] < _lenS2[:, None]
        _causal = jnp.tril(jnp.ones((512, 512), dtype=bool))
        mask_Bx1xSxS2_bk1 = jnp.broadcast_to(_validS2[:, None, None, :], (8, 1, 512, 64))
        return (x, ctx_1024, mask_Bx1xSxS2_bk1)
    x, ctx_1024, mask_Bx1xSxS2_bk1 = _rec_inputs()

    def _L0_attn_setup():
        import jax, jax.numpy as jnp
        import numpy as np
        B, S, D = (4, 512, 256)
        DQK = D // 4
        key = jax.random.key(seed)
        ks = jax.random.split(key, 7)
        s = 1.0 / np.sqrt(D)
        return {'x': jax.random.normal(ks[0], (B, S, D), dtype=jnp.float32), 'Wq': jax.random.uniform(ks[1], (D, DQK), jnp.float32, -s, s), 'bq': jax.random.uniform(ks[2], (DQK,), jnp.float32, -s, s), 'Wk': jax.random.uniform(ks[3], (D, DQK), jnp.float32, -s, s), 'bk': jax.random.uniform(ks[4], (DQK,), jnp.float32, -s, s), 'Wv': jax.random.uniform(ks[5], (D, D), jnp.float32, -s, s), 'bv': jax.random.uniform(ks[6], (D,), jnp.float32, -s, s)}
    _L0_attn_all = _L0_attn_setup()
    _L0_attn_in = {k: v for k, v in _L0_attn_all.items() if k in ('Wq', 'bq', 'Wk', 'bk', 'Wv', 'bv')}
    del _L0_attn_all

    def _L0_xattn_setup():
        import jax, jax.numpy as jnp
        import numpy as np
        HEADS = 16
        D_MODEL = 256
        D_K = D_MODEL // HEADS
        B, S = (2, 512)
        NEG = -1000000000.0
        key = jax.random.key(seed)
        ks = jax.random.split(key, 8)
        q = jax.random.normal(ks[0], (B, S, D_MODEL), dtype=jnp.float32)
        k = jax.random.normal(ks[1], (B, S, D_MODEL), dtype=jnp.float32)
        v = jax.random.normal(ks[2], (B, S, D_MODEL), dtype=jnp.float32)
        mask = jax.random.randint(ks[3], (B, 1, S, S), 0, 2) > 0
        scale = 1.0 / np.sqrt(D_MODEL)
        Wq = jax.random.normal(ks[4], (D_MODEL, D_MODEL), dtype=jnp.float32) * scale
        Wk = jax.random.normal(ks[5], (D_MODEL, D_MODEL), dtype=jnp.float32) * scale
        Wv = jax.random.normal(ks[6], (D_MODEL, D_MODEL), dtype=jnp.float32) * scale
        Wo = jax.random.normal(ks[7], (D_MODEL, D_MODEL), dtype=jnp.float32) * scale
        return {'q': q, 'k': k, 'v': v, 'mask': mask, 'Wq': Wq, 'Wk': Wk, 'Wv': Wv, 'Wo': Wo}
    _L0_xattn_all = _L0_xattn_setup()
    _L0_xattn_in = {k: v for k, v in _L0_xattn_all.items() if k in ('Wq', 'Wk', 'Wv', 'Wo')}
    del _L0_xattn_all

    def _L0_ffn_setup():
        import jax, jax.numpy as jnp
        import numpy as np
        HIDDEN = 256
        NUM_EXPERTS = 8
        TOP_K = 2
        BATCH, SEQ = (4, 1024)
        key = jax.random.key(seed)
        ks = jax.random.split(key, 7)
        s = 0.02
        x = jax.random.normal(ks[0], (BATCH, SEQ, HIDDEN), dtype=jnp.float32)
        router_w = jax.random.normal(ks[1], (HIDDEN, NUM_EXPERTS), dtype=jnp.float32) * s
        router_b = jnp.zeros((NUM_EXPERTS,), dtype=jnp.float32)
        w1 = jax.random.normal(ks[2], (NUM_EXPERTS, HIDDEN, 2 * HIDDEN), dtype=jnp.float32) * s
        b1 = jnp.zeros((NUM_EXPERTS, 2 * HIDDEN), dtype=jnp.float32)
        w2 = jax.random.normal(ks[3], (NUM_EXPERTS, 2 * HIDDEN, HIDDEN), dtype=jnp.float32) * s
        b2 = jnp.zeros((NUM_EXPERTS, HIDDEN), dtype=jnp.float32)
        return {'x': x, 'router_w': router_w, 'router_b': router_b, 'w1': w1, 'b1': b1, 'w2': w2, 'b2': b2}
    _L0_ffn_all = _L0_ffn_setup()
    _L0_ffn_in = {k: v for k, v in _L0_ffn_all.items() if k in ('router_w', 'router_b', 'w1', 'b1', 'w2', 'b2')}
    del _L0_ffn_all

    def _L1_attn_setup():
        import jax, jax.numpy as jnp
        import numpy as np
        B, S, E, H = (2, 512, 256, 16)
        D = E // H
        NEG_INF = -1e+30

        def alibi_slopes(n_head):
            return jnp.asarray([2.0 ** (-8.0 * (i + 1) / n_head) for i in range(n_head)], dtype=jnp.float32)
        key = jax.random.key(seed)
        ks = jax.random.split(key, 5)
        scale = 0.02
        return {'x': jax.random.normal(ks[0], (B, S, E), dtype=jnp.float32), 'W_kqv': jax.random.normal(ks[1], (E, 3 * E), dtype=jnp.float32) * scale, 'b_kqv': jnp.zeros((3 * E,), dtype=jnp.float32), 'W_proj': jax.random.normal(ks[2], (E, E), dtype=jnp.float32) * scale, 'b_proj': jnp.zeros((E,), dtype=jnp.float32), 'slopes': alibi_slopes(H)}
    _L1_attn_all = _L1_attn_setup()
    _L1_attn_in = {k: v for k, v in _L1_attn_all.items() if k in ('W_kqv', 'b_kqv', 'W_proj', 'b_proj', 'slopes')}
    del _L1_attn_all

    def _L1_xattn_setup():
        import jax, jax.numpy as jnp
        import numpy as np
        B, L_ENC, L_DEC, D = (16, 128, 128, 256)
        key = jax.random.key(seed)
        k1, k2, k3, k4, k5, k6 = jax.random.split(key, 6)
        encoder_hc = jax.random.normal(k1, (B, L_ENC, D), dtype=jnp.float32)
        decoder_hq = jax.random.normal(k2, (B, L_DEC, D), dtype=jnp.float32)
        w_sim = jax.random.normal(k3, (3 * D,), dtype=jnp.float32) * 0.02
        b_sim = jax.random.normal(k4, (1,), dtype=jnp.float32) * 0.02
        W_qv = jax.random.normal(k5, (4 * D, D), dtype=jnp.float32) * 0.02
        b_qv = jax.random.normal(k6, (D,), dtype=jnp.float32) * 0.02
        return {'encoder_hc': encoder_hc, 'decoder_hq': decoder_hq, 'w_sim': w_sim, 'b_sim': b_sim, 'W_qv': W_qv, 'b_qv': b_qv}
    _L1_xattn_all = _L1_xattn_setup()
    _L1_xattn_in = {k: v for k, v in _L1_xattn_all.items() if k in ('w_sim', 'b_sim', 'W_qv', 'b_qv')}
    del _L1_xattn_all

    def _L1_ffn_setup():
        import jax, jax.numpy as jnp
        import numpy as np
        B, S, H, I, E, K = (4, 512, 256, 688, 8, 2)

        def _ffn(x, wg, wu, wd):
            return jax.nn.silu(x @ wg) * (x @ wu) @ wd
        key = jax.random.key(seed)
        ks = jax.random.split(key, 8)
        s = 0.02
        return {'x': jax.random.normal(ks[0], (B, S, H), jnp.float32), 'gate_w': jax.random.normal(ks[1], (E, H), jnp.float32) * (1.0 / np.sqrt(H)), 'wg': jax.random.normal(ks[2], (E, H, I), jnp.float32) * s, 'wu': jax.random.normal(ks[3], (E, H, I), jnp.float32) * s, 'wd': jax.random.normal(ks[4], (E, I, H), jnp.float32) * s, 'sg': jax.random.normal(ks[5], (H, I), jnp.float32) * s, 'su': jax.random.normal(ks[6], (H, I), jnp.float32) * s, 'sd': jax.random.normal(ks[7], (I, H), jnp.float32) * s}
    _L1_ffn_all = _L1_ffn_setup()
    _L1_ffn_in = {k: v for k, v in _L1_ffn_all.items() if k in ('gate_w', 'wg', 'wu', 'wd', 'sg', 'su', 'sd')}
    del _L1_ffn_all
    return {'x': x, 'ctx_1024': ctx_1024, 'mask_Bx1xSxS2_bk1': mask_Bx1xSxS2_bk1, 'L0_attn_Wq': _L0_attn_in['Wq'], 'L0_attn_bq': _L0_attn_in['bq'], 'L0_attn_Wk': _L0_attn_in['Wk'], 'L0_attn_bk': _L0_attn_in['bk'], 'L0_attn_Wv': _L0_attn_in['Wv'], 'L0_attn_bv': _L0_attn_in['bv'], 'L0_xattn_Wq': _L0_xattn_in['Wq'], 'L0_xattn_Wk': _L0_xattn_in['Wk'], 'L0_xattn_Wv': _L0_xattn_in['Wv'], 'L0_xattn_Wo': _L0_xattn_in['Wo'], 'L0_ffn_router_w': _L0_ffn_in['router_w'], 'L0_ffn_router_b': _L0_ffn_in['router_b'], 'L0_ffn_w1': _L0_ffn_in['w1'], 'L0_ffn_b1': _L0_ffn_in['b1'], 'L0_ffn_w2': _L0_ffn_in['w2'], 'L0_ffn_b2': _L0_ffn_in['b2'], 'L1_attn_W_kqv': _L1_attn_in['W_kqv'], 'L1_attn_b_kqv': _L1_attn_in['b_kqv'], 'L1_attn_W_proj': _L1_attn_in['W_proj'], 'L1_attn_b_proj': _L1_attn_in['b_proj'], 'L1_attn_slopes': _L1_attn_in['slopes'], 'L1_xattn_w_sim': _L1_xattn_in['w_sim'], 'L1_xattn_b_sim': _L1_xattn_in['b_sim'], 'L1_xattn_W_qv': _L1_xattn_in['W_qv'], 'L1_xattn_b_qv': _L1_xattn_in['b_qv'], 'L1_ffn_gate_w': _L1_ffn_in['gate_w'], 'L1_ffn_wg': _L1_ffn_in['wg'], 'L1_ffn_wu': _L1_ffn_in['wu'], 'L1_ffn_wd': _L1_ffn_in['wd'], 'L1_ffn_sg': _L1_ffn_in['sg'], 'L1_ffn_su': _L1_ffn_in['su'], 'L1_ffn_sd': _L1_ffn_in['sd']}

def reference(x, ctx_1024, mask_Bx1xSxS2_bk1, L0_attn_Wq, L0_attn_bq, L0_attn_Wk, L0_attn_bk, L0_attn_Wv, L0_attn_bv, L0_xattn_Wq, L0_xattn_Wk, L0_xattn_Wv, L0_xattn_Wo, L0_ffn_router_w, L0_ffn_router_b, L0_ffn_w1, L0_ffn_b1, L0_ffn_w2, L0_ffn_b2, L1_attn_W_kqv, L1_attn_b_kqv, L1_attn_W_proj, L1_attn_b_proj, L1_attn_slopes, L1_xattn_w_sim, L1_xattn_b_sim, L1_xattn_W_qv, L1_xattn_b_qv, L1_ffn_gate_w, L1_ffn_wg, L1_ffn_wu, L1_ffn_wd, L1_ffn_sg, L1_ffn_su, L1_ffn_sd):
    import jax
    import jax.numpy as jnp

    def _L0_attn_ref(x, Wq, bq, Wk, bk, Wv, bv):
        import jax, jax.numpy as jnp
        import numpy as np
        B, S, D = (4, 512, 256)
        DQK = D // 4
        Q = jnp.einsum('bsd,de->bse', x, Wq) + bq
        K = jnp.einsum('bsd,de->bse', x, Wk) + bk
        V = jnp.einsum('bsd,de->bse', x, Wv) + bv
        scores = jnp.einsum('bqe,bke->bqk', Q, K)
        attn = jax.nn.softmax(scores, axis=-1)
        attended = jnp.einsum('bqk,bkd->bqd', attn, V)
        return attended + x

    def _L0_xattn_ref(q, k, v, mask, Wq, Wk, Wv, Wo):
        import jax, jax.numpy as jnp
        import numpy as np
        HEADS = 16
        D_MODEL = 256
        D_K = D_MODEL // HEADS
        B, S = (2, 512)
        NEG = -1000000000.0
        b, s, _ = q.shape

        def proj(x, W):
            return (x @ W.T).reshape(b, -1, HEADS, D_K).transpose(0, 2, 1, 3)
        qh, kh, vh = (proj(q, Wq), proj(k, Wk), proj(v, Wv))
        att = jnp.einsum('bhqd,bhkd->bhqk', qh, kh) / jnp.sqrt(jnp.float32(D_K))
        att = jnp.where(mask, NEG, att)
        att = jax.nn.softmax(att, axis=-1)
        out = jnp.einsum('bhqk,bhkd->bhqd', att, vh)
        out = out.transpose(0, 2, 1, 3).reshape(b, -1, D_MODEL)
        return out @ Wo.T

    def _L0_ffn_ref(x, router_w, router_b, w1, b1, w2, b2):
        import jax, jax.numpy as jnp
        import numpy as np
        HIDDEN = 256
        NUM_EXPERTS = 8
        TOP_K = 2
        BATCH, SEQ = (4, 1024)
        logits = jnp.einsum('bsh,he->bse', x, router_w) + router_b
        probs = jax.nn.softmax(logits, axis=-1)
        topk_p, topk_i = jax.lax.top_k(probs, TOP_K)
        topk_p = topk_p / jnp.sum(topk_p, axis=-1, keepdims=True)
        out = jnp.zeros_like(x)
        for e in range(NUM_EXPERTS):
            w = jnp.sum(jnp.where(topk_i == e, topk_p, 0.0), axis=-1)
            h = jax.nn.relu(jnp.einsum('bsh,hf->bsf', x, w1[e]) + b1[e])
            y = jnp.einsum('bsf,fh->bsh', h, w2[e]) + b2[e]
            out = out + w[..., None] * y
        return out

    def _L1_attn_ref(x, W_kqv, b_kqv, W_proj, b_proj, slopes):
        import jax, jax.numpy as jnp
        import numpy as np
        B, S, E, H = (2, 512, 256, 16)
        D = E // H
        NEG_INF = -1e+30

        def alibi_slopes(n_head):
            return jnp.asarray([2.0 ** (-8.0 * (i + 1) / n_head) for i in range(n_head)], dtype=jnp.float32)
        b, s, e = x.shape
        kqv = x @ W_kqv + b_kqv
        k, q, v = jnp.split(kqv, 3, axis=-1)
        k = k.reshape(b, s, H, D)
        q = q.reshape(b, s, H, D)
        v = v.reshape(b, s, H, D)
        attn = jnp.einsum('bqhd,bkhd->bhqk', q, k) * (1.0 / jnp.sqrt(jnp.float32(D)))
        i = jnp.arange(s)[:, None]
        j = jnp.arange(s)[None, :]
        rel = (j - i).astype(jnp.float32)
        bias = slopes[:, None, None] * jnp.tril(rel)
        bias = jnp.where(j > i, NEG_INF, bias)
        attn = jax.nn.softmax(attn + bias[None], axis=-1)
        y = jnp.einsum('bhqk,bkhd->bqhd', attn, v).reshape(b, s, e)
        return y @ W_proj + b_proj

    def _L1_xattn_ref(encoder_hc, decoder_hq, w_sim, b_sim, W_qv, b_qv):
        import jax, jax.numpy as jnp
        import numpy as np
        B, L_ENC, L_DEC, D = (16, 128, 128, 256)
        d = encoder_hc.shape[-1]
        w1, w2, w3 = (w_sim[:d], w_sim[d:2 * d], w_sim[2 * d:])
        Sim = (encoder_hc @ w1)[:, :, None] + (decoder_hq @ w2)[:, None, :] + jnp.einsum('bid,bjd->bij', encoder_hc * w3, decoder_hq) + b_sim[0]
        A = jax.nn.softmax(Sim, axis=2)
        hq_hat = jnp.einsum('bij,bjd->bid', A, decoder_hq)
        Batt = jax.nn.softmax(jnp.max(Sim, axis=2), axis=1)
        hc_bar = jnp.einsum('bi,bid->bd', Batt, encoder_hc)[:, None, :]
        hc_hat = jnp.broadcast_to(hc_bar, encoder_hc.shape)
        feats = jnp.concatenate([encoder_hc, hq_hat, encoder_hc * hq_hat, encoder_hc * hc_hat], axis=-1)
        hcq = feats @ W_qv + b_qv
        return hcq

    def _L1_ffn_ref(x, gate_w, wg, wu, wd, sg, su, sd):
        import jax, jax.numpy as jnp
        import numpy as np
        B, S, H, I, E, K = (4, 512, 256, 688, 8, 2)

        def _ffn(x, wg, wu, wd):
            return jax.nn.silu(x @ wg) * (x @ wu) @ wd
        Bb, Ss, Hh = x.shape
        xt = x.reshape(-1, Hh)
        T = xt.shape[0]
        scores = jax.nn.softmax(xt @ gate_w.T, axis=-1)
        topw, topi = jax.lax.top_k(scores, K)
        topw = topw / (jnp.sum(topw, axis=-1, keepdims=True) + 1e-20)
        cw = jnp.zeros((T, E), xt.dtype).at[jnp.arange(T)[:, None], topi].add(topw)
        expert_out = jax.vmap(lambda g, u, d: _ffn(xt, g, u, d))(wg, wu, wd)
        y = jnp.einsum('te,eth->th', cw, expert_out)
        y = y + _ffn(xt, sg, su, sd)
        return y.reshape(Bb, Ss, Hh)
    x = x + _L0_attn_ref(_layernorm(x, axis=-1), L0_attn_Wq, L0_attn_bq, L0_attn_Wk, L0_attn_bk, L0_attn_Wv, L0_attn_bv)
    x = x + _L0_xattn_ref(_layernorm(x, axis=-1), ctx_1024, ctx_1024, mask_Bx1xSxS2_bk1, L0_xattn_Wq, L0_xattn_Wk, L0_xattn_Wv, L0_xattn_Wo)
    x = x + _L0_ffn_ref(_layernorm(x, axis=-1), L0_ffn_router_w, L0_ffn_router_b, L0_ffn_w1, L0_ffn_b1, L0_ffn_w2, L0_ffn_b2)
    x = x + _L1_attn_ref(_layernorm(x, axis=-1), L1_attn_W_kqv, L1_attn_b_kqv, L1_attn_W_proj, L1_attn_b_proj, L1_attn_slopes)
    x = x + _L1_xattn_ref(_layernorm(x, axis=-1), ctx_1024, L1_xattn_w_sim, L1_xattn_b_sim, L1_xattn_W_qv, L1_xattn_b_qv)
    x = x + _L1_ffn_ref(_layernorm(x, axis=-1), L1_ffn_gate_w, L1_ffn_wg, L1_ffn_wu, L1_ffn_wd, L1_ffn_sg, L1_ffn_su, L1_ffn_sd)
    return x

_drawn_inputs = setup_inputs


def setup_inputs(seed=0):
    import zlib

    import numpy as np

    out = dict(_drawn_inputs(seed))
    spreads = {'L0_ffn_router_b': (0.0, 0.369),
     'L0_ffn_b1': (0.0, 0.761),
     'L0_ffn_b2': (0.0, 0.1),
     'L1_attn_b_kqv': (0.0, 0.513),
     'L1_attn_b_proj': (0.0, 0.1)}
    factors = {'L0_attn_bq': 4.732,
     'L0_attn_bk': 8.0,
     'L0_attn_bv': 3.041,
     'L1_attn_W_kqv': 2.968,
     'L1_attn_slopes': 5.48,
     'L1_xattn_b_qv': 5.868,
     'L1_ffn_gate_w': 6.749,
     'L1_ffn_wg': 6.013,
     'L1_ffn_wu': 5.937,
     'L1_ffn_wd': 5.933,
     'L1_ffn_sg': 4.48,
     'L1_ffn_su': 4.431,
     'L1_ffn_sd': 4.434}
    for name, (base, spread) in spreads.items():
        noise = np.random.default_rng([zlib.crc32(name.encode()), seed]).standard_normal(out[name].shape)
        drawn = base * np.exp(spread * noise) if base else spread * noise
        out[name] = jnp.asarray(drawn.astype(out[name].dtype))
    for name, factor in factors.items():
        out[name] = (out[name] * factor).astype(out[name].dtype)
    return out
```

```python
from contextlib import ExitStack

import concourse.bass as bass
from concourse import mybir

ALU = mybir.AluOpType
ACT = mybir.ActivationFunctionType
AX = mybir.AxisListType
F32 = mybir.dt.float32
F32R = mybir.dt.float32r
I32 = mybir.dt.int32
U8 = mybir.dt.uint8

P = 128
B, S, D = 8, 512, 256
KT = D // P
TB = S // P
NT = B * TB
BANK = 512
SC = 64
EPS = 1e-5


def after(eng, sem, count):
    if not isinstance(count, int) or count > 0:
        eng.wait_ge(sem, count)


def wait_apart(eng, sem, count, met):
    if not isinstance(count, int):
        count = eng.to_reg(count)
    eng.wait_ge(*met)
    eng.wait_ge(sem, count)


def over_sequences(eng, body):
    body(0, 1)
    with eng.Fori(1, B - 1) as b:
        body(b, b + 1)
    body(B - 1, None)


def over_pairs(eng, body):
    body(0, 0)
    body(1, 1)
    with eng.Fori(1, B // 2 - 1) as u:
        for j in range(2):
            body(u * 2 + j, j)
    body(B - 2, 0)
    body(B - 1, 1)


def within(b):
    return not isinstance(b, int) or b < B


class Norm:

    def __init__(self, nc, ctx, g, tag, psum, depth=1):
        self.nc, self.g, self.psum = nc, g, psum
        sb = lambda name, shape, dt=F32: ctx.enter_context(nc.sbuf_tensor(f"{tag}_{name}", shape, dt))
        sem = lambda name: g.stage_semaphore(f"{tag}_{name}")
        self.stats = sb("stats", [P, TB, 6])
        self.half = sb("half", [P, 4, TB])
        self.mean = sb("mean", [P, TB])
        self.var = sb("var", [P, TB])
        self.var_eps = sb("var_eps", [P, TB])
        self.rstd = sb("rstd", [P, TB])
        self.rows = [sb(f"xn{i}", [P, TB, D]) for i in range(depth)]
        self.columns = [sb(f"xnT{i}", [P, KT, S]) for i in range(depth)]
        self.xn, self.xnT = self.rows[0], self.columns[0]
        self.depth = depth
        self.stats_done = sem("stats_done")
        self.halves_done = sem("halves_done")
        self.mean_done = sem("mean_done")
        self.var_done = sem("var_done")
        self.rstd_done = sem("rstd_done")
        self.rows_done = sem("rows_done")
        self.turned = sem("turned")
        self.columns_done = sem("columns_done")

    def vector_stats(self, b):
        v, x, st = self.nc.vector, self.g.x, self.stats
        for t in range(TB):
            v.bn_stats(st[:, t, :], x[:, b * TB + t, :]).then_inc(self.stats_done, 1)
        v.wait_ge(self.stats_done, b * TB + TB)
        v.tensor_tensor(self.half[:, 0], st[:, :, 1], st[:, :, 4], ALU.subtract).then_inc(self.halves_done, 1)
        v.tensor_tensor(self.half[:, 1], st[:, :, 1], st[:, :, 4], ALU.add).then_inc(self.halves_done, 1)
        v.tensor_tensor(self.half[:, 2], st[:, :, 2], st[:, :, 5], ALU.add).then_inc(self.halves_done, 1)
        v.wait_ge(self.halves_done, b * 4 + 3)
        v.scalar_tensor_tensor(out=self.half[:, 3], in0=self.half[:, 0], scalar=0.25, in1=self.half[:, 0],
                               op0=ALU.mult, op1=ALU.mult).then_inc(self.halves_done, 1)
        v.tensor_scalar(self.mean[:, :], self.half[:, 1], 0.5, None, ALU.mult).then_inc(self.mean_done, 1)
        v.wait_ge(self.halves_done, b * 4 + 4)
        v.scalar_tensor_tensor(out=self.var[:, :], in0=self.half[:, 2], scalar=1.0 / D, in1=self.half[:, 3],
                               op0=ALU.mult, op1=ALU.add).then_inc(self.var_done, 1)
        v.wait_ge(self.var_done, b * 2 + 1)
        v.tensor_scalar(self.var_eps[:, :], self.var[:, :], EPS, None, ALU.add).then_inc(self.var_done, 1)

    def gpsimd(self, b):
        p = self.nc.gpsimd
        p.wait_ge(self.var_done, b * 2 + 2)
        after(p, self.rows_done, b * TB)
        p.tensor_tensor(self.rstd[:, :], self.var_eps[:, :], self.g.minus_half[:, 0:TB], ALU.pow).then_inc(self.rstd_done, 1)

    def vector_rows(self, b, free=(), buf=0):
        v = self.nc.vector
        v.wait_ge(self.mean_done, b + 1)
        v.wait_ge(self.rstd_done, b + 1)
        after(v, self.turned, b - self.depth + 1)
        for s, n in free:
            after(v, s, n)
        for t in range(TB):
            v.tensor_scalar(self.rows[buf][:, t, :], self.g.x[:, b * TB + t, :], self.mean[:, t:t + 1],
                            self.rstd[:, t:t + 1], ALU.subtract, ALU.mult).then_inc(self.rows_done, 1)

    def tensor(self, b, free=(), buf=0):
        pe = self.nc.tensor
        after(pe, self.columns_done, b)
        for s, n in free:
            after(pe, s, n)
        for t in range(TB):
            pe.wait_ge(self.rows_done, b * TB + t + 1)
            for k in range(KT):
                last = pe.transpose(self.psum[:, k, t * P:(t + 1) * P], self.rows[buf][:, t, k * P:(k + 1) * P], self.g.ident[:, :])
        last.then_inc(self.turned, 1)

    def scalar(self, b, free=(), buf=0):
        a = self.nc.scalar
        a.wait_ge(self.turned, b + 1)
        for s, n in free:
            after(a, s, n)
        a.activation(self.columns[buf][:, :, :], self.psum[:, :, :], ACT.Copy).then_inc(self.columns_done, 1)


class Globals:

    def __init__(self, nc):
        self.nc, self.stage_semaphores = nc, []

    def stage_semaphore(self, name):
        self.stage_semaphores.append(self.nc.alloc_semaphore(name))
        return self.stage_semaphores[-1]

    def end_stage(self):
        self.nc.clear_and_free_semaphores(self.stage_semaphores)
        self.nc.all_engine_barrier()
        self.stage_semaphores = []


def setup(nc, ctx, io):
    g = Globals(nc)
    sb = lambda name, shape, dt=F32: ctx.enter_context(nc.sbuf_tensor(name, shape, dt))
    g.x = sb("x_rows", [P, NT, D])
    g.ident = sb("ident", [P, P])
    g.minus_half = sb("minus_half", [P, NT])
    g.ones = sb("ones", [P, P])
    g.zero_row = sb("zero_row", [P, D])
    g.slot = sb("slot", [P, NT, 2], I32)
    g.share = sb("share", [P, NT, 2])
    g.tile_expert = sb("tile_expert", [1, SLOT_TILES + NT], I32)
    g.slots_x = nc.dram_tensor("slots_x", [(SLOT_TILES + NT) * P, D], F32, kind="Internal").ap()
    g.slots_y = nc.dram_tensor("slots_y", [(SLOT_TILES + NT) * P, D], F32, kind="Internal").ap()
    g.zeroed = ctx.enter_context(nc.semaphore("zeroed"))
    x_loaded, consts = g.stage_semaphore("x_loaded"), g.stage_semaphore("consts")
    with nc.Block() as block:
        @block.sync
        def _(sp):
            sp.dma_start(g.x[:, :, :], io["x"].rearrange("b (t p) d -> p (b t) d", p=P)).then_inc(x_loaded, 16)
            sp.wait_ge(consts, 4)
            sp.dma_start(g.slots_x[0:SLOT_TILES * P, :].rearrange("(p r) d -> p r d", p=P),
                         g.zero_row[:, :].unsqueeze(1).broadcast_to([P, SLOT_TILES, D])).then_inc(g.zeroed, 16)
            sp.wait_ge(x_loaded, 16)

        @block.gpsimd
        def _(pool):
            pool.memset(g.ident[:, :], 0.0).then_inc(consts, 1)
            pool.memset(g.minus_half[:, :], -0.5).then_inc(consts, 1)
            pool.memset(g.ones[:, :], 1.0).then_inc(consts, 1)
            pool.memset(g.zero_row[:, :], 0.0).then_inc(consts, 1)
            pool.wait_ge(consts, 4)
            pool.affine_select(out=g.ident[:, :], in_=g.ident[:, :], compare_op=ALU.not_equal, fill=1.0,
                               base=0, pattern=[[-1, P]], channel_multiplier=1).then_inc(consts, 1)
            pool.wait_ge(consts, 5)
    return g


def l0_attention(nc, io, g):
    H = 64
    with ExitStack() as ctx:
        sb = lambda name, shape, dt=F32: ctx.enter_context(nc.sbuf_tensor("a0_" + name, shape, dt))
        sem = lambda name: g.stage_semaphore("a0_" + name)
        turn = ctx.enter_context(nc.psum_tensor("a0_turn", [P, KT, S], F32))
        proj = ctx.enter_context(nc.psum_tensor("a0_proj", [P, 2, BANK], F32))
        score = ctx.enter_context(nc.psum_tensor("a0_score", [P, 2, BANK], F32))
        shift = ctx.enter_context(nc.psum_tensor("a0_shift", [P, BANK], F32))
        norm = Norm(nc, ctx, g, "a0", turn)
        wq2, wk2 = sb("wq2", [P, KT, 2, H]), sb("wk2", [P, KT, 2, H])
        wv = sb("wv", [P, KT, D])
        bq2, bk2, bv = sb("bq2", [P, 1]), sb("bk2", [P, 1]), sb("bv", [P, D])
        qhi, qlo, khl = (sb(n, [P, S], F32R) for n in ("qhi", "qlo", "khl"))
        v1 = sb("v1", [P, TB, D + 1])
        negmax = sb("negmax", [P, TB])
        shift_hl = sb("shift_hl", [H, S], F32R)
        ones_r = sb("ones_r", [H, P], F32R)
        prob = sb("prob", [P, TB, S])
        rinv = sb("rinv", [P, TB])

        loaded, ready = sem("loaded"), sem("ready")
        qk_done, q_hi, q_lo, k_done = sem("qk_done"), sem("q_hi"), sem("q_lo"), sem("k_done")
        k_hi = sem("k_hi")
        v_done, v_kept = sem("v_done"), sem("v_kept")
        s_done, max_done = sem("s_done"), sem("max_done")
        shift_done, shift_hi, shift_lo = sem("shift_done"), sem("shift_hi"), sem("shift_lo")
        st_done, exp_done = sem("st_done"), sem("exp_done")
        o_done, rinv_done, x_done, res_done = sem("o_done"), sem("rinv_done"), sem("x_done"), sem("res_done")
        block = ctx.enter_context(nc.Block())

        @block.sync
        def _(sp):
            for half in range(2):
                sp.dma_start(wq2[:, :, half, :], io["L0_attn_Wq"].rearrange("(k p) e -> p k e", p=P)).then_inc(loaded, 16)
                sp.dma_start(wk2[:, :, half, :], io["L0_attn_Wk"].rearrange("(k p) e -> p k e", p=P)).then_inc(loaded, 16)
                sp.dma_start(bq2[half * H:(half + 1) * H, :], io["L0_attn_bq"].rearrange("(p o) -> p o", o=1)).then_inc(loaded, 16)
                sp.dma_start(bk2[half * H:(half + 1) * H, :], io["L0_attn_bk"].rearrange("(p o) -> p o", o=1)).then_inc(loaded, 16)
            sp.dma_start(wv[:, :, :], io["L0_attn_Wv"].rearrange("(k p) e -> p k e", p=P)).then_inc(loaded, 16)
            sp.dma_start(bv[:, :], io["L0_attn_bv"].partition_broadcast(P)).then_inc(loaded, 16)

        LOADS = 16 * 10

        @block.gpsimd
        def _(pool):
            pool.memset(v1[:, :, D:D + 1], 1.0).then_inc(ready, 1)
            pool.memset(shift_hl[:, :].bitcast(F32), 0.0).then_inc(ready, 1)
            pool.memset(ones_r[:, :].bitcast(F32), 1.0).then_inc(ready, 1)
            norm.gpsimd(0)

            def body(b, nxt):
                pool.wait_ge(norm.rows_done, b * TB + TB)
                pool.tensor_tensor(g.x[:, bass.ds(b * TB, TB), :], g.x[:, bass.ds(b * TB, TB), :], norm.xn[:, :, :],
                                   ALU.add).then_inc(res_done, 1)
                if nxt is not None:
                    norm.gpsimd(nxt)
            over_sequences(pool, body)

        @block.tensor
        def _(pe):
            pe.wait_ge(loaded, LOADS)
            pe.wait_ge(ready, 3)
            norm.tensor(0)

            def body(b, nxt):
                pe.wait_ge(norm.columns_done, b + 1)
                after(pe, x_done, b * TB)
                for i, w in enumerate((wq2, wk2)):
                    for k in range(KT):
                        last = pe.matmul(proj[:, i, :], w[:, k].rearrange("p a e -> p (a e)"), norm.xnT[:, k, :],
                                         start=k == 0, stop=k == KT - 1)
                    last.then_inc(qk_done, 1)
                for t in range(TB):
                    if t % 2 == 0:
                        if t == 0:
                            pe.wait_ge(q_lo, b + 1)
                        else:
                            pe.wait_ge(k_done, b + 1)
                    for k in range(KT):
                        last = pe.matmul(proj[:, t // 2, (t % 2) * D:(t % 2 + 1) * D], norm.xnT[:, k, t * P:(t + 1) * P],
                                         wv[:, k, :], start=k == 0, stop=k == KT - 1)
                    if t % 2:
                        last.then_inc(v_done, 1)
                for t in range(TB):
                    if t >= 2:
                        pe.wait_ge(max_done, b * TB + t - 1)
                    else:
                        after(pe, exp_done, b * TB + t - 1)
                    for n, q in enumerate((qhi, qlo)):
                        last = pe.matmul(score[:, t % 2, :], q[:, t * P:(t + 1) * P], khl[:, :], start=n == 0, stop=n == 1)
                    last.then_inc(s_done, 1)
                pe.wait_ge(max_done, b * TB + TB)
                after(pe, shift_lo, b)
                for t in range(TB):
                    last = pe.matmul(shift[0:1, t * P:(t + 1) * P], negmax[:, t:t + 1], g.ident[:, :], start=True, stop=True)
                last.then_inc(shift_done, 1)
                if nxt is not None:
                    norm.tensor(nxt)
                for t in range(TB):
                    if t == 0:
                        pe.wait_ge(shift_lo, b + 1)
                    if t >= 2:
                        pe.wait_ge(exp_done, b * TB + t - 1)
                    pe.matmul(score[:, t % 2, :], khl[:, t * P:(t + 1) * P], qhi[:, :], start=True, stop=False)
                    pe.matmul(score[:, t % 2, :], khl[:, t * P:(t + 1) * P], qlo[:, :], start=False, stop=False)
                    pe.matmul(score[:, t % 2, :], ones_r[:, :], shift_hl[:, :], start=False, stop=True).then_inc(st_done, 1)
                for t in range(TB):
                    if t == 0:
                        pe.wait_ge(v_kept, b * 2 + 2)
                        pe.wait_ge(exp_done, b * TB + TB)
                    if t >= 2:
                        pe.wait_ge(x_done, b * TB + t - 1)
                    for j in range(TB):
                        last = pe.matmul(proj[:, t % 2, 0:D + 1], prob[:, j, t * P:(t + 1) * P], v1[:, j, :],
                                         start=j == 0, stop=j == TB - 1)
                    last.then_inc(o_done, 1)
            over_sequences(pe, body)

        @block.scalar
        def _(act):
            act.wait_ge(loaded, LOADS)
            norm.scalar(0)

            def body(b, nxt):
                act.wait_ge(qk_done, b * 2 + 1)
                after(act, st_done, b * TB)
                act.activation(qhi[:, :], proj[:, 0, :], ACT.Identity, bias=bq2[:, 0:1]).then_inc(q_hi, 1)
                act.wait_ge(qk_done, b * 2 + 2)
                act.activation(khl[:, :], proj[:, 1, :], ACT.Identity, bias=bk2[:, 0:1]).then_inc(k_hi, 1)
                act.wait_ge(shift_done, b + 1)
                after(act, st_done, b * TB)
                act.activation(shift_hl[0:1, :], shift[0:1, :], ACT.Copy).then_inc(shift_hi, 1)
                if nxt is not None:
                    norm.scalar(nxt, free=[(v_done, b * 2 + 2)])
                for t in range(TB):
                    act.wait_ge(st_done, b * TB + t + 1)
                    after(act, o_done, b * TB)
                    act.activation(prob[:, t, :], score[:, t % 2, :], ACT.Exp).then_inc(exp_done, 1)
            over_sequences(act, body)

        @block.vector
        def _(dve):
            dve.wait_ge(loaded, LOADS)
            norm.vector_stats(0)
            norm.vector_rows(0)

            def body(b, nxt):
                dve.wait_ge(q_hi, b + 1)
                after(dve, st_done, b * TB)
                dve.scalar_tensor_tensor(out=qlo[:, :], in0=proj[:, 0, :], scalar=bq2[:, 0:1], in1=qhi[:, :].bitcast(F32),
                                         op0=ALU.add, op1=ALU.subtract).then_inc(q_lo, 1)
                dve.wait_ge(k_hi, b + 1)
                dve.scalar_tensor_tensor(out=khl[H:P, :], in0=proj[H:P, 1, :], scalar=bk2[H:P, 0:1],
                                         in1=khl[H:P, :].bitcast(F32), op0=ALU.add, op1=ALU.subtract).then_inc(k_done, 1)
                for i in range(2):
                    dve.wait_ge(v_done, b * 2 + i + 1)
                    after(dve, o_done, b * TB)
                    dve.tensor_tensor(v1[:, 2 * i:2 * i + 2, 0:D], proj[:, i, :].rearrange("p (t d) -> p t d", t=2),
                                      bv[:, :].unsqueeze(1).broadcast_to([P, 2, D]), ALU.add).then_inc(v_kept, 1)
                for t in range(TB):
                    dve.wait_ge(s_done, b * TB + t + 1)
                    after(dve, shift_done, b)
                    dve.tensor_reduce(negmax[:, t:t + 1], score[:, t % 2, :], AX.X, ALU.max, negate=True).then_inc(max_done, 1)
                if nxt is not None:
                    norm.vector_stats(nxt)
                dve.wait_ge(shift_hi, b + 1)
                dve.tensor_tensor(shift_hl[32:33, :], shift[0:1, :], shift_hl[0:1, :].bitcast(F32), ALU.subtract).then_inc(shift_lo, 1)
                if nxt is not None:
                    norm.vector_rows(nxt, free=[(res_done, b + 1)])
                for t in range(TB):
                    dve.wait_ge(o_done, b * TB + t + 1)
                    dve.reciprocal(rinv[:, t:t + 1], proj[:, t % 2, D:D + 1]).then_inc(rinv_done, 1)
                    dve.wait_ge(rinv_done, b * TB + t + 1)
                    dve.wait_ge(res_done, b + 1)
                    xt = g.x[:, b * TB + t, :]
                    dve.scalar_tensor_tensor(out=xt, in0=proj[:, t % 2, 0:D], scalar=rinv[:, t:t + 1], in1=xt,
                                             op0=ALU.mult, op1=ALU.add).then_inc(x_done, 1)
            over_sequences(dve, body)


def load_context(nc, ctx, io, g):
    g.ctxT = ctx.enter_context(nc.sbuf_tensor("ctxT", [P, KT, B * SC], F32))
    with ExitStack() as tmp:
        rows = tmp.enter_context(nc.sbuf_tensor("ctx_rows2", [P, B * SC // P, D], F32))
        turn = tmp.enter_context(nc.psum_tensor("ctx_turn", [P, KT, B * SC], F32))
        loaded, turned, kept = (g.stage_semaphore("ctx_" + n) for n in ("loaded", "turned", "kept"))
        block = tmp.enter_context(nc.Block())

        @block.sync
        def _(sp):
            sp.dma_start(rows[:, :, :], io["ctx_1024"].rearrange("(c b) j d -> (b j) c d", b=P // SC)).then_inc(loaded, 16)

        @block.tensor
        def _(pe):
            pe.wait_ge(loaded, 16)
            for c in range(B * SC // P):
                for k in range(KT):
                    last = pe.transpose(turn[:, k, c * P:(c + 1) * P], rows[:, c, k * P:(k + 1) * P], g.ident[:, :])
            last.then_inc(turned, 1)

        @block.scalar
        def _(act):
            act.wait_ge(turned, 1)
            act.activation(g.ctxT[:, :, :], turn[:, :, :], ACT.Copy).then_inc(kept, 1)
            act.wait_ge(kept, 1)


def l0_cross_attention(nc, io, g):
    HEADS, HD = 16, 16
    HH = P // HD
    PAIRS = HEADS // 2
    NEG, BIG = -1e9, 3e38
    with ExitStack() as ctx:
        sb = lambda name, shape, dt=F32: ctx.enter_context(nc.sbuf_tensor("c0_" + name, shape, dt))
        sem = lambda name: g.stage_semaphore("c0_" + name)
        turn = ctx.enter_context(nc.psum_tensor("c0_turn", [P, 2, BANK], F32))
        proj = ctx.enter_context(nc.psum_tensor("c0_proj", [P, 2, BANK], F32))
        score = ctx.enter_context(nc.psum_tensor("c0_score", [P, 2, 2, BANK], F32))
        norm = Norm(nc, ctx, g, "c0", turn)
        w_rows = sb("w_rows", [P, 4, KT, D])
        wT = sb("wT", [P, 4, KT, D])
        mask8 = sb("mask8", [P, NT, SC], U8)
        cap = sb("cap", [P, NT, SC])
        kT = sb("kT", [P, KT, B * SC])
        head_of_row = sb("head_of_row", [P, HH])
        head_of_key = sb("head_of_key", [P, 2 * HD])
        kblk = sb("kblk", [P, KT, HH, SC])
        ctx2 = sb("ctx2", [P, KT, 2, SC])
        vblk = sb("vblk", [P, PAIRS, 2 * HD])
        qT = sb("qT", [P, KT, S])
        prob = sb("prob", [P, TB, HEADS * SC])
        most, total, share = (sb(n, [P, TB, HEADS]) for n in ("most", "total", "share"))
        probT = sb("probT", [P, PAIRS, S])
        oT = sb("oT", [P, KT, S])

        loaded, masks, ready, caps = sem("loaded"), sem("masks"), sem("ready"), sem("caps")
        w_turned, w_kept, kt_done, kt_kept = sem("w_turned"), sem("w_kept"), sem("kt_done"), sem("kt_kept")
        kblk_done, ctx2_done = sem("kblk_done"), sem("ctx2_done")
        q_done, q_kept, v_done, v_kept = sem("q_done"), sem("q_kept"), sem("v_done"), sem("v_kept")
        s_done, capped, max_done, less_max = sem("s_done"), sem("capped"), sem("max_done"), sem("less_max")
        exp_done, sum_done, share_done, prob_done = sem("exp_done"), sem("sum_done"), sem("share_done"), sem("prob_done")
        p_turned, p_kept = sem("p_turned"), sem("p_kept")
        o_done, o_kept, w_done, x_done = sem("o_done"), sem("o_kept"), sem("w_done"), sem("x_done")
        block = ctx.enter_context(nc.Block())

        @block.sync
        def _(sp):
            for i, n in enumerate(("Wq", "Wk", "Wv", "Wo")):
                sp.dma_start(w_rows[:, i], io["L0_xattn_" + n].rearrange("(k p) d -> p k d", p=P)).then_inc(loaded, 16)
            sp.dma_start(mask8[:, :, :], io["mask_Bx1xSxS2_bk1"].rearrange("b o (t p) j -> p (b o t) j", p=P)).then_inc(masks, 16)

        @block.gpsimd
        def _(pool):
            pool.memset(head_of_row[:, :], 1.0).then_inc(ready, 1)
            pool.memset(head_of_key[:, :], 0.0).then_inc(ready, 1)
            pool.wait_ge(ready, 2)
            pool.affine_select(out=head_of_row[:, :], in_=head_of_row[:, :], compare_op=ALU.is_ge, fill=0.0, base=0,
                               pattern=[[-HD, HH]], channel_multiplier=1).then_inc(ready, 1)
            pool.wait_ge(ready, 3)
            pool.memset(head_of_key[0:SC, 0:HD], 1.0).then_inc(ready, 1)
            pool.wait_ge(ready, 4)
            pool.memset(head_of_key[SC:P, HD:2 * HD], 1.0).then_inc(ready, 1)
            pool.wait_ge(ready, 5)
            pool.affine_select(out=head_of_row[:, :], in_=head_of_row[:, :], compare_op=ALU.is_ge, fill=0.0, base=HD - 1,
                               pattern=[[HD, HH]], channel_multiplier=-1).then_inc(ready, 1)
            pool.wait_ge(ready, 6)
            pool.wait_ge(kt_kept, 1)

            def stage(b):
                after(pool, s_done, b * TB)
                for k in range(KT):
                    pool.tensor_tensor(kblk[:, k], kT[:, k, bass.ds(b * SC, SC)].unsqueeze(1).broadcast_to([P, HH, SC]),
                                       head_of_row[:, :].unsqueeze(2).broadcast_to([P, HH, SC]), ALU.mult).then_inc(kblk_done, 1)
                after(pool, v_done, b)
                pool.tensor_copy(ctx2[:, :, 0], g.ctxT[:, :, bass.ds(b * SC, SC)]).then_inc(ctx2_done, 1)
                pool.tensor_copy(ctx2[:, :, 1], g.ctxT[:, :, bass.ds(b * SC, SC)]).then_inc(ctx2_done, 1)

            norm.gpsimd(0)
            stage(0)

            def body(b, nxt):
                for t in range(TB):
                    pool.wait_ge(share_done, b * TB + t + 1)
                    p3 = prob[:, t].rearrange("p (h j) -> p h j", h=HEADS)
                    pool.tensor_tensor(p3, p3, share[:, t].unsqueeze(2).broadcast_to([P, HEADS, SC]), ALU.mult).then_inc(prob_done, 1)
                    if t == 0 and nxt is not None:
                        norm.gpsimd(nxt)
                if nxt is not None:
                    stage(nxt)
            over_sequences(pool, body)

        @block.tensor
        def _(pe):
            pe.wait_ge(loaded, 64)
            for i in range(4):
                for k in range(KT):
                    for e in range(KT):
                        last = pe.transpose(score[:, i // 2, i % 2, k * D + e * P:k * D + (e + 1) * P],
                                            w_rows[:, i, e, k * P:(k + 1) * P], g.ident[:, :])
                last.then_inc(w_turned, 1)
            pe.wait_ge(w_kept, 4)
            for h in range(KT):
                for k in range(KT):
                    last = pe.matmul(proj[:, h, :], wT[:, 1, k, h * P:(h + 1) * P], g.ctxT[:, k, :], start=k == 0, stop=k == KT - 1)
            last.then_inc(kt_done, 1)
            norm.tensor(0)
            pe.wait_ge(kt_kept, 1)

            def turn_probs(b, t):
                pe.wait_ge(prob_done, b * TB + t + 1)
                if t > 0:
                    pe.wait_ge(p_kept, b * TB + t)
                else:
                    pe.wait_ge(norm.columns_done, b + 1)
                for i in range(PAIRS):
                    last = pe.transpose(turn[:, i // 4, (i % 4) * P:(i % 4 + 1) * P], prob[:, t, i * P:(i + 1) * P], g.ident[:, :])
                last.then_inc(p_turned, 1)

            def body(b, nxt):
                pe.wait_ge(norm.columns_done, b + 1)
                after(pe, x_done, b * 2)
                for h in range(KT):
                    for k in range(KT):
                        last = pe.matmul(proj[:, h, :], wT[:, 0, k, h * P:(h + 1) * P], norm.xnT[:, k, :], start=k == 0, stop=k == KT - 1)
                    last.then_inc(q_done, 1)
                pe.wait_ge(ctx2_done, b * 2 + 2)
                pe.wait_ge(q_kept, b * 2 + 1)
                for k in range(KT):
                    last = pe.matmul(proj[:, 0, 0:D], ctx2[:, k].rearrange("p a j -> p (a j)"), wT[:, 2, k, :], start=k == 0, stop=k == KT - 1)
                last.then_inc(v_done, 1)
                for t in range(TB):
                    if t == 0:
                        pe.wait_ge(q_kept, b * 2 + 2)
                        pe.wait_ge(kblk_done, b * 2 + 2)
                    after(pe, capped, b * TB + t - 1)
                    for h in range(KT):
                        last = pe.matmul(score[:, t % 2, h, :], qT[:, h, t * P:(t + 1) * P], kblk[:, h].rearrange("p h j -> p (h j)"),
                                         start=True, stop=True)
                    last.then_inc(s_done, 1)
                    if t >= 2:
                        turn_probs(b, t - 2)
                turn_probs(b, TB - 2)
                turn_probs(b, TB - 1)
                if nxt is not None:
                    norm.tensor(nxt, free=[(p_kept, b * TB + TB)])
                pe.wait_ge(p_kept, b * TB + TB)
                pe.wait_ge(v_kept, b + 1)
                for i in range(PAIRS):
                    r = 2 * HD * (i % 4)
                    last = pe.matmul(proj[r:r + 2 * HD, i // 4, :], vblk[:, i, :], probT[:, i, :], start=True, stop=True)
                last.then_inc(o_done, 1)
                pe.wait_ge(o_kept, b + 1)
                for t in range(TB):
                    for k in range(KT):
                        last = pe.matmul(proj[:, t // 2, (t % 2) * D:(t % 2 + 1) * D], oT[:, k, t * P:(t + 1) * P], wT[:, 3, k, :],
                                         start=k == 0, stop=k == KT - 1)
                    if t % 2:
                        last.then_inc(w_done, 1)
            over_sequences(pe, body)

        @block.scalar
        def _(act):
            for i in range(4):
                act.wait_ge(w_turned, i + 1)
                act.activation(wT[:, i].rearrange("p k e -> p (k e)"), score[:, i // 2, i % 2, :], ACT.Copy).then_inc(w_kept, 1)
            act.wait_ge(kt_done, 1)
            act.activation(kT[:, :, :], proj[:, :, :], ACT.Copy).then_inc(kt_kept, 1)
            norm.scalar(0)

            def body(b, nxt):
                for h in range(KT):
                    act.wait_ge(q_done, b * 2 + h + 1)
                    after(act, s_done, b * TB)
                    act.activation(qT[:, h, :], proj[:, h, :], ACT.Copy, scale=HD ** -0.5).then_inc(q_kept, 1)

                def keep_turned(t):
                    act.wait_ge(p_turned, b * TB + t + 1)
                    after(act, o_done, b)
                    act.activation(probT[:, :, t * P:(t + 1) * P], turn[:, :, :].rearrange("p a (i q) -> p (a i) q", i=4),
                                   ACT.Copy).then_inc(p_kept, 1)
                for t in range(TB):
                    act.wait_ge(less_max, b * TB + t + 1)
                    act.activation(prob[:, t, :], prob[:, t, :], ACT.Exp).then_inc(exp_done, 1)
                    if t >= 1:
                        keep_turned(t - 1)
                keep_turned(TB - 1)
                if nxt is not None:
                    norm.scalar(nxt, free=[(q_done, b * 2 + 2)])
                act.wait_ge(o_done, b + 1)
                after(act, w_done, b * 2)
                act.activation(oT[:, :, :], proj[:, :, :], ACT.Copy).then_inc(o_kept, 1)
            over_sequences(act, body)

        @block.vector
        def _(dve):
            norm.vector_stats(0)
            norm.vector_rows(0)
            dve.wait_ge(masks, 16)
            dve.tensor_scalar(cap[:, :, :], mask8[:, :, :], -BIG, BIG, ALU.mult, ALU.add).then_inc(caps, 1)
            dve.wait_ge(caps, 1)
            dve.scalar_tensor_tensor(out=cap[:, :, :], in0=mask8[:, :, :], scalar=NEG, in1=cap[:, :, :],
                                     op0=ALU.mult, op1=ALU.add).then_inc(caps, 1)
            dve.wait_ge(caps, 2)
            dve.wait_ge(ready, 6)

            def body(b, nxt):
                def three(t):
                    return prob[:, t].rearrange("p (h j) -> p h j", h=HEADS)

                def masked(t):
                    dve.wait_ge(s_done, b * TB + t + 1)
                    after(dve, p_turned, b * TB)
                    for h in range(KT):
                        step = dve.tensor_tensor(three(t)[:, h * HH:(h + 1) * HH], score[:, t % 2, h].rearrange("p (h j) -> p h j", h=HH),
                                                 cap[:, bass.ds(b * TB + t, 1), :].broadcast_to([P, HH, SC]), ALU.min)
                    step.then_inc(capped, 1)

                def less_maximum(t):
                    dve.wait_ge(capped, b * TB + t + 1)
                    dve.tensor_reduce(most[:, t], three(t), AX.X, ALU.max).then_inc(max_done, 1)
                    dve.wait_ge(max_done, b * TB + t + 1)
                    dve.tensor_tensor(three(t), three(t), most[:, t].unsqueeze(2).broadcast_to([P, HEADS, SC]),
                                      ALU.subtract).then_inc(less_max, 1)

                def shares(t):
                    dve.wait_ge(exp_done, b * TB + t + 1)
                    after(dve, prob_done, b * TB + t)
                    dve.tensor_reduce(total[:, t], three(t), AX.X, ALU.add).then_inc(sum_done, 1)
                    dve.wait_ge(sum_done, b * TB + t + 1)
                    dve.reciprocal(share[:, t], total[:, t]).then_inc(share_done, 1)

                dve.wait_ge(v_done, b + 1)
                after(dve, o_done, b)
                dve.tensor_tensor(vblk[:, :, :], proj[:, 0, 0:D].rearrange("p (i c) -> p i c", i=PAIRS),
                                  head_of_key[:, :].unsqueeze(1).broadcast_to([P, PAIRS, 2 * HD]), ALU.mult).then_inc(v_kept, 1)
                for t in range(TB + 2):
                    if t < TB:
                        masked(t)
                    if 1 <= t <= TB:
                        less_maximum(t - 1)
                    if t >= 2:
                        shares(t - 2)
                    if t == 2 and nxt is not None:
                        norm.vector_stats(nxt)
                    if t == TB and nxt is not None:
                        norm.vector_rows(nxt)
                for i in range(2):
                    dve.wait_ge(w_done, b * 2 + i + 1)
                    xt = g.x[:, bass.ds(b * TB + 2 * i, 2), :]
                    dve.tensor_tensor(xt, proj[:, i, :].rearrange("p (t d) -> p t d", t=2), xt, ALU.add).then_inc(x_done, 1)
            over_sequences(dve, body)


E = 8
SLOT_TILES = 72


def route(nc, io, g, tag, gate_by_rows, gate_name, bias_name, tiny, shared):
    with ExitStack() as ctx:
        sb = lambda name, shape, dt=F32: ctx.enter_context(nc.sbuf_tensor(f"{tag}_{name}", shape, dt))
        sem = lambda name: g.stage_semaphore(f"{tag}_{name}")
        turn = ctx.enter_context(nc.psum_tensor(f"{tag}_turn", [P, 2, BANK], F32))
        logit = ctx.enter_context(nc.psum_tensor(f"{tag}_logit", [P, 2, BANK], F32))
        count = ctx.enter_context(nc.psum_tensor(f"{tag}_count", [P, 2, NT, E], F32))
        norm = Norm(nc, ctx, g, tag, turn)
        gate = sb("gate", [P, KT, E])
        gate_rows = sb("gate_rows", [E, D])
        gate_bias = sb("gate_bias", [P, E])
        mean_all, rstd_all = sb("mean_all", [P, NT]), sb("rstd_all", [P, NT])
        L, EX, PR = (sb(n, [P, NT, E]) for n in ("L", "EX", "PR"))
        CAND, REST, POS, BOTH = (sb(n, [P, NT, E]) for n in ("CAND", "REST", "POS", "BOTH"))
        CHOICE = sb("CHOICE", [P, 2, NT, E])
        R1, R2 = sb("R1", [P, NT]), sb("R2", [P, NT])
        TOP = sb("TOP", [P, 2, NT])
        POSF = sb("POSF", [P, NT, 2])
        rank = sb("rank", [P, E])
        rank_i = sb("rank_i", [P, E], I32)
        before = sb("before", [P, P])
        upto = sb("upto", [P, NT, E])
        tiles, tiles_i, tiles_end, tiles_start = sb("tiles", [P, E]), sb("tiles_i", [P, E], I32), sb("tiles_end", [P, E]), sb("tiles_start", [P, E])
        tile_no_i, tile_no = sb("tile_no_i", [1, SLOT_TILES], I32), sb("tile_no", [1, SLOT_TILES])
        past, expert_f = sb("past", [1, SLOT_TILES, E]), sb("expert_f", [1, SLOT_TILES])
        rows = sb("rows", [P, TB, D])
        stat4 = sb("stat4", [P, 2, TB])
        slot4 = sb("slot4", [P, TB, 2], I32)

        loaded, ready, gate_turned, gate_kept = sem("loaded"), sem("ready"), sem("gate_turned"), sem("gate_kept")
        l_done, l_kept, stats_kept = sem("l_done"), sem("l_kept"), sem("stats_kept")
        chain, shifted, exp_done, chosen, counted = sem("chain"), sem("shifted"), sem("exp_done"), sem("chosen"), sem("counted")
        placed, staged, rows_ready = sem("placed"), sem("staged"), sem("rows_ready")
        sorted_ = [sem(f"sorted{t}") for t in range(TB)]
        own_stored = [sem(f"own_stored{t}") for t in range(TB)]
        block = ctx.enter_context(nc.Block())

        @block.sync
        def _(sp):
            if gate_by_rows:
                sp.dma_start(gate_rows[:, :], io[gate_name]).then_inc(loaded, 16)
            else:
                sp.dma_start(gate[:, :, :], io[gate_name].rearrange("(k p) e -> p k e", p=P)).then_inc(loaded, 16)
            if bias_name:
                sp.wait_ge(ready, 1)
                sp.dma_start(gate_bias[:, :], io[bias_name].partition_broadcast(P)).then_inc(loaded, 16)
            if shared:
                own = g.slots_x[SLOT_TILES * P:, :].rearrange("(i p) d -> i p d", p=P)

                def store(b, nxt):
                    for t in range(TB):
                        sp.wait_ge(rows_ready, b * TB + t + 1)
                        sp.dma_start(own[b * TB + t], rows[:, t, :]).then_inc(own_stored[t], 16)
                over_sequences(sp, store)
                for t in range(TB):
                    sp.wait_ge(own_stored[t], 16 * B)

        LOADS = 32 if bias_name else 16

        @block.gpsimd
        def _(pool):
            pool.memset(gate_bias[:, :], 0.0).then_inc(ready, 1)
            pool.memset(before[:, :], 1.0).then_inc(ready, 1)
            pool.iota(rank_i[:, :], [[-1, E]], base=E, channel_multiplier=0).then_inc(ready, 1)
            pool.iota(tile_no_i[:, :], [[1, SLOT_TILES]], base=0, channel_multiplier=0).then_inc(ready, 1)
            pool.wait_ge(ready, 4)
            pool.affine_select(out=before[:, :], in_=before[:, :], compare_op=ALU.is_gt, fill=0.0, base=0,
                               pattern=[[1, P]], channel_multiplier=-1).then_inc(ready, 1)
            norm.gpsimd(0)

            def keep_stats(b, nxt):
                pool.wait_ge(norm.rstd_done, b + 1)
                pool.tensor_copy(mean_all[:, bass.ds(b * TB, TB)], norm.mean[:, :]).then_inc(stats_kept, 1)
                pool.tensor_copy(rstd_all[:, bass.ds(b * TB, TB)], norm.rstd[:, :]).then_inc(stats_kept, 1)
                if nxt is not None:
                    pool.wait_ge(stats_kept, b * 2 + 2)
                    norm.gpsimd(nxt)
            over_sequences(pool, keep_stats)

            pool.wait_ge(g.zeroed, 16)

            def scatter(b, nxt):
                for t in range(TB):
                    wait_apart(pool, rows_ready, b * TB + t + 1, (g.zeroed, 16))
                    for c in range(2):
                        pool.indirect_dma_start(g.slots_x[0:SLOT_TILES * P, :], bass.IndirectOffsetOnAxis(ap=slot4[:, t, c:c + 1], axis=0),
                                                rows[:, t, :], None).then_inc(sorted_[t], 16)
            over_sequences(pool, scatter)
            for t in range(TB):
                pool.wait_ge(sorted_[t], 32 * B)

        @block.tensor
        def _(pe):
            pe.wait_ge(loaded, LOADS)
            pe.wait_ge(ready, 5)
            if gate_by_rows:
                for k in range(KT):
                    last = pe.transpose(logit[:, 0, k * E:(k + 1) * E], gate_rows[:, k * P:(k + 1) * P], g.ident[0:E, 0:E])
                last.then_inc(gate_turned, 1)
                pe.wait_ge(gate_kept, 1)
            norm.tensor(0)

            def body(b, nxt):
                if nxt is not None:
                    norm.tensor(nxt)
                pe.wait_ge(norm.columns_done, b + 1)
                after(pe, l_kept, b)
                for t in range(TB):
                    for k in range(KT):
                        last = pe.matmul(logit[:, 0, t * E:(t + 1) * E], norm.xnT[:, k, t * P:(t + 1) * P], gate[:, k, :],
                                         start=k == 0, stop=k == KT - 1)
                last.then_inc(l_done, 1)
            over_sequences(pe, body)
            pe.wait_ge(chosen, 1)
            pe.matmul(count[:, 0].rearrange("p t e -> p (t e)"), before[:, :], BOTH[:, :, :].rearrange("p t e -> p (t e)"), start=True, stop=True)
            pe.matmul(count[:, 1].rearrange("p t e -> p (t e)"), g.ones[:, :], BOTH[:, :, :].rearrange("p t e -> p (t e)"),
                      start=True, stop=True).then_inc(counted, 1)

        @block.scalar
        def _(act):
            if gate_by_rows:
                act.wait_ge(gate_turned, 1)
                act.activation(gate[:, :, :], logit[:, 0, 0:KT * E].rearrange("p (k e) -> p k e", k=KT), ACT.Copy).then_inc(gate_kept, 1)
            norm.scalar(0)

            def body(b, nxt):
                if nxt is not None:
                    norm.scalar(nxt, free=[(l_done, b + 1)])
            over_sequences(act, body)
            act.wait_ge(shifted, 1)
            act.activation(EX[:, :, :], L[:, :, :], ACT.Exp).then_inc(exp_done, 1)

        @block.vector
        def _(dve):
            norm.vector_stats(0)
            norm.vector_rows(0)

            def body(b, nxt):
                if nxt is not None:
                    dve.wait_ge(stats_kept, b * 2 + 2)
                    norm.vector_stats(nxt)
                    norm.vector_rows(nxt)
                dve.wait_ge(l_done, b + 1)
                dve.tensor_tensor(L[:, bass.ds(b * TB, TB), :], logit[:, 0, 0:TB * E].rearrange("p (t e) -> p t e", t=TB),
                                  gate_bias[:, :].unsqueeze(1).broadcast_to([P, TB, E]), ALU.add).then_inc(l_kept, 1)
            dve.wait_ge(loaded, LOADS)
            dve.wait_ge(ready, 5)
            over_sequences(dve, body)

            steps = [0]

            def link(ins):
                steps[0] += 1
                ins.then_inc(chain, 1)
                dve.wait_ge(chain, steps[0])

            def bc(a):
                return a.unsqueeze(2).broadcast_to([P, NT, E])

            def bt(a):
                return a.unsqueeze(1).broadcast_to([P, NT, E])

            dve.wait_ge(l_kept, B)
            link(dve.tensor_reduce(R1[:, :], L[:, :, :], AX.X, ALU.max))
            dve.tensor_tensor(L[:, :, :], L[:, :, :], bc(R1[:, :]), ALU.subtract).then_inc(shifted, 1)
            link(dve.tensor_copy(rank[:, :], rank_i[:, :]))
            link(dve.tensor_copy(tile_no[:, :], tile_no_i[:, :]))
            dve.wait_ge(exp_done, 1)
            link(dve.tensor_reduce(R1[:, :], EX[:, :, :], AX.X, ALU.add))
            link(dve.reciprocal(R2[:, :], R1[:, :]))
            link(dve.tensor_tensor(PR[:, :, :], EX[:, :, :], bc(R2[:, :]), ALU.mult))
            for c in range(2):
                left = PR if c == 0 else REST
                link(dve.tensor_reduce(TOP[:, c], left[:, :, :], AX.X, ALU.max))
                link(dve.tensor_tensor(CAND[:, :, :], left[:, :, :], bc(TOP[:, c]), ALU.is_ge))
                link(dve.tensor_tensor(CAND[:, :, :], CAND[:, :, :], bt(rank[:, :]), ALU.mult))
                link(dve.tensor_reduce(R1[:, :], CAND[:, :, :], AX.X, ALU.max))
                link(dve.tensor_tensor(CHOICE[:, c], CAND[:, :, :], bc(R1[:, :]), ALU.is_equal))
                if c == 0:
                    link(dve.scalar_tensor_tensor(out=REST[:, :, :], in0=CHOICE[:, 0], scalar=-2.0, in1=PR[:, :, :],
                                                  op0=ALU.mult, op1=ALU.add))
            dve.tensor_tensor(BOTH[:, :, :], CHOICE[:, 0], CHOICE[:, 1], ALU.add).then_inc(chosen, 1)
            link(dve.tensor_tensor(R1[:, :], TOP[:, 0], TOP[:, 1], ALU.add))
            link(dve.tensor_scalar(R1[:, :], R1[:, :], tiny, None, ALU.add))
            link(dve.reciprocal(R2[:, :], R1[:, :]))
            for c in range(2):
                link(dve.tensor_tensor(g.share[:, :, c], TOP[:, c], R2[:, :], ALU.mult))
            dve.wait_ge(counted, 1)
            for e in range(E):
                link(dve.tensor_tensor_scan(upto[:, :, e], g.ones[:, 0:NT], count[:, 1, :, e], 0.0, ALU.mult, ALU.add))
            link(dve.tensor_scalar(tiles[:, :], upto[:, NT - 1, :], float(P - 1), None, ALU.add))
            link(dve.tensor_copy(tiles_i[:, :], tiles[:, :]))
            link(dve.tensor_scalar(tiles_i[:, :], tiles_i[:, :], P.bit_length() - 1, None, ALU.logical_shift_right))
            link(dve.tensor_copy(tiles[:, :], tiles_i[:, :]))
            link(dve.tensor_tensor_scan(tiles_end[:, :], g.ones[:, 0:E], tiles[:, :], 0.0, ALU.mult, ALU.add))
            link(dve.tensor_tensor(tiles_start[:, :], tiles_end[:, :], tiles[:, :], ALU.subtract))
            link(dve.tensor_tensor(POS[:, :, :], upto[:, :, :], count[:, 1], ALU.subtract))
            link(dve.tensor_tensor(POS[:, :, :], POS[:, :, :], count[:, 0], ALU.add))
            link(dve.scalar_tensor_tensor(out=POS[:, :, :], in0=bt(tiles_start[:, :]), scalar=float(P), in1=POS[:, :, :],
                                          op0=ALU.mult, op1=ALU.add))
            for c in range(2):
                link(dve.tensor_tensor(CAND[:, :, :], CHOICE[:, c], POS[:, :, :], ALU.mult))
                link(dve.tensor_reduce(POSF[:, :, c], CAND[:, :, :], AX.X, ALU.add))
            link(dve.tensor_copy(g.slot[:, :, :], POSF[:, :, :]))
            link(dve.tensor_tensor(past[:, :, :], tile_no[:, :].unsqueeze(2).broadcast_to([1, SLOT_TILES, E]),
                                   tiles_end[0:1, :].unsqueeze(1).broadcast_to([1, SLOT_TILES, E]), ALU.is_ge))
            link(dve.tensor_reduce(expert_f[:, :], past[:, :, :], AX.X, ALU.add))
            link(dve.tensor_scalar(expert_f[:, :], expert_f[:, :], float(E - 1), None, ALU.min))
            link(dve.tensor_copy(g.tile_expert[:, 0:SLOT_TILES], expert_f[:, :]))
            link(dve.memset(expert_f[:, 0:NT], float(E)))
            link(dve.tensor_copy(g.tile_expert[:, SLOT_TILES:], expert_f[:, 0:NT]))

            def rows_of(b, nxt):
                for t in range(TB):
                    after(dve, sorted_[t], 32 * b)
                    if shared:
                        after(dve, own_stored[t], 16 * b)
                dve.tensor_copy(stat4[:, 0], mean_all[:, bass.ds(b * TB, TB)]).then_inc(staged, 1)
                dve.tensor_copy(stat4[:, 1], rstd_all[:, bass.ds(b * TB, TB)]).then_inc(staged, 1)
                dve.tensor_copy(slot4[:, :, :], g.slot[:, bass.ds(b * TB, TB), :]).then_inc(staged, 1)
                dve.wait_ge(staged, b * 3 + 3)
                for t in range(TB):
                    dve.tensor_scalar(rows[:, t, :], g.x[:, b * TB + t, :], stat4[:, 0, t:t + 1], stat4[:, 1, t:t + 1],
                                      ALU.subtract, ALU.mult).then_inc(rows_ready, 1)
            dve.wait_ge(stats_kept, 2 * B)
            over_sequences(dve, rows_of)


def combine(nc, g, tag, shared):
    with ExitStack() as ctx:
        sb = lambda name, shape, dt=F32: ctx.enter_context(nc.sbuf_tensor(f"{tag}_{name}", shape, dt))
        sem = lambda name: g.stage_semaphore(f"{tag}_{name}")
        slot4, share4 = sb("slot4", [P, TB, 2], I32), sb("share4", [P, TB, 2])
        rows = sb("rows", [P, TB, 2, D])
        own_rows = sb("own_rows", [P, TB, D])
        staged, used, half, whole = sem("staged"), sem("used"), sem("half"), sem("whole")
        own_in = [sem(f"own_in{t}") for t in range(TB)]
        fetched = [sem(f"fetched{t}") for t in range(TB)]
        block = ctx.enter_context(nc.Block())

        @block.gpsimd
        def _(pool):
            def body(b, nxt):
                for t in range(TB):
                    after(pool, fetched[t], 32 * b)
                after(pool, used, b * TB)
                pool.tensor_copy(slot4[:, :, :], g.slot[:, bass.ds(b * TB, TB), :]).then_inc(staged, 1)
                pool.tensor_copy(share4[:, :, :], g.share[:, bass.ds(b * TB, TB), :]).then_inc(staged, 1)
                wait_apart(pool, staged, b * 2 + 2, (staged, 2))
                for t in range(TB):
                    for c in range(2):
                        pool.indirect_dma_start(rows[:, t, c, :], None, g.slots_y[0:SLOT_TILES * P, :],
                                                bass.IndirectOffsetOnAxis(ap=slot4[:, t, c:c + 1], axis=0)).then_inc(fetched[t], 16)
            over_sequences(pool, body)

        @block.sync
        def _(sp):
            if shared:
                own = g.slots_y[SLOT_TILES * P:, :].rearrange("(i p) d -> i p d", p=P)

                def body(b, nxt):
                    for t in range(TB):
                        after(sp, used, (b - 1) * TB + t + 1)
                        sp.dma_start(own_rows[:, t, :], own[b * TB + t]).then_inc(own_in[t], 16)
                over_sequences(sp, body)

        @block.vector
        def _(dve):
            def body(b, nxt):
                dve.wait_ge(staged, b * 2 + 2)
                for t in range(TB):
                    dve.wait_ge(fetched[t], 32 * b + 32)
                    xt = g.x[:, b * TB + t, :]
                    dve.scalar_tensor_tensor(out=xt, in0=rows[:, t, 0, :], scalar=share4[:, t, 0:1], in1=xt,
                                             op0=ALU.mult, op1=ALU.add).then_inc(half, 1)
                    dve.wait_ge(half, b * TB + t + 1)
                    if shared:
                        dve.wait_ge(own_in[t], 16 * b + 16)
                        dve.tensor_tensor(xt, own_rows[:, t, :], xt, ALU.add).then_inc(whole, 1)
                        dve.wait_ge(whole, b * TB + t + 1)
                    dve.scalar_tensor_tensor(out=xt, in0=rows[:, t, 1, :], scalar=share4[:, t, 1:2], in1=xt,
                                             op0=ALU.mult, op1=ALU.add).then_inc(used, 1)
            over_sequences(dve, body)


def over_tiles(eng, n, steps, unroll=2):
    head = 4
    loops = (n - 2 - head) // unroll
    for i in range(head):
        steps(i, i % unroll, n)
    with eng.Fori(head // unroll, head // unroll + loops) as u:
        for j in range(unroll):
            steps(u * unroll + j, j, None)
    for i in range(head + loops * unroll, n + 2):
        steps(i, i % unroll, n)


def l0_experts(nc, io, g):
    F = 2 * D
    C = F // P
    N = SLOT_TILES
    with ExitStack() as ctx:
        sb = lambda name, shape, dt=F32: ctx.enter_context(nc.sbuf_tensor("e0_" + name, shape, dt))
        sem = lambda name: g.stage_semaphore("e0_" + name)
        ps = lambda name, shape: ctx.enter_context(nc.psum_tensor("e0_" + name, shape, F32))
        xt_ps, h_ps, ht_ps, y_ps = ps("xt_ps", [P, BANK]), ps("h_ps", [P, 2, BANK]), ps("ht_ps", [P, 2, BANK]), ps("y_ps", [P, 2, BANK])
        w1, w2 = sb("w1", [P, E, KT, F]), sb("w2", [P, E, C, D])
        b1, b2 = sb("b1", [P, E, F]), sb("b2", [P, E, D])
        xin, xT = sb("xin", [P, 2, D]), sb("xT", [P, 2, D])
        h, hT, y = sb("h", [P, 2, F]), sb("hT", [P, 2, F]), sb("y", [P, 2, D])

        loaded, x_in = sem("loaded"), [sem(f"x_in{j}") for j in range(2)]
        x_turned, x_kept, h_done, h_kept, h_turned, ht_kept = (sem(n) for n in ("x_turned", "x_kept", "h_done", "h_kept", "h_turned", "ht_kept"))
        y_done, y_kept, y_out = sem("y_done"), sem("y_kept"), [sem(f"y_out{j}") for j in range(2)]
        block = ctx.enter_context(nc.Block())
        rows_x = g.slots_x.rearrange("(i p) d -> i p d", p=P)
        rows_y = g.slots_y.rearrange("(i p) d -> i p d", p=P)

        @block.sync
        def _(sp):
            sp.dma_start(b1[:, :, :], io["L0_ffn_b1"].partition_broadcast(P)).then_inc(loaded, 16)
            sp.dma_start(b2[:, :, :], io["L0_ffn_b2"].partition_broadcast(P)).then_inc(loaded, 16)
            for e in range(E):
                sp.dma_start(w1[:, e], io["L0_ffn_w1"][e].rearrange("(k p) f -> p k f", p=P)).then_inc(loaded, 16)
                sp.dma_start(w2[:, e], io["L0_ffn_w2"][e].rearrange("(c p) d -> p c d", p=P)).then_inc(loaded, 16)

            def fetch(i, j):
                after(sp, x_turned, i - 1)
                sp.dma_start(xin[:, j, :], rows_x[i]).then_inc(x_in[j], 16)

            fetch(0, 0)
            fetch(1, 1)

            def steps(i, j, n):
                if n is None or 2 <= i:
                    sp.wait_ge(y_kept, i - 1)
                    sp.dma_start(rows_y[i - 2], y[:, j, :]).then_inc(y_out[j], 16)
                if n is None or i + 2 < n:
                    fetch(i + 2, j)
            over_tiles(sp, N, steps)
            for j in range(2):
                sp.wait_ge(y_out[j], 16 * N // 2)

        @block.tensor
        def _(pe):
            def turn_x(i, j):
                pe.wait_ge(x_in[j], (i - j) * 8 + 16)
                after(pe, x_kept, i)
                for k in range(KT):
                    last = pe.transpose(xt_ps[:, k * P:(k + 1) * P], xin[:, j, k * P:(k + 1) * P], g.ident[:, :])
                last.then_inc(x_turned, 1)

            turn_x(0, 0)
            pe.wait_ge(loaded, 16 * (2 + 2 * E))

            def steps(i, j, n):
                if n is None or i < n:
                    e = pe.value_load(g.tile_expert[0:1, i:i + 1] if isinstance(i, int) else g.tile_expert[0:1, bass.ds(i, 1)],
                                      min_val=0, max_val=E - 1)
                    pe.wait_ge(x_kept, i + 1)
                    after(pe, h_kept, i - 1)
                    for k in range(KT):
                        last = pe.matmul(h_ps[:, j, :], xT[:, j, k * P:(k + 1) * P], w1[:, e, k, :], start=k == 0, stop=k == KT - 1)
                    last.then_inc(h_done, 1)
                if n is None or 1 <= i <= n:
                    pe.wait_ge(h_kept, i)
                    after(pe, ht_kept, i - 2)
                    for c in range(C):
                        last = pe.transpose(ht_ps[:, 1 - j, c * P:(c + 1) * P], h[:, 1 - j, c * P:(c + 1) * P], g.ident[:, :])
                    last.then_inc(h_turned, 1)
                if n is None or 2 <= i:
                    e = pe.value_load(g.tile_expert[0:1, i - 2:i - 1] if isinstance(i, int) else g.tile_expert[0:1, bass.ds(i - 2, 1)],
                                      min_val=0, max_val=E - 1)
                    pe.wait_ge(ht_kept, i - 1)
                    after(pe, y_kept, i - 3)
                    for c in range(C):
                        last = pe.matmul(y_ps[:, j, 0:D], hT[:, j, c * P:(c + 1) * P], w2[:, e, c, :], start=c == 0, stop=c == C - 1)
                    last.then_inc(y_done, 1)
                if n is None or i + 1 < n:
                    turn_x(i + 1, 1 - j)
            over_tiles(pe, N, steps)

        @block.scalar
        def _(act):
            def steps(i, j, n):
                if n is None or 1 <= i <= n:
                    act.wait_ge(h_turned, i)
                    after(act, y_done, i - 2)
                    act.activation(hT[:, 1 - j, :], ht_ps[:, 1 - j, :], ACT.Relu).then_inc(ht_kept, 1)
            over_tiles(act, N, steps)

        @block.vector
        def _(dve):
            def keep_x(i, j):
                dve.wait_ge(x_turned, i + 1)
                after(dve, h_done, i - 1)
                dve.tensor_copy(xT[:, j, :], xt_ps[:, 0:D]).then_inc(x_kept, 1)

            keep_x(0, 0)
            dve.wait_ge(loaded, 16 * (2 + 2 * E))

            def steps(i, j, n):
                if n is None or i < n:
                    e = dve.value_load(g.tile_expert[0:1, i:i + 1] if isinstance(i, int) else g.tile_expert[0:1, bass.ds(i, 1)],
                                       min_val=0, max_val=E - 1)
                    dve.wait_ge(h_done, i + 1)
                    after(dve, h_turned, i - 1)
                    dve.tensor_tensor(h[:, j, :], h_ps[:, j, :], b1[:, e, :], ALU.add).then_inc(h_kept, 1)
                if n is None or 2 <= i:
                    e = dve.value_load(g.tile_expert[0:1, i - 2:i - 1] if isinstance(i, int) else g.tile_expert[0:1, bass.ds(i - 2, 1)],
                                       min_val=0, max_val=E - 1)
                    dve.wait_ge(y_done, i - 1)
                    if n is None or i >= 4:
                        dve.wait_ge(y_out[j], (i - j) * 8 - 16)
                    dve.tensor_tensor(y[:, j, :], y_ps[:, j, 0:D], b2[:, e, :], ALU.add).then_inc(y_kept, 1)
                if n is None or i + 1 < n:
                    keep_x(i + 1, 1 - j)
            over_tiles(dve, N, steps)


def l0_ffn(nc, io, g):
    route(nc, io, g, "r0", False, "L0_ffn_router_w", "L0_ffn_router_b", 0.0, False)
    l0_experts(nc, io, g)
    combine(nc, g, "m0", False)


def l1_experts(nc, io, g):
    F = io["L1_ffn_sg"].shape[1]
    H = F // 2
    C = -(-F // P)
    N = SLOT_TILES + NT
    NE = E + 1
    with ExitStack() as ctx:
        sb = lambda name, shape, dt=F32: ctx.enter_context(nc.sbuf_tensor("e1_" + name, shape, dt))
        sem = lambda name: g.stage_semaphore("e1_" + name)
        ps = lambda name, shape: ctx.enter_context(nc.psum_tensor("e1_" + name, shape, F32))
        up_ps, ht_ps, xt_ps, y_ps = ps("up_ps", [P, 4, BANK]), ps("ht_ps", [P, 2, BANK]), ps("xt_ps", [P, BANK]), ps("y_ps", [P, BANK])
        wgu, wd = sb("wgu", [P, NE, KT, 2, F]), sb("wd", [P, NE, C, D])
        xin, xT = sb("xin", [P, 2, D]), sb("xT", [P, 2, D])
        act_g, h = sb("act_g", [P, H]), sb("h", [P, C * P])
        hT, y = sb("hT", [P, 2, C * P]), sb("y", [P, 2, D])

        ready, loaded, x_in = sem("ready"), sem("loaded"), [sem(f"x_in{j}") for j in range(2)]
        x_turned, x_kept, up_done, gated, h_kept, h_turned, ht_kept = (
            sem(n) for n in ("x_turned", "x_kept", "up_done", "gated", "h_kept", "h_turned", "ht_kept"))
        y_done, y_kept, y_out = sem("y_done"), sem("y_kept"), [sem(f"y_out{j}") for j in range(2)]
        block = ctx.enter_context(nc.Block())
        rows_x = g.slots_x.rearrange("(i p) d -> i p d", p=P)
        rows_y = g.slots_y.rearrange("(i p) d -> i p d", p=P)
        LOADS = 16 * 4 * NE

        @block.sync
        def _(sp):
            sp.wait_ge(ready, 2)
            for e in range(NE):
                wg, wu, w = ((io["L1_ffn_wg"][e], io["L1_ffn_wu"][e], io["L1_ffn_wd"][e]) if e < E else
                             (io["L1_ffn_sg"], io["L1_ffn_su"], io["L1_ffn_sd"]))
                sp.dma_start(wgu[:, e, :, 0, :], wg.rearrange("(k p) f -> p k f", p=P)).then_inc(loaded, 16)
                sp.dma_start(wgu[:, e, :, 1, :], wu.rearrange("(k p) f -> p k f", p=P)).then_inc(loaded, 16)
                sp.dma_start(wd[:, e, 0:C - 1, :], w[0:(C - 1) * P, :].rearrange("(c p) d -> p c d", p=P)).then_inc(loaded, 16)
                sp.dma_start(wd[0:F - (C - 1) * P, e, C - 1, :], w[(C - 1) * P:, :]).then_inc(loaded, 16)

            def fetch(i, j):
                after(sp, x_turned, i - 1)
                sp.dma_start(xin[:, j, :], rows_x[i]).then_inc(x_in[j], 16)

            fetch(0, 0)
            fetch(1, 1)

            def steps(i, j, n):
                if n is None or 2 <= i:
                    sp.wait_ge(y_kept, i - 1)
                    sp.dma_start(rows_y[i - 2], y[:, j, :]).then_inc(y_out[j], 16)
                if n is None or i + 2 < n:
                    fetch(i + 2, j)
            over_tiles(sp, N, steps)
            for j in range(2):
                sp.wait_ge(y_out[j], 16 * N // 2)

        @block.gpsimd
        def _(pool):
            pool.memset(wd[:, :, C - 1, :], 0.0).then_inc(ready, 1)
            pool.memset(h[:, F:], 0.0).then_inc(ready, 1)

        @block.tensor
        def _(pe):
            def turn_x(i, j):
                pe.wait_ge(x_in[j], (i - j) * 8 + 16)
                after(pe, x_kept, i)
                for k in range(KT):
                    last = pe.transpose(xt_ps[:, k * P:(k + 1) * P], xin[:, j, k * P:(k + 1) * P], g.ident[:, :])
                last.then_inc(x_turned, 1)

            turn_x(0, 0)
            pe.wait_ge(loaded, LOADS)

            def steps(i, j, n):
                if n is None or i < n:
                    e = pe.value_load(g.tile_expert[0:1, i:i + 1] if isinstance(i, int) else g.tile_expert[0:1, bass.ds(i, 1)],
                                      min_val=0, max_val=E)
                    pe.wait_ge(x_kept, i + 1)
                    for half in range(2):
                        after(pe, h_kept, 2 * i - 1 + half)
                        for u in range(2):
                            for k in range(KT):
                                last = pe.matmul(up_ps[:, 2 * half + u, 0:H], xT[:, j, k * P:(k + 1) * P],
                                                 wgu[:, e, k, u, half * H:(half + 1) * H], start=k == 0, stop=k == KT - 1)
                            last.then_inc(up_done, 1)
                if n is None or 1 <= i <= n:
                    pe.wait_ge(h_kept, 2 * i)
                    after(pe, ht_kept, i - 1)
                    for c in range(C):
                        last = pe.transpose(ht_ps[:, c // 4, (c % 4) * P:(c % 4 + 1) * P], h[:, c * P:(c + 1) * P], g.ident[:, :])
                    last.then_inc(h_turned, 1)
                if n is None or 2 <= i:
                    e = pe.value_load(g.tile_expert[0:1, i - 2:i - 1] if isinstance(i, int) else g.tile_expert[0:1, bass.ds(i - 2, 1)],
                                      min_val=0, max_val=E)
                    pe.wait_ge(ht_kept, i - 1)
                    after(pe, y_kept, i - 2)
                    for c in range(C):
                        last = pe.matmul(y_ps[:, 0:D], hT[:, j, c * P:(c + 1) * P], wd[:, e, c, :], start=c == 0, stop=c == C - 1)
                    last.then_inc(y_done, 1)
                if n is None or i + 1 < n:
                    turn_x(i + 1, 1 - j)
            over_tiles(pe, N, steps)

        @block.scalar
        def _(act):
            def steps(i, j, n):
                if n is None or i < n:
                    for half in range(2):
                        act.wait_ge(up_done, 4 * i + 2 * half + 1)
                        after(act, h_kept, 2 * i + half)
                        act.activation(act_g[:, :], up_ps[:, 2 * half, 0:H], ACT.Silu).then_inc(gated, 1)
                if n is None or 1 <= i <= n:
                    act.wait_ge(h_turned, i)
                    after(act, y_done, i - 2)
                    act.activation(hT[:, 1 - j, 0:4 * P], ht_ps[:, 0, :], ACT.Copy)
                    act.activation(hT[:, 1 - j, 4 * P:], ht_ps[:, 1, 0:(C - 4) * P], ACT.Copy).then_inc(ht_kept, 1)
            over_tiles(act, N, steps)

        @block.vector
        def _(dve):
            def keep_x(i, j):
                dve.wait_ge(x_turned, i + 1)
                after(dve, up_done, 4 * (i - 1))
                dve.tensor_copy(xT[:, j, :], xt_ps[:, 0:D]).then_inc(x_kept, 1)

            keep_x(0, 0)

            def steps(i, j, n):
                if n is None or i < n:
                    for half in range(2):
                        dve.wait_ge(gated, 2 * i + half + 1)
                        dve.wait_ge(up_done, 4 * i + 2 * half + 2)
                        after(dve, h_turned, i)
                        dve.tensor_tensor(h[:, half * H:(half + 1) * H], act_g[:, :], up_ps[:, 2 * half + 1, 0:H],
                                          ALU.mult).then_inc(h_kept, 1)
                if n is None or 2 <= i:
                    dve.wait_ge(y_done, i - 1)
                    if n is None or i >= 4:
                        dve.wait_ge(y_out[j], (i - j) * 8 - 16)
                    dve.tensor_copy(y[:, j, :], y_ps[:, 0:D]).then_inc(y_kept, 1)
                if n is None or i + 1 < n:
                    keep_x(i + 1, 1 - j)
            over_tiles(dve, N, steps)


def l1_ffn(nc, io, g):
    route(nc, io, g, "r1", True, "L1_ffn_gate_w", None, 1e-20, True)
    l1_experts(nc, io, g)
    combine(nc, g, "m1", True)


def l1_attention(nc, io, g):
    HEADS, HD, GH = 16, 16, 4
    G = HEADS // GH
    UNITS = 3 * GH
    PARTS = 4 * HD
    ROW_J, ROW_I, ROW_M = PARTS, 96, 98
    NEG = -1e30
    Q_UNITS = (((3, 0),), ((2, 0), (0, 3 * P)), ((1, 0),))
    K_UNITS = (((0, 0),), ((1, 0), (3, 3 * P)), ((2, 0),))
    K_AT = {t: u * BANK + off for u, unit in enumerate(K_UNITS) for t, off in unit}
    HEAD_COLS = TB * (TB + 1) // 2 * P
    with ExitStack() as ctx:
        sb = lambda name, shape, dt=F32: ctx.enter_context(nc.sbuf_tensor("a1_" + name, shape, dt))
        sem = lambda name: g.stage_semaphore("a1_" + name)
        ps = lambda name, shape: ctx.enter_context(nc.psum_tensor("a1_" + name, shape, F32))
        work = ps("work", [P, 2, BANK])
        s_ps, st_ps = ps("s_ps", [P, 2, BANK]), ps("st_ps", [P, 2, BANK])
        o_ps, m_ps = ps("o_ps", [P, BANK]), ps("m_ps", [P, BANK])
        norm = Norm(nc, ctx, g, "a1", work)
        w = sb("w", [P, KT, 3 * D])
        w_qk = sb("w_qk", [P, KT, 2, KT, P])
        bias = sb("bias", [P, 2, KT])
        bv = sb("bv", [P, D])
        w_out = sb("w_out", [P, G, D])
        hi, lo = sb("hi", [P, 2, KT, S], F32R), sb("lo", [P, 2, KT, S], F32R)
        qs, ks = sb("qs", [P, HEADS, S], F32R), sb("ks", [P, HEADS, S], F32R)
        v = sb("v", [P, TB, HEADS, 2 * HD])
        slope, slope_hi, slope_lo = sb("slope", [1, HEADS]), sb("slope_hi", [1, HEADS], F32R), sb("slope_lo", [1, HEADS], F32R)
        slope2 = sb("slope2", [P, HEADS], F32R)
        count_i, count = sb("count_i", [P, S], I32), sb("count", [P, S])
        causal = sb("causal", [P, S])
        causalT = sb("causalT", [P, P], F32R)
        causalT_f = sb("causalT_f", [P, P])
        ident_r = sb("ident_r", [P, P], F32R)
        pick = sb("pick", [P, P])
        most = sb("most", [P, 2, GH, TB])
        m_hi, m_lo = sb("m_hi", [GH * TB, 2, P], F32R), sb("m_lo", [GH * TB, 2, P], F32R)
        prob = sb("prob", [P, GH, HEAD_COLS])
        o_raw, rinv, o = sb("o_raw", [P, S]), sb("rinv", [P, S]), sb("o", [P, G, S])

        loaded, ready, consts = sem("loaded"), sem("ready"), sem("consts")
        slopes_placed = sem("slopes_placed")
        qk_done, qk_hi, qk_lo = sem("qk_done"), sem("qk_hi"), sem("qk_lo")
        v_done, v_kept = sem("v_done"), sem("v_kept")
        s_done, max_done, m_turned, m_high, m_low = sem("s_done"), sem("max_done"), sem("m_turned"), sem("m_high"), sem("m_low")
        st_done, exp_done = sem("st_done"), sem("exp_done")
        o_done, o_kept, sums_done, rinv_done, o_normed = sem("o_done"), sem("o_kept"), sem("sums_done"), sem("rinv_done"), sem("o_normed")
        w_done, x_done = sem("w_done"), sem("x_done")
        spread = [sem(f"spread{i}") for i in range(KT)]
        m_placed = [sem(f"m_placed{i}") for i in range(G)]
        block = ctx.enter_context(nc.Block())
        SPREAD, PLACED = 16 * 8, 16 * 2
        CONSTS = 13
        LOADS = 16 * (1 + 4 + 1 + HEADS + 1 + 1)

        @block.sync
        def _(sp):
            sp.wait_ge(ready, 1)
            sp.dma_start(w[:, :, :], io["L1_attn_W_kqv"].rearrange("(k p) e -> p k e", p=P)).then_inc(loaded, 16)
            for i in range(2):
                for k in range(KT):
                    at = (1 - i) * D + k * P
                    sp.dma_start(bias[:, i, k:k + 1], io["L1_attn_b_kqv"][at:at + P].rearrange("(h d) -> d h", d=HD),
                                 allow_slow_non_contiguous=True).then_inc(loaded, 16)
            sp.dma_start(bv[:, :], io["L1_attn_b_kqv"][2 * D:3 * D].partition_broadcast(P)).then_inc(loaded, 16)
            for head in range(HEADS):
                r = 2 * HD * (head % GH)
                sp.dma_start(w_out[r:r + HD, head // GH, :], io["L1_attn_W_proj"][head * HD:(head + 1) * HD, :]).then_inc(loaded, 16)
            sp.dma_start(w_out[HD:HD + 1, 0, :], io["L1_attn_b_proj"].rearrange("(o d) -> o d", o=1)).then_inc(loaded, 16)
            sp.dma_start(slope[:, :], io["L1_attn_slopes"].rearrange("(o h) -> o h", o=1)).then_inc(loaded, 16)
            sp.wait_ge(consts, 2)
            for r in (ROW_J, ROW_I):
                sp.dma_start(slope2[r:r + 1, :].bitcast(F32), slope_hi[:, :].bitcast(F32)).then_inc(slopes_placed, 16)
                sp.dma_start(slope2[r + 1:r + 2, :].bitcast(F32), slope_lo[:, :].bitcast(F32)).then_inc(slopes_placed, 16)
            sp.wait_ge(ready, 5)
            sp.wait_ge(consts, CONSTS)

            def spread_half(b, half):
                sp.wait_ge(qk_lo, 4 * b + 2 * half + 2)
                heads = slice(half * HEADS // 2, (half + 1) * HEADS // 2)
                for part in range(4):
                    rows = slice(part * HD, (part + 1) * HD)
                    for dst, src in ((qs, (hi, lo)[part % 2][:, 0]), (ks, (hi, lo)[part // 2][:, 1])):
                        sp.dma_start(dst[rows, heads, :].bitcast(F32), src[:, half, :].bitcast(F32)).then_inc(spread[half], 16)

            spread_half(0, 0)

            def body(b, nxt):
                for gr in range(G):
                    n = b * G + gr
                    sp.wait_ge(m_low, n + 1)
                    for i, part in enumerate((m_hi, m_lo)):
                        sp.dma_start(qs[ROW_M + i:ROW_M + i + 1, gr * GH:(gr + 1) * GH, :].rearrange("o h (t q) -> o (h t) q", t=TB).bitcast(F32),
                                     part[:, gr % 2, :].bitcast(F32)).then_inc(m_placed[gr], 16)
                    if gr == 0:
                        spread_half(b, 1)
                    if gr == 2 and nxt is not None:
                        spread_half(nxt, 0)
            over_sequences(sp, body)

        @block.gpsimd
        def _(pool):
            pool.memset(w_out[:, :, :], 0.0).then_inc(ready, 1)
            pool.memset(qs[:, :, :].bitcast(F32), 0.0).then_inc(ready, 1)
            pool.memset(ks[:, :, :].bitcast(F32), 0.0).then_inc(ready, 1)
            pool.memset(v[:, :, :, HD:], 0.0).then_inc(ready, 1)
            pool.wait_ge(ready, 4)
            pool.memset(v[:, :, :, HD:HD + 1], 1.0).then_inc(ready, 1)
            pool.iota(count_i[:, :], [[1, S]], base=0, channel_multiplier=0).then_inc(ready, 1)
            pool.memset(causal[:, :], 0.0).then_inc(ready, 1)
            pool.memset(causalT_f[:, :], 0.0).then_inc(ready, 1)
            pool.memset(pick[:, :], 0.0).then_inc(ready, 1)
            pool.wait_ge(ready, 9)
            pool.affine_select(out=causal[:, S - P:], in_=causal[:, S - P:], compare_op=ALU.is_ge, fill=NEG, base=0,
                               pattern=[[-1, P]], channel_multiplier=1).then_inc(ready, 1)
            pool.affine_select(out=causalT_f[:, :], in_=causalT_f[:, :], compare_op=ALU.is_ge, fill=NEG, base=0,
                               pattern=[[1, P]], channel_multiplier=-1).then_inc(ready, 1)
            pick3 = pick[:, :].rearrange("p (a c) -> p a c", a=GH)
            pool.affine_select(out=pick3, in_=pick3, compare_op=ALU.not_equal, fill=1.0, base=-HD,
                               pattern=[[-2 * HD, GH], [0, 2 * HD]], channel_multiplier=1).then_inc(ready, 1)
            norm.gpsimd(0)

            def body(b, nxt):
                if nxt is not None:
                    norm.gpsimd(nxt)
            over_sequences(pool, body)

        READY = 12

        @block.tensor
        def _(pe):
            def project_qk(b):
                pe.wait_ge(norm.columns_done, b + 1)
                for i in range(4):
                    if i >= 2:
                        pe.wait_ge(qk_lo, 4 * b + i - 1)
                    for k in range(KT):
                        last = pe.matmul(work[:, i % 2, :], w_qk[:, k, i % 2, i // 2], norm.xnT[:, k, :], start=k == 0, stop=k == KT - 1)
                    last.then_inc(qk_done, 1)

            def project_v(b):
                pe.wait_ge(qk_lo, 4 * b + 4)
                for t in range(TB):
                    for k in range(KT):
                        last = pe.matmul(work[:, t // 2, (t % 2) * D:(t % 2 + 1) * D], norm.xnT[:, k, t * P:(t + 1) * P],
                                         w[:, k, 2 * D:], start=k == 0, stop=k == KT - 1)
                    if t % 2:
                        last.then_inc(v_done, 1)

            def score_by_query(b, gr):
                n = b * G + gr
                pe.wait_ge(spread[gr // 2], SPREAD * (b + 1))
                for u in range(UNITS):
                    head = gr * GH + u // 3
                    after(pe, max_done, UNITS * n + u - 1)
                    for t, off in Q_UNITS[u % 3]:
                        last = pe.matmul(s_ps[:, u % 2, off:off + (t + 1) * P], qs[0:ROW_M, head, t * P:(t + 1) * P],
                                         ks[0:ROW_M, head, 0:(t + 1) * P], start=True, stop=True)
                    last.then_inc(s_done, 1)

            def turn_maxima(b, gr):
                n = b * G + gr
                pe.wait_ge(max_done, UNITS * (n + 1))
                after(pe, rinv_done, n - 1)
                pe.transpose(m_ps[0:GH * TB, 0:P], most[:, gr % 2].rearrange("p h t -> p (h t)"), g.ident[:, :]).then_inc(m_turned, 1)

            def score_by_key(b, gr):
                n = b * G + gr
                pe.wait_ge(m_placed[gr], PLACED * (b + 1))
                for u in range(UNITS):
                    head = gr * GH + u // 3
                    after(pe, exp_done, UNITS * n + u - 1)
                    for t, off in K_UNITS[u % 3]:
                        pe.matmul(st_ps[:, u % 2, off:off + S - t * P], ks[:, head, t * P:(t + 1) * P], qs[:, head, t * P:],
                                  start=True, stop=False)
                        last = pe.matmul(st_ps[:, u % 2, off:off + P], ident_r[:, :], causalT[:, :], start=False, stop=True)
                    last.then_inc(st_done, 1)

            def outputs(b, gr):
                n = b * G + gr
                pe.wait_ge(exp_done, UNITS * (n + 1))
                pe.wait_ge(v_kept, 2 * b + 2)
                after(pe, o_kept, n)
                for t in range(TB):
                    for h in range(GH):
                        r = 2 * HD * h
                        last = pe.matmul(o_ps[r:r + 2 * HD, t * P:], v[:, t, gr * GH + h, :],
                                         prob[:, h, K_AT[t]:K_AT[t] + S - t * P], start=t == 0, stop=t == TB - 1)
                last.then_inc(o_done, 1)

            def spread_sums(b, gr):
                n = b * G + gr
                pe.wait_ge(o_kept, n + 1)
                after(pe, m_low, min(n + 2, B * G) if isinstance(n, int) else n + 2)
                pe.matmul(m_ps[:, :], pick[:, :], o_raw[:, :], start=True, stop=True).then_inc(sums_done, 1)

            def project_out(b, nxt):
                pe.wait_ge(o_normed, G * (b + 1))
                if nxt is not None:
                    pe.wait_ge(v_kept, 2 * b + 4)
                for t in range(TB):
                    for gr in range(G):
                        last = pe.matmul(work[:, t // 2, (t % 2) * D:(t % 2 + 1) * D], o[:, gr, t * P:(t + 1) * P], w_out[:, gr, :],
                                         start=gr == 0, stop=gr == G - 1)
                    if t % 2:
                        last.then_inc(w_done, 1)

            pe.wait_ge(loaded, LOADS)
            pe.wait_ge(consts, CONSTS)
            pe.wait_ge(ready, READY)
            norm.tensor(0)
            project_qk(0)
            score_by_query(0, 0)

            def body(b, nxt):
                for gr in range(G):
                    before = (b, gr - 1) if gr else (b - 1, G - 1)
                    first = isinstance(b, int) and b == 0
                    turn_maxima(b, gr)
                    if gr < G - 1:
                        score_by_query(b, gr + 1)
                    elif nxt is not None:
                        score_by_query(nxt, 0)
                    if gr == 2 and nxt is not None:
                        project_qk(nxt)
                    if gr or not first:
                        outputs(*before)
                    if gr == 0:
                        project_v(b)
                    score_by_key(b, gr)
                    if gr or not first:
                        spread_sums(*before)
                    if gr == 1:
                        if not first:
                            project_out(b - 1, b)
                        if nxt is not None:
                            norm.tensor(nxt, free=[(x_done, 2 * b), (v_kept, 2 * b + 2)])
            over_sequences(pe, body)
            outputs(B - 1, G - 1)
            spread_sums(B - 1, G - 1)
            project_out(B - 1, None)

        @block.scalar
        def _(act):
            def high_qk(b):
                for i in range(4):
                    act.wait_ge(qk_done, 4 * b + i + 1)
                    if i == 0:
                        for s in spread:
                            after(act, s, SPREAD * b)
                    act.activation(hi[:, i % 2, i // 2, :], work[:, i % 2, :], ACT.Identity,
                                   bias=bias[:, i % 2, i // 2:i // 2 + 1]).then_inc(qk_hi, 1)

            def high_maxima(b, gr):
                n = b * G + gr
                act.wait_ge(m_turned, n + 1)
                after(act, m_placed[(gr - 2) % G], PLACED * (b + (gr >= 2)))
                act.activation(m_hi[:, gr % 2, :], m_ps[0:GH * TB, 0:P], ACT.Copy, scale=-1.0).then_inc(m_high, 1)

            def exponentials(b, gr):
                n = b * G + gr
                after(act, o_done, n)
                for u in range(UNITS):
                    cols = sum((TB - t) * P for t, _ in K_UNITS[u % 3])
                    act.wait_ge(st_done, UNITS * n + u + 1)
                    act.activation(prob[:, u // 3, (u % 3) * BANK:(u % 3) * BANK + cols], st_ps[:, u % 2, 0:cols], ACT.Exp).then_inc(exp_done, 1)

            act.wait_ge(loaded, LOADS)
            act.wait_ge(consts, CONSTS)
            norm.scalar(0)
            high_qk(0)

            def body(b, nxt):
                for gr in range(G):
                    high_maxima(b, gr)
                    if gr == 2 and nxt is not None:
                        high_qk(nxt)
                    exponentials(b, gr)
                    if gr == 1 and nxt is not None:
                        norm.scalar(nxt, free=[(v_done, 2 * b + 2)])
            over_sequences(act, body)

        @block.vector
        def _(dve):
            dve.wait_ge(loaded, LOADS)
            dve.tensor_copy(slope_hi[:, :], slope[:, :]).then_inc(consts, 1)
            dve.wait_ge(consts, 1)
            dve.tensor_tensor(slope_lo[:, :], slope[:, :], slope_hi[:, :].bitcast(F32), ALU.subtract).then_inc(consts, 1)
            for half in range(KT):
                for i, scale in enumerate((HD ** -0.5, 1.0)):
                    at = (1 - i) * D + half * P
                    dve.tensor_scalar(w_qk[:, :, i, half, :].rearrange("p k (d h) -> p k d h", d=HD),
                                      w[:, :, at:at + P].rearrange("p k (h d) -> p k d h", d=HD), scale, None, ALU.mult).then_inc(consts, 1)
            dve.tensor_scalar(bias[:, 0, :], bias[:, 0, :], HD ** -0.5, None, ALU.mult).then_inc(consts, 1)
            dve.wait_ge(ready, READY)
            dve.tensor_copy(causalT[:, :], causalT_f[:, :]).then_inc(consts, 1)
            dve.tensor_copy(ident_r[:, :], g.ident[:, :]).then_inc(consts, 1)
            dve.tensor_copy(count[:, :], count_i[:, :]).then_inc(consts, 1)
            dve.memset(ks[ROW_I:ROW_M + 2, :, :].bitcast(F32), 1.0).then_inc(consts, 1)
            dve.wait_ge(consts, CONSTS - 2)
            dve.wait_ge(slopes_placed, 64)
            by_head = lambda r: slope2[r:r + 2, :].bitcast(F32).unsqueeze(2).broadcast_to([2, HEADS, S])
            by_place = lambda r: count[r:r + 2, :].unsqueeze(1).broadcast_to([2, HEADS, S])
            dve.tensor_copy(qs[ROW_J:ROW_J + 2, :, :], by_head(ROW_J))
            dve.tensor_copy(ks[ROW_J:ROW_J + 2, :, :], by_place(ROW_J))
            dve.tensor_scalar(qs[ROW_I:ROW_I + 2, :, :], by_place(ROW_I), -1.0, None, ALU.mult).then_inc(consts, 1)
            dve.tensor_copy(ks[ROW_I:ROW_I + 2, :, :], by_head(ROW_I)).then_inc(consts, 1)

            def low_qk(b):
                for i in range(4):
                    dve.wait_ge(qk_hi, 4 * b + i + 1)
                    part = hi[:, i % 2, i // 2, :].bitcast(F32)
                    dve.scalar_tensor_tensor(out=lo[:, i % 2, i // 2, :], in0=work[:, i % 2, :], scalar=bias[:, i % 2, i // 2:i // 2 + 1],
                                             in1=part, op0=ALU.add, op1=ALU.subtract).then_inc(qk_lo, 1)

            def maxima(b, gr):
                n = b * G + gr
                after(dve, m_turned, n - 1)
                for u in range(UNITS):
                    wait_apart(dve, s_done, UNITS * n + u + 1, (ready, READY))
                    for t, off in Q_UNITS[u % 3]:
                        cols = (t + 1) * P
                        last = dve.tensor_tensor_reduce(s_ps[:, u % 2, off:off + cols], s_ps[:, u % 2, off:off + cols], causal[:, S - cols:], 1.0,
                                                        -3.0e38, ALU.add, ALU.max, most[:, gr % 2, u // 3, t:t + 1])
                    last.then_inc(max_done, 1)

            def low_maxima(b, gr):
                n = b * G + gr
                dve.wait_ge(m_high, n + 1)
                dve.scalar_tensor_tensor(out=m_lo[:, gr % 2, :], in0=m_ps[0:GH * TB, 0:P], scalar=-1.0,
                                         in1=m_hi[:, gr % 2, :].bitcast(F32), op0=ALU.mult, op1=ALU.subtract).then_inc(m_low, 1)

            def keep_outputs(b, gr):
                n = b * G + gr
                dve.wait_ge(o_done, n + 1)
                after(dve, sums_done, n)
                after(dve, o_normed, n)
                dve.tensor_copy(o_raw[:, :], o_ps[:, :]).then_inc(o_kept, 1)

            def keep_values(b):
                for i in range(2):
                    dve.wait_ge(v_done, 2 * b + i + 1)
                    after(dve, o_done, G * b)
                    dve.tensor_tensor(v[:, 2 * i:2 * i + 2, :, 0:HD], work[:, i, :].rearrange("p (t h d) -> p t h d", t=2, h=HEADS),
                                      bv[:, :].rearrange("p (h d) -> p h d", h=HEADS).unsqueeze(1).broadcast_to([P, 2, HEADS, HD]),
                                      ALU.add).then_inc(v_kept, 1)

            def normalise(b, gr):
                n = b * G + gr
                dve.wait_ge(sums_done, n + 1)
                dve.reciprocal(rinv[:, :], m_ps[:, :]).then_inc(rinv_done, 1)
                dve.wait_ge(rinv_done, n + 1)
                after(dve, w_done, 2 * b)
                dve.tensor_tensor(o[:, gr, :], o_raw[:, :], rinv[:, :], ALU.mult).then_inc(o_normed, 1)

            def add_to_x(b):
                for i in range(2):
                    dve.wait_ge(w_done, 2 * b + i + 1)
                    xt = g.x[:, bass.ds(b * TB + 2 * i, 2), :]
                    dve.tensor_tensor(xt, work[:, i, :].rearrange("p (t d) -> p t d", t=2), xt, ALU.add).then_inc(x_done, 1)

            norm.vector_stats(0)
            norm.vector_rows(0)
            low_qk(0)
            maxima(0, 0)

            def body(b, nxt):
                for gr in range(G):
                    before = (b, gr - 1) if gr else (b - 1, G - 1)
                    first = isinstance(b, int) and b == 0
                    low_maxima(b, gr)
                    if gr < G - 1:
                        maxima(b, gr + 1)
                    elif nxt is not None:
                        maxima(nxt, 0)
                    if gr == 2 and nxt is not None:
                        low_qk(nxt)
                    if gr or not first:
                        keep_outputs(*before)
                    if gr == 0:
                        keep_values(b)
                        if nxt is not None:
                            norm.vector_stats(nxt)
                    if gr or not first:
                        normalise(*before)
                    if gr == 0 and nxt is not None:
                        norm.vector_rows(nxt)
                    if gr == 1 and not first:
                        add_to_x(b - 1)
            over_sequences(dve, body)
            keep_outputs(B - 1, G - 1)
            normalise(B - 1, G - 1)
            add_to_x(B - 1)


def l1_cross_attention(nc, io, g):
    with ExitStack() as ctx:
        sb = lambda name, shape, dt=F32: ctx.enter_context(nc.sbuf_tensor("c1_" + name, shape, dt))
        sem = lambda name: g.stage_semaphore("c1_" + name)
        ps = lambda name, shape: ctx.enter_context(nc.psum_tensor("c1_" + name, shape, F32))
        turn = ps("turn", [P, KT, S])
        sim_ps, at_ps, small = ps("sim_ps", [P, BANK]), ps("at_ps", [P, S]), ps("small", [P, BANK])
        out_ps = ps("out_ps", [P, 2, BANK])
        norm = Norm(nc, ctx, g, "c1", turn, depth=2)
        w = sb("w", [P, 4, KT, D])
        w_sim, b_sim = sb("w_sim", [P, 3, KT]), sb("b_sim", [P, 1])
        w2_wide = sb("w2_wide", [P, KT, P])
        key = sb("key", [P, KT, B * SC])
        key_bias = sb("key_bias", [P, B * SC])
        cw2 = sb("cw2", [P, B, D])
        c_rows = sb("c_rows", [P, D])
        sim = sb("sim", [P, TB, SC])
        least, total, share = (sb(n, [P, TB]) for n in ("least", "total", "share"))
        tile_least, all_least, shift = sb("tile_least", [P, 1]), sb("all_least", [1, 1]), sb("shift", [P, 1])
        att = sb("att", [P, TB, P])
        attT = sb("attT", [P, S])
        weight = sb("weight", [P, TB])
        weight_sum, weight_inv, hbar = sb("weight_sum", [P, 1]), sb("weight_inv", [P, 1]), sb("hbar", [P, KT])
        acT, prodT = sb("acT", [P, KT, S]), sb("prodT", [P, KT, S])
        w14 = sb("w14", [P, KT, D])

        loaded, ready, consts = sem("loaded"), sem("ready"), sem("consts")
        bias_done, bias_kept, cw2_done, cw2_kept, b_loaded = (sem(n) for n in ("bias_done", "bias_kept", "cw2_done", "cw2_kept", "b_loaded"))
        c_loaded = sem("c_loaded")
        sim_done, sim_kept, least_done, tile_done = sem("sim_done"), sem("sim_kept"), sem("least_done"), sem("tile_done")
        exp_done, total_done, share_done, att_done = sem("exp_done"), sem("total_done"), sem("share_done"), sem("att_done")
        tile_turned, all_done, all_spread, shift_done = sem("tile_turned"), sem("all_done"), sem("all_spread"), sem("shift_done")
        weight_done, hbar_done, hsum_done, hinv_done, hbar_kept, w14_done = (sem(n) for n in (
            "weight_done", "hbar_done", "hsum_done", "hinv_done", "hbar_kept", "w14_done"))
        att_turned, attT_kept, ac_done, ac_kept, prod_done = (sem(n) for n in (
            "att_turned", "attT_kept", "ac_done", "ac_kept", "prod_done"))
        out_done, x_done = sem("out_done"), sem("x_done")
        block = ctx.enter_context(nc.Block())
        ROW_AT, SHIFT_AT, SUM_AT, HBAR_AT = 0, P, P + 8, P + 16

        @block.sync
        def _(sp):
            sp.dma_start(w_sim[:, :, :], io["L1_xattn_w_sim"].rearrange("(f k p) -> p f k", f=3, p=P),
                         allow_slow_non_contiguous=True).then_inc(loaded, 16)
            sp.dma_start(b_sim[:, :], io["L1_xattn_b_sim"].partition_broadcast(P)).then_inc(loaded, 16)
            sp.dma_start(w[:, :, :, :], io["L1_xattn_W_qv"].rearrange("(f k p) e -> p f k e", f=4, p=P)).then_inc(loaded, 16)
            sp.wait_ge(ready, 3)
            sp.dma_start(cw2[SC:SC + 1, :, :], io["L1_xattn_b_qv"].rearrange("(o q d) -> o q d", o=1, q=1).broadcast_to([1, B, D])).then_inc(b_loaded, 16)

            def body(b, nxt):
                after(sp, ac_done, b)
                sp.dma_start(c_rows[0:SC, :], io["ctx_1024"][b]).then_inc(c_loaded, 16)
            over_sequences(sp, body)

        @block.gpsimd
        def _(pool):
            pool.memset(cw2[:, :, :], 0.0).then_inc(ready, 1)
            pool.memset(c_rows[:, :], 0.0).then_inc(ready, 1)
            pool.memset(att[:, :, SC:], 0.0).then_inc(ready, 1)
            pool.wait_ge(ready, 3)
            pool.memset(att[:, :, SC:SC + 1], 1.0).then_inc(ready, 1)

            def attend(b):
                pool.wait_ge(share_done, b + 1)
                pool.tensor_tensor(att[:, :, 0:SC], att[:, :, 0:SC], share[:, :].unsqueeze(2).broadcast_to([P, TB, SC]),
                                   ALU.mult).then_inc(att_done, 1)

            norm.gpsimd(0)
            norm.gpsimd(1)
            attend(0)

            def body(b, j):
                if within(b + 1):
                    attend(b + 1)
                if within(b + 2):
                    norm.gpsimd(b + 2)
            over_pairs(pool, body)

        @block.tensor
        def _(pe):
            pe.wait_ge(loaded, 48)
            pe.wait_ge(consts, 4)
            for k in range(KT):
                last = pe.matmul(turn[:, 0, :], w2_wide[:, k, :], g.ctxT[:, k, :], start=k == 0, stop=k == KT - 1)
            last.then_inc(bias_done, 1)
            for i in range(B):
                if i == 4:
                    pe.wait_ge(cw2_kept, 1)
                for k in range(KT):
                    last = pe.matmul(out_ps[0:SC, (i % 4) // 2, (i % 2) * D:(i % 2 + 1) * D], g.ctxT[:, k, i * SC:(i + 1) * SC], w[:, 1, k, :],
                                     start=k == 0, stop=k == KT - 1)
                if i % 4 == 3:
                    last.then_inc(cw2_done, 1)

            def similarity(b, j):
                pe.wait_ge(norm.columns_done, b + 1)
                after(pe, sim_kept, b)
                for t in range(TB):
                    for k in range(KT):
                        last = pe.matmul(sim_ps[:, t * SC:(t + 1) * SC], norm.columns[j][:, k, t * P:(t + 1) * P],
                                         key[:, k, bass.ds(b * SC, SC)], start=k == 0, stop=k == KT - 1)
                last.then_inc(sim_done, 1)

            def turn_least(b):
                pe.wait_ge(tile_done, b + 1)
                after(pe, hbar_kept, b)
                pe.matmul(small[0:1, ROW_AT:ROW_AT + P], tile_least[:, :], g.ident[:, :], start=True, stop=True).then_inc(tile_turned, 1)

            def spread_least(b):
                pe.wait_ge(all_done, b + 1)
                pe.matmul(small[:, SHIFT_AT:SHIFT_AT + 1], g.ones[0:1, :], all_least[:, :], start=True, stop=True).then_inc(all_spread, 1)

            def turn_attention(b):
                pe.wait_ge(att_done, b + 1)
                after(pe, attT_kept, b)
                for t in range(TB):
                    last = pe.transpose(at_ps[:, t * P:(t + 1) * P], att[:, t, :], g.ident[:, :])
                last.then_inc(att_turned, 1)

            def weighted_mean(b, j):
                pe.wait_ge(weight_done, b + 1)
                pe.matmul(small[:, SUM_AT:SUM_AT + TB], g.ones[:, :], weight[:, :], start=True, stop=True)
                for k in range(KT):
                    for t in range(TB):
                        last = pe.matmul(small[:, HBAR_AT + k:HBAR_AT + k + 1], norm.rows[j][:, t, k * P:(k + 1) * P], weight[:, t:t + 1],
                                         start=t == 0, stop=t == TB - 1)
                last.then_inc(hbar_done, 1)

            def attended(b):
                pe.wait_ge(attT_kept, b + 1)
                pe.wait_ge(c_loaded, (b + 1) * 16)
                for k in range(KT):
                    last = pe.matmul(turn[:, k, :], c_rows[:, k * P:(k + 1) * P], attT[:, :], start=True, stop=True)
                last.then_inc(ac_done, 1)

            def output(b, j, t):
                bank = out_ps[:, t // 2, (t % 2) * D:(t % 2 + 1) * D]
                if t % 2 == 0:
                    after(pe, x_done, b * 2 - 1 + t // 2)
                tile = slice(t * P, (t + 1) * P)
                pe.matmul(bank, attT[:, tile], cw2[:, b, :], start=True, stop=False)
                if t == 0:
                    pe.wait_ge(w14_done, (b + 1) * KT)
                for k in range(KT):
                    pe.matmul(bank, norm.columns[j][:, k, tile], w14[:, k, :], start=False, stop=False)
                if t == 0:
                    pe.wait_ge(prod_done, b + 1)
                for k in range(KT):
                    last = pe.matmul(bank, prodT[:, k, tile], w[:, 2, k, :], start=False, stop=k == KT - 1)
                if t % 2:
                    last.then_inc(out_done, 1)

            norm.tensor(0, free=[(bias_kept, 1)])
            similarity(0, 0)
            turn_least(0)
            spread_least(0)
            turn_attention(0)
            weighted_mean(0, 0)
            pe.wait_ge(cw2_kept, 2)
            pe.wait_ge(b_loaded, 16)

            def body(b, j):
                ahead = within(b + 1)
                attended(b)
                if ahead:
                    norm.tensor(b + 1, free=[(ac_kept, b + 1)], buf=1 - j)
                output(b, j, 0)
                if ahead:
                    similarity(b + 1, 1 - j)
                output(b, j, 1)
                if ahead:
                    turn_least(b + 1)
                output(b, j, 2)
                if ahead:
                    spread_least(b + 1)
                output(b, j, 3)
                if ahead:
                    turn_attention(b + 1)
                    weighted_mean(b + 1, 1 - j)
            over_pairs(pe, body)

        @block.scalar
        def _(act):
            act.wait_ge(ready, 4)
            for i in range(2):
                act.wait_ge(cw2_done, i + 1)
                act.activation(cw2[0:SC, 4 * i:4 * i + 4, :].rearrange("p (a c) d -> p a (c d)", a=2), out_ps[0:SC, :, :], ACT.Copy).then_inc(cw2_kept, 1)

            def exponentials(b):
                act.wait_ge(least_done, b + 1)
                after(act, att_turned, b)
                for t in range(TB):
                    act.activation(att[:, t, 0:SC], sim[:, t, :], ACT.Exp, bias=least[:, t:t + 1]).then_inc(exp_done, 1)

            def weights(b):
                act.wait_ge(shift_done, b + 1)
                after(act, hbar_done, b)
                act.activation(weight[:, :], least[:, :], ACT.Exp, bias=shift[:, 0:1], scale=-1.0).then_inc(weight_done, 1)

            def keep_attT(b):
                act.wait_ge(att_turned, b + 1)
                after(act, out_done, b * 2)
                act.activation(attT[:, :], at_ps[:, :], ACT.Copy).then_inc(attT_kept, 1)

            norm.scalar(0)
            exponentials(0)
            weights(0)
            keep_attT(0)

            def body(b, j):
                act.wait_ge(ac_done, b + 1)
                after(act, prod_done, b)
                act.activation(acT[:, :, :], turn[:, :, :], ACT.Copy).then_inc(ac_kept, 1)
                if within(b + 1):
                    norm.scalar(b + 1, free=[(out_done, b * 2)], buf=1 - j)
                    exponentials(b + 1)
                    weights(b + 1)
                    keep_attT(b + 1)
            over_pairs(act, body)

        @block.vector
        def _(dve):
            dve.wait_ge(loaded, 48)
            for k in range(KT):
                dve.tensor_scalar(w2_wide[:, k, :], g.ones[:, :], w_sim[:, 1, k:k + 1], None, ALU.mult).then_inc(consts, 1)
                dve.tensor_scalar(key[:, k, :], g.ctxT[:, k, :], w_sim[:, 2, k:k + 1], w_sim[:, 0, k:k + 1], ALU.mult, ALU.add).then_inc(consts, 1)
            norm.vector_stats(0)
            norm.vector_rows(0, buf=0)
            dve.wait_ge(bias_done, 1)
            dve.tensor_scalar(key_bias[:, :], turn[:, 0, :], b_sim[:, 0:1], None, ALU.add).then_inc(bias_kept, 1)
            dve.wait_ge(bias_kept, 1)
            norm.vector_stats(1)
            norm.vector_rows(1, buf=1)

            def maxima(b):
                dve.wait_ge(sim_done, b + 1)
                after(dve, exp_done, b * TB)
                dve.tensor_tensor(sim[:, :, :], sim_ps[:, 0:TB * SC].rearrange("p (t j) -> p t j", t=TB),
                                  key_bias[:, bass.ds(b * SC, SC)].unsqueeze(1).broadcast_to([P, TB, SC]), ALU.add).then_inc(sim_kept, 1)
                dve.wait_ge(sim_kept, b + 1)
                after(dve, weight_done, b)
                dve.tensor_reduce(least[:, :], sim[:, :, :], AX.X, ALU.max, negate=True).then_inc(least_done, 1)
                dve.wait_ge(least_done, b + 1)
                after(dve, tile_turned, b)
                dve.tensor_reduce(tile_least[:, :], least[:, :], AX.X, ALU.min).then_inc(tile_done, 1)

            def shares(b):
                dve.wait_ge(exp_done, (b + 1) * TB)
                dve.tensor_reduce(total[:, :], att[:, :, 0:SC], AX.X, ALU.add).then_inc(total_done, 1)
                dve.wait_ge(total_done, b + 1)
                after(dve, att_done, b)
                dve.reciprocal(share[:, :], total[:, :]).then_inc(share_done, 1)

            def shifts(b):
                dve.wait_ge(tile_turned, b + 1)
                after(dve, all_spread, b)
                dve.tensor_reduce(all_least[:, :], small[0:1, ROW_AT:ROW_AT + P], AX.X, ALU.min).then_inc(all_done, 1)
                dve.wait_ge(all_spread, b + 1)
                after(dve, weight_done, b)
                dve.tensor_copy(shift[:, :], small[:, SHIFT_AT:SHIFT_AT + 1]).then_inc(shift_done, 1)

            maxima(0)
            shares(0)
            shifts(0)

            def body(b, j):
                dve.wait_ge(hbar_done, b + 1)
                dve.tensor_reduce(weight_sum[:, :], small[:, SUM_AT:SUM_AT + TB], AX.X, ALU.add).then_inc(hsum_done, 1)
                dve.wait_ge(hsum_done, b + 1)
                dve.reciprocal(weight_inv[:, :], weight_sum[:, :]).then_inc(hinv_done, 1)
                dve.wait_ge(hinv_done, b + 1)
                dve.tensor_scalar(hbar[:, :], small[:, HBAR_AT:HBAR_AT + KT], weight_inv[:, 0:1], None, ALU.mult).then_inc(hbar_kept, 1)
                dve.wait_ge(hbar_kept, b + 1)
                after(dve, out_done, b * 2)
                for k in range(KT):
                    dve.scalar_tensor_tensor(out=w14[:, k, :], in0=w[:, 3, k, :], scalar=hbar[:, k:k + 1], in1=w[:, 0, k, :],
                                             op0=ALU.mult, op1=ALU.add).then_inc(w14_done, 1)
                dve.wait_ge(ac_kept, b + 1)
                dve.tensor_tensor(prodT[:, :, :], acT[:, :, :], norm.columns[j][:, :, :], ALU.mult).then_inc(prod_done, 1)
                if within(b + 1):
                    maxima(b + 1)
                    shares(b + 1)
                    shifts(b + 1)
                if within(b + 2):
                    norm.vector_stats(b + 2)
                    norm.vector_rows(b + 2, free=[(hbar_done, b + 1)], buf=j)
                for i in range(2):
                    dve.wait_ge(out_done, b * 2 + i + 1)
                    xt = g.x[:, bass.ds(b * TB + 2 * i, 2), :]
                    dve.tensor_tensor(xt, out_ps[:, i, :].rearrange("p (t d) -> p t d", t=2), xt, ALU.add).then_inc(x_done, 1)
            over_pairs(dve, body)


def store(nc, g, out):
    stored = g.stage_semaphore("stored")
    with nc.Block() as block:
        @block.sync
        def _(sp):
            sp.dma_start(out.rearrange("b (t p) d -> p (b t) d", p=P), g.x[:, :, :]).then_inc(stored, 16)
            sp.wait_ge(stored, 16)


def build(nc, io, out, phases=tuple(range(6))):
    stages = [l0_attention, l0_cross_attention, l0_ffn, l1_attention, l1_cross_attention, l1_ffn]
    with ExitStack() as ctx:
        g = setup(nc, ctx, io)
        g.end_stage()
        with ExitStack() as attention:
            load_context(nc, attention, io, g)
            for n in phases:
                if n < 5:
                    stages[n](nc, io, g)
                    g.end_stage()
        if 5 in phases:
            stages[5](nc, io, g)
        store(nc, g, out)


_INS = ['x', 'ctx_1024', 'mask_Bx1xSxS2_bk1', 'L0_attn_Wq', 'L0_attn_bq', 'L0_attn_Wk', 'L0_attn_bk', 'L0_attn_Wv',
        'L0_attn_bv', 'L0_xattn_Wq', 'L0_xattn_Wk', 'L0_xattn_Wv', 'L0_xattn_Wo', 'L0_ffn_router_w', 'L0_ffn_router_b',
        'L0_ffn_w1', 'L0_ffn_b1', 'L0_ffn_w2', 'L0_ffn_b2', 'L1_attn_W_kqv', 'L1_attn_b_kqv', 'L1_attn_W_proj',
        'L1_attn_b_proj', 'L1_attn_slopes', 'L1_xattn_w_sim', 'L1_xattn_b_sim', 'L1_xattn_W_qv', 'L1_xattn_b_qv',
        'L1_ffn_gate_w', 'L1_ffn_wg', 'L1_ffn_wu', 'L1_ffn_wd', 'L1_ffn_sg', 'L1_ffn_su', 'L1_ffn_sd']


def kernel(**inputs):
    import numpy as _np
    import concourse.bacc as _bacc
    from concourse import mybir as _mybir
    from concourse.bass_utils import run_bass_kernel_spmd as _run

    nc = _bacc.Bacc("TRN2", target_bir_lowering=False, num_devices=1)
    arrays, io = {}, {}
    for name in _INS:
        a = _np.ascontiguousarray(inputs[name])
        arrays[f"in_{name}"] = a
        io[name] = nc.dram_tensor(f"in_{name}", a.shape, _mybir.dt.from_np(a.dtype), kind="ExternalInput").ap()
    out = nc.dram_tensor("out", (8, 512, 256), _mybir.dt.float32, kind="ExternalOutput").ap()
    build(nc, io, out)
    r = _run(nc, [arrays], core_ids=[0])
    return r.results[0]["out"]
```

```python
from contextlib import ExitStack

import concourse.bass as bass
from concourse import mybir

ALU = mybir.AluOpType
ACT = mybir.ActivationFunctionType
AX = mybir.AxisListType
F32 = mybir.dt.float32
F32R = mybir.dt.float32r
I32 = mybir.dt.int32
U8 = mybir.dt.uint8

P = 128
B, S, D = 8, 512, 256
KT = D // P
TB = S // P
NT = B * TB
BANK = 512
SC = 64
EPS = 1e-5


def after(eng, sem, count):
    if not isinstance(count, int) or count > 0:
        eng.wait_ge(sem, count)


def wait_apart(eng, sem, count, met):
    if not isinstance(count, int):
        count = eng.to_reg(count)
    eng.wait_ge(*met)
    eng.wait_ge(sem, count)


def over_sequences(eng, body):
    body(0, 1)
    with eng.Fori(1, B - 1) as b:
        body(b, b + 1)
    body(B - 1, None)


def over_pairs(eng, body):
    body(0, 0)
    body(1, 1)
    with eng.Fori(1, B // 2 - 1) as u:
        for j in range(2):
            body(u * 2 + j, j)
    body(B - 2, 0)
    body(B - 1, 1)


def within(b):
    return not isinstance(b, int) or b < B


class Norm:

    def __init__(self, nc, ctx, g, tag, psum, depth=1):
        self.nc, self.g, self.psum = nc, g, psum
        sb = lambda name, shape, dt=F32: ctx.enter_context(nc.sbuf_tensor(f"{tag}_{name}", shape, dt))
        sem = lambda name: g.stage_semaphore(f"{tag}_{name}")
        self.stats = sb("stats", [P, TB, 6])
        self.half = sb("half", [P, 4, TB])
        self.mean = sb("mean", [P, TB])
        self.var = sb("var", [P, TB])
        self.var_eps = sb("var_eps", [P, TB])
        self.rstd = sb("rstd", [P, TB])
        self.rows = [sb(f"xn{i}", [P, TB, D]) for i in range(depth)]
        self.columns = [sb(f"xnT{i}", [P, KT, S]) for i in range(depth)]
        self.xn, self.xnT = self.rows[0], self.columns[0]
        self.depth = depth
        self.stats_done = sem("stats_done")
        self.halves_done = sem("halves_done")
        self.mean_done = sem("mean_done")
        self.var_done = sem("var_done")
        self.rstd_done = sem("rstd_done")
        self.rows_done = sem("rows_done")
        self.turned = sem("turned")
        self.columns_done = sem("columns_done")

    def vector_stats(self, b):
        v, x, st = self.nc.vector, self.g.x, self.stats
        for t in range(TB):
            v.bn_stats(st[:, t, :], x[:, b * TB + t, :]).then_inc(self.stats_done, 1)
        v.wait_ge(self.stats_done, b * TB + TB)
        v.tensor_tensor(self.half[:, 0], st[:, :, 1], st[:, :, 4], ALU.subtract).then_inc(self.halves_done, 1)
        v.tensor_tensor(self.half[:, 1], st[:, :, 1], st[:, :, 4], ALU.add).then_inc(self.halves_done, 1)
        v.tensor_tensor(self.half[:, 2], st[:, :, 2], st[:, :, 5], ALU.add).then_inc(self.halves_done, 1)
        v.wait_ge(self.halves_done, b * 4 + 3)
        v.scalar_tensor_tensor(out=self.half[:, 3], in0=self.half[:, 0], scalar=0.25, in1=self.half[:, 0],
                               op0=ALU.mult, op1=ALU.mult).then_inc(self.halves_done, 1)
        v.tensor_scalar(self.mean[:, :], self.half[:, 1], 0.5, None, ALU.mult).then_inc(self.mean_done, 1)
        v.wait_ge(self.halves_done, b * 4 + 4)
        v.scalar_tensor_tensor(out=self.var[:, :], in0=self.half[:, 2], scalar=1.0 / D, in1=self.half[:, 3],
                               op0=ALU.mult, op1=ALU.add).then_inc(self.var_done, 1)
        v.wait_ge(self.var_done, b * 2 + 1)
        v.tensor_scalar(self.var_eps[:, :], self.var[:, :], EPS, None, ALU.add).then_inc(self.var_done, 1)

    def gpsimd(self, b):
        p = self.nc.gpsimd
        p.wait_ge(self.var_done, b * 2 + 2)
        after(p, self.rows_done, b * TB)
        p.tensor_tensor(self.rstd[:, :], self.var_eps[:, :], self.g.minus_half[:, 0:TB], ALU.pow).then_inc(self.rstd_done, 1)

    def vector_rows(self, b, free=(), buf=0):
        v = self.nc.vector
        v.wait_ge(self.mean_done, b + 1)
        v.wait_ge(self.rstd_done, b + 1)
        after(v, self.turned, b - self.depth + 1)
        for s, n in free:
            after(v, s, n)
        for t in range(TB):
            v.tensor_scalar(self.rows[buf][:, t, :], self.g.x[:, b * TB + t, :], self.mean[:, t:t + 1],
                            self.rstd[:, t:t + 1], ALU.subtract, ALU.mult).then_inc(self.rows_done, 1)

    def tensor(self, b, free=(), buf=0):
        pe = self.nc.tensor
        after(pe, self.columns_done, b)
        for s, n in free:
            after(pe, s, n)
        for t in range(TB):
            pe.wait_ge(self.rows_done, b * TB + t + 1)
            for k in range(KT):
                last = pe.transpose(self.psum[:, k, t * P:(t + 1) * P], self.rows[buf][:, t, k * P:(k + 1) * P], self.g.ident[:, :])
        last.then_inc(self.turned, 1)

    def scalar(self, b, free=(), buf=0):
        a = self.nc.scalar
        a.wait_ge(self.turned, b + 1)
        for s, n in free:
            after(a, s, n)
        a.activation(self.columns[buf][:, :, :], self.psum[:, :, :], ACT.Copy).then_inc(self.columns_done, 1)


class Globals:

    def __init__(self, nc):
        self.nc, self.stage_semaphores = nc, []

    def stage_semaphore(self, name):
        self.stage_semaphores.append(self.nc.alloc_semaphore(name))
        return self.stage_semaphores[-1]

    def end_stage(self):
        self.nc.clear_and_free_semaphores(self.stage_semaphores)
        self.nc.all_engine_barrier()
        self.stage_semaphores = []


def setup(nc, ctx, io):
    g = Globals(nc)
    sb = lambda name, shape, dt=F32: ctx.enter_context(nc.sbuf_tensor(name, shape, dt))
    g.x = sb("x_rows", [P, NT, D])
    g.ident = sb("ident", [P, P])
    g.minus_half = sb("minus_half", [P, NT])
    g.ones = sb("ones", [P, P])
    g.zero_row = sb("zero_row", [P, D])
    g.slot = sb("slot", [P, NT, 2], I32)
    g.share = sb("share", [P, NT, 2])
    g.experts = sb("experts", [1, EXPERT_WORDS], I32)
    g.mean_all, g.rstd_all = sb("mean_all", [P, NT]), sb("rstd_all", [P, NT])
    g.slots_x = nc.dram_tensor("slots_x", [SLOT_TILES * P, D], F32, kind="Internal").ap()
    g.slots_y = nc.dram_tensor("slots_y", [SLOT_TILES * P, D], F32, kind="Internal").ap()
    g.zeroed = ctx.enter_context(nc.semaphore("zeroed"))
    g.x_first = ctx.enter_context(nc.semaphore("x_first"))
    g.x_rest = ctx.enter_context(nc.semaphore("x_rest"))
    consts = g.stage_semaphore("consts")
    with nc.Block() as block:
        @block.sync
        def _(sp):
            x_rows = io["x"].rearrange("b (t p) d -> p (b t) d", p=P)
            sp.dma_start(g.x[:, 0:TB, :], x_rows[:, 0:TB, :]).then_inc(g.x_first, 16)
            sp.dma_start(g.x[:, TB:, :], x_rows[:, TB:, :]).then_inc(g.x_rest, 16)

        @block.gpsimd
        def _(pool):
            pool.memset(g.ident[:, :], 0.0).then_inc(consts, 1)
            pool.memset(g.minus_half[:, :], -0.5).then_inc(consts, 1)
            pool.memset(g.ones[:, :], 1.0).then_inc(consts, 1)
            pool.memset(g.zero_row[:, :], 0.0).then_inc(consts, 1)
            pool.wait_ge(consts, 4)
            pool.affine_select(out=g.ident[:, :], in_=g.ident[:, :], compare_op=ALU.not_equal, fill=1.0,
                               base=0, pattern=[[-1, P]], channel_multiplier=1).then_inc(consts, 1)
            pool.wait_ge(consts, 5)
    return g


def l0_attention(nc, io, g):
    H = 64
    with ExitStack() as ctx:
        sb = lambda name, shape, dt=F32: ctx.enter_context(nc.sbuf_tensor("a0_" + name, shape, dt))
        sem = lambda name: g.stage_semaphore("a0_" + name)
        turn = ctx.enter_context(nc.psum_tensor("a0_turn", [P, KT, S], F32))
        proj = ctx.enter_context(nc.psum_tensor("a0_proj", [P, 2, BANK], F32))
        score = ctx.enter_context(nc.psum_tensor("a0_score", [P, 2, BANK], F32))
        shift = ctx.enter_context(nc.psum_tensor("a0_shift", [P, BANK], F32))
        norm = Norm(nc, ctx, g, "a0", turn)
        wq2, wk2 = sb("wq2", [P, KT, 2, H]), sb("wk2", [P, KT, 2, H])
        wv = sb("wv", [P, KT, D])
        bq2, bk2, bv = sb("bq2", [P, 1]), sb("bk2", [P, 1]), sb("bv", [P, D])
        qhi, qlo, khl = (sb(n, [P, S], F32R) for n in ("qhi", "qlo", "khl"))
        v1 = sb("v1", [P, TB, D + 1])
        negmax = sb("negmax", [P, TB])
        shift_hl = sb("shift_hl", [H, S], F32R)
        ones_r = sb("ones_r", [H, P], F32R)
        prob = sb("prob", [P, TB, S])
        rinv = sb("rinv", [P, TB])

        loaded, ready = sem("loaded"), sem("ready")
        qk_done, q_hi, q_lo, k_done = sem("qk_done"), sem("q_hi"), sem("q_lo"), sem("k_done")
        k_hi = sem("k_hi")
        v_done, v_kept = sem("v_done"), sem("v_kept")
        s_done, max_done = sem("s_done"), sem("max_done")
        shift_done, shift_hi, shift_lo = sem("shift_done"), sem("shift_hi"), sem("shift_lo")
        st_done, exp_done = sem("st_done"), sem("exp_done")
        o_done, rinv_done, x_done, res_done = sem("o_done"), sem("rinv_done"), sem("x_done"), sem("res_done")
        block = ctx.enter_context(nc.Block())

        @block.sync
        def _(sp):
            for half in range(2):
                sp.dma_start(wq2[:, :, half, :], io["L0_attn_Wq"].rearrange("(k p) e -> p k e", p=P)).then_inc(loaded, 16)
                sp.dma_start(wk2[:, :, half, :], io["L0_attn_Wk"].rearrange("(k p) e -> p k e", p=P)).then_inc(loaded, 16)
                sp.dma_start(bq2[half * H:(half + 1) * H, :], io["L0_attn_bq"].rearrange("(p o) -> p o", o=1)).then_inc(loaded, 16)
                sp.dma_start(bk2[half * H:(half + 1) * H, :], io["L0_attn_bk"].rearrange("(p o) -> p o", o=1)).then_inc(loaded, 16)
            sp.dma_start(wv[:, :, :], io["L0_attn_Wv"].rearrange("(k p) e -> p k e", p=P)).then_inc(loaded, 16)
            sp.dma_start(bv[:, :], io["L0_attn_bv"].partition_broadcast(P)).then_inc(loaded, 16)
            sp.wait_ge(g.x_rest, 16)
            sp.dma_start(g.slots_x.rearrange("(p r) d -> p r d", p=P),
                         g.zero_row[:, :].unsqueeze(1).broadcast_to([P, SLOT_TILES, D])).then_inc(g.zeroed, 16)

        LOADS = 16 * 10

        @block.gpsimd
        def _(pool):
            pool.memset(v1[:, :, D:D + 1], 1.0).then_inc(ready, 1)
            pool.memset(shift_hl[:, :].bitcast(F32), 0.0).then_inc(ready, 1)
            pool.memset(ones_r[:, :].bitcast(F32), 1.0).then_inc(ready, 1)
            norm.gpsimd(0)

            def body(b, nxt):
                pool.wait_ge(norm.rows_done, b * TB + TB)
                pool.tensor_tensor(g.x[:, bass.ds(b * TB, TB), :], g.x[:, bass.ds(b * TB, TB), :], norm.xn[:, :, :],
                                   ALU.add).then_inc(res_done, 1)
                if nxt is not None:
                    norm.gpsimd(nxt)
            over_sequences(pool, body)

        @block.tensor
        def _(pe):
            pe.wait_ge(loaded, LOADS)
            pe.wait_ge(ready, 3)
            norm.tensor(0)

            def body(b, nxt):
                pe.wait_ge(norm.columns_done, b + 1)
                after(pe, x_done, b * TB)
                for i, w in enumerate((wq2, wk2)):
                    for k in range(KT):
                        last = pe.matmul(proj[:, i, :], w[:, k].rearrange("p a e -> p (a e)"), norm.xnT[:, k, :],
                                         start=k == 0, stop=k == KT - 1)
                    last.then_inc(qk_done, 1)
                for t in range(TB):
                    if t % 2 == 0:
                        if t == 0:
                            pe.wait_ge(q_lo, b + 1)
                        else:
                            pe.wait_ge(k_done, b + 1)
                    for k in range(KT):
                        last = pe.matmul(proj[:, t // 2, (t % 2) * D:(t % 2 + 1) * D], norm.xnT[:, k, t * P:(t + 1) * P],
                                         wv[:, k, :], start=k == 0, stop=k == KT - 1)
                    if t % 2:
                        last.then_inc(v_done, 1)
                for t in range(TB):
                    if t >= 2:
                        pe.wait_ge(max_done, b * TB + t - 1)
                    else:
                        after(pe, exp_done, b * TB + t - 1)
                    for n, q in enumerate((qhi, qlo)):
                        last = pe.matmul(score[:, t % 2, :], q[:, t * P:(t + 1) * P], khl[:, :], start=n == 0, stop=n == 1)
                    last.then_inc(s_done, 1)
                pe.wait_ge(max_done, b * TB + TB)
                after(pe, shift_lo, b)
                for t in range(TB):
                    last = pe.matmul(shift[0:1, t * P:(t + 1) * P], negmax[:, t:t + 1], g.ident[:, :], start=True, stop=True)
                last.then_inc(shift_done, 1)
                if nxt is not None:
                    norm.tensor(nxt)
                for t in range(TB):
                    if t == 0:
                        pe.wait_ge(shift_lo, b + 1)
                    if t >= 2:
                        pe.wait_ge(exp_done, b * TB + t - 1)
                    pe.matmul(score[:, t % 2, :], khl[:, t * P:(t + 1) * P], qhi[:, :], start=True, stop=False)
                    pe.matmul(score[:, t % 2, :], khl[:, t * P:(t + 1) * P], qlo[:, :], start=False, stop=False)
                    pe.matmul(score[:, t % 2, :], ones_r[:, :], shift_hl[:, :], start=False, stop=True).then_inc(st_done, 1)
                for t in range(TB):
                    if t == 0:
                        pe.wait_ge(v_kept, b * 2 + 2)
                        pe.wait_ge(exp_done, b * TB + TB)
                    if t >= 2:
                        pe.wait_ge(x_done, b * TB + t - 1)
                    for j in range(TB):
                        last = pe.matmul(proj[:, t % 2, 0:D + 1], prob[:, j, t * P:(t + 1) * P], v1[:, j, :],
                                         start=j == 0, stop=j == TB - 1)
                    last.then_inc(o_done, 1)
            over_sequences(pe, body)

        @block.scalar
        def _(act):
            act.wait_ge(loaded, LOADS)
            norm.scalar(0)

            def body(b, nxt):
                act.wait_ge(qk_done, b * 2 + 1)
                after(act, st_done, b * TB)
                act.activation(qhi[:, :], proj[:, 0, :], ACT.Identity, bias=bq2[:, 0:1]).then_inc(q_hi, 1)
                act.wait_ge(qk_done, b * 2 + 2)
                act.activation(khl[:, :], proj[:, 1, :], ACT.Identity, bias=bk2[:, 0:1]).then_inc(k_hi, 1)
                act.wait_ge(shift_done, b + 1)
                after(act, st_done, b * TB)
                act.activation(shift_hl[0:1, :], shift[0:1, :], ACT.Copy).then_inc(shift_hi, 1)
                if nxt is not None:
                    norm.scalar(nxt, free=[(v_done, b * 2 + 2)])
                for t in range(TB):
                    act.wait_ge(st_done, b * TB + t + 1)
                    after(act, o_done, b * TB)
                    act.activation(prob[:, t, :], score[:, t % 2, :], ACT.Exp).then_inc(exp_done, 1)
            over_sequences(act, body)

        @block.vector
        def _(dve):
            dve.wait_ge(g.x_first, 16)
            norm.vector_stats(0)
            norm.vector_rows(0)
            dve.wait_ge(loaded, LOADS)

            def body(b, nxt):
                if nxt is not None:
                    if isinstance(b, int):
                        dve.wait_ge(g.x_rest, 16)
                    norm.vector_stats(nxt)
                dve.wait_ge(q_hi, b + 1)
                after(dve, st_done, b * TB)
                dve.scalar_tensor_tensor(out=qlo[:, :], in0=proj[:, 0, :], scalar=bq2[:, 0:1], in1=qhi[:, :].bitcast(F32),
                                         op0=ALU.add, op1=ALU.subtract).then_inc(q_lo, 1)
                dve.wait_ge(k_hi, b + 1)
                dve.scalar_tensor_tensor(out=khl[H:P, :], in0=proj[H:P, 1, :], scalar=bk2[H:P, 0:1],
                                         in1=khl[H:P, :].bitcast(F32), op0=ALU.add, op1=ALU.subtract).then_inc(k_done, 1)
                for i in range(2):
                    dve.wait_ge(v_done, b * 2 + i + 1)
                    after(dve, o_done, b * TB)
                    dve.tensor_tensor(v1[:, 2 * i:2 * i + 2, 0:D], proj[:, i, :].rearrange("p (t d) -> p t d", t=2),
                                      bv[:, :].unsqueeze(1).broadcast_to([P, 2, D]), ALU.add).then_inc(v_kept, 1)
                for t in range(TB):
                    dve.wait_ge(s_done, b * TB + t + 1)
                    after(dve, shift_done, b)
                    dve.tensor_reduce(negmax[:, t:t + 1], score[:, t % 2, :], AX.X, ALU.max, negate=True).then_inc(max_done, 1)
                if nxt is not None:
                    norm.vector_rows(nxt, free=[(res_done, b + 1)])
                dve.wait_ge(shift_hi, b + 1)
                dve.tensor_tensor(shift_hl[32:33, :], shift[0:1, :], shift_hl[0:1, :].bitcast(F32), ALU.subtract).then_inc(shift_lo, 1)
                for t in range(TB):
                    dve.wait_ge(o_done, b * TB + t + 1)
                    dve.reciprocal(rinv[:, t:t + 1], proj[:, t % 2, D:D + 1]).then_inc(rinv_done, 1)
                    dve.wait_ge(rinv_done, b * TB + t + 1)
                    dve.wait_ge(res_done, b + 1)
                    xt = g.x[:, b * TB + t, :]
                    dve.scalar_tensor_tensor(out=xt, in0=proj[:, t % 2, 0:D], scalar=rinv[:, t:t + 1], in1=xt,
                                             op0=ALU.mult, op1=ALU.add).then_inc(x_done, 1)
            over_sequences(dve, body)


def load_context(nc, ctx, io, g):
    g.ctxT = ctx.enter_context(nc.sbuf_tensor("ctxT", [P, KT, B * SC], F32))
    with ExitStack() as tmp:
        rows = tmp.enter_context(nc.sbuf_tensor("ctx_rows2", [P, B * SC // P, D], F32))
        turn = tmp.enter_context(nc.psum_tensor("ctx_turn", [P, KT, B * SC], F32))
        loaded, turned, kept = (g.stage_semaphore("ctx_" + n) for n in ("loaded", "turned", "kept"))
        block = tmp.enter_context(nc.Block())

        @block.sync
        def _(sp):
            sp.dma_start(rows[:, :, :], io["ctx_1024"].rearrange("(c b) j d -> (b j) c d", b=P // SC)).then_inc(loaded, 16)

        @block.tensor
        def _(pe):
            pe.wait_ge(loaded, 16)
            for c in range(B * SC // P):
                for k in range(KT):
                    last = pe.transpose(turn[:, k, c * P:(c + 1) * P], rows[:, c, k * P:(k + 1) * P], g.ident[:, :])
            last.then_inc(turned, 1)

        @block.scalar
        def _(act):
            act.wait_ge(turned, 1)
            act.activation(g.ctxT[:, :, :], turn[:, :, :], ACT.Copy).then_inc(kept, 1)
            act.wait_ge(kept, 1)


def l0_cross_attention(nc, io, g):
    HEADS, HD = 16, 16
    HH = P // HD
    PAIRS = HEADS // 2
    NEG, BIG = -1e9, 3e38
    with ExitStack() as ctx:
        sb = lambda name, shape, dt=F32: ctx.enter_context(nc.sbuf_tensor("c0_" + name, shape, dt))
        sem = lambda name: g.stage_semaphore("c0_" + name)
        turn = ctx.enter_context(nc.psum_tensor("c0_turn", [P, 2, BANK], F32))
        proj = ctx.enter_context(nc.psum_tensor("c0_proj", [P, 2, BANK], F32))
        score = ctx.enter_context(nc.psum_tensor("c0_score", [P, 2, 2, BANK], F32))
        norm = Norm(nc, ctx, g, "c0", turn)
        w_rows = sb("w_rows", [P, 4, KT, D])
        wT = sb("wT", [P, 4, KT, D])
        mask8 = sb("mask8", [P, NT, SC], U8)
        cap = sb("cap", [P, NT, SC])
        kT = sb("kT", [P, KT, B * SC])
        head_of_row = sb("head_of_row", [P, HH])
        head_of_key = sb("head_of_key", [P, 2 * HD])
        kblk = sb("kblk", [P, KT, HH, SC])
        ctx2 = sb("ctx2", [P, KT, 2, SC])
        vblk = [sb(f"vblk{j}", [P, PAIRS, 2 * HD]) for j in range(2)]
        qT = sb("qT", [P, KT, S])
        prob = [sb(f"prob{j}", [P, TB, HEADS * SC]) for j in range(2)]
        most, total, share = (sb(n, [P, TB, HEADS]) for n in ("most", "total", "share"))
        probT = sb("probT", [P, PAIRS, S])
        oT = sb("oT", [P, KT, S])

        loaded, masks, ready, caps = sem("loaded"), sem("masks"), sem("ready"), sem("caps")
        w_turned, w_kept, kt_done, kt_kept = sem("w_turned"), sem("w_kept"), sem("kt_done"), sem("kt_kept")
        kblk_done, ctx2_done = sem("kblk_done"), sem("ctx2_done")
        q_done, q_kept, v_done, v_kept = sem("q_done"), sem("q_kept"), sem("v_done"), sem("v_kept")
        s_done, capped, max_done, less_max = sem("s_done"), sem("capped"), sem("max_done"), sem("less_max")
        exp_done, sum_done, share_done, prob_done = sem("exp_done"), sem("sum_done"), sem("share_done"), sem("prob_done")
        p_turned, p_kept = sem("p_turned"), sem("p_kept")
        o_done, o_kept, w_done, x_done = sem("o_done"), sem("o_kept"), sem("w_done"), sem("x_done")
        block = ctx.enter_context(nc.Block())

        @block.sync
        def _(sp):
            for i, n in enumerate(("Wq", "Wk", "Wv", "Wo")):
                sp.dma_start(w_rows[:, i], io["L0_xattn_" + n].rearrange("(k p) d -> p k d", p=P)).then_inc(loaded, 16)
            sp.dma_start(mask8[:, :, :], io["mask_Bx1xSxS2_bk1"].rearrange("b o (t p) j -> p (b o t) j", p=P)).then_inc(masks, 16)

        @block.gpsimd
        def _(pool):
            pool.memset(head_of_row[:, :], 1.0).then_inc(ready, 1)
            pool.memset(head_of_key[:, :], 0.0).then_inc(ready, 1)
            pool.wait_ge(ready, 2)
            pool.affine_select(out=head_of_row[:, :], in_=head_of_row[:, :], compare_op=ALU.is_ge, fill=0.0, base=0,
                               pattern=[[-HD, HH]], channel_multiplier=1).then_inc(ready, 1)
            pool.wait_ge(ready, 3)
            pool.memset(head_of_key[0:SC, 0:HD], 1.0).then_inc(ready, 1)
            pool.wait_ge(ready, 4)
            pool.memset(head_of_key[SC:P, HD:2 * HD], 1.0).then_inc(ready, 1)
            pool.wait_ge(ready, 5)
            pool.affine_select(out=head_of_row[:, :], in_=head_of_row[:, :], compare_op=ALU.is_ge, fill=0.0, base=HD - 1,
                               pattern=[[HD, HH]], channel_multiplier=-1).then_inc(ready, 1)
            pool.wait_ge(ready, 6)
            pool.wait_ge(kt_kept, 1)

            def stage(b):
                after(pool, s_done, b * TB)
                for k in range(KT):
                    pool.tensor_tensor(kblk[:, k], kT[:, k, bass.ds(b * SC, SC)].unsqueeze(1).broadcast_to([P, HH, SC]),
                                       head_of_row[:, :].unsqueeze(2).broadcast_to([P, HH, SC]), ALU.mult).then_inc(kblk_done, 1)
                after(pool, v_done, b)
                pool.tensor_copy(ctx2[:, :, 0], g.ctxT[:, :, bass.ds(b * SC, SC)]).then_inc(ctx2_done, 1)
                pool.tensor_copy(ctx2[:, :, 1], g.ctxT[:, :, bass.ds(b * SC, SC)]).then_inc(ctx2_done, 1)

            def normalise(b, j, t):
                pool.wait_ge(share_done, b * TB + t + 1)
                p3 = prob[j][:, t].rearrange("p (h j) -> p h j", h=HEADS)
                pool.tensor_tensor(p3, p3, share[:, t].unsqueeze(2).broadcast_to([P, HEADS, SC]), ALU.mult).then_inc(prob_done, 1)

            def body(b, j):
                for t in range(TB):
                    if t == 0 and within(b + 2):
                        norm.gpsimd(b + 2)
                    if within(b + 1):
                        normalise(b + 1, 1 - j, t)
                    if t == 2 and within(b + 2):
                        stage(b + 2)

            norm.gpsimd(0)
            stage(0)
            body(-1, 1)
            over_pairs(pool, body)

        @block.tensor
        def _(pe):
            pe.wait_ge(loaded, 64)
            for i in range(4):
                for k in range(KT):
                    for e in range(KT):
                        last = pe.transpose(score[:, i // 2, i % 2, k * D + e * P:k * D + (e + 1) * P],
                                            w_rows[:, i, e, k * P:(k + 1) * P], g.ident[:, :])
                last.then_inc(w_turned, 1)
            pe.wait_ge(w_kept, 4)
            for h in range(KT):
                for k in range(KT):
                    last = pe.matmul(proj[:, h, :], wT[:, 1, k, h * P:(h + 1) * P], g.ctxT[:, k, :], start=k == 0, stop=k == KT - 1)
            last.then_inc(kt_done, 1)
            norm.tensor(0)
            pe.wait_ge(kt_kept, 1)

            def project(b):
                pe.wait_ge(norm.columns_done, b + 1)
                after(pe, x_done, (b - 1) * 2)
                for h in range(KT):
                    for k in range(KT):
                        last = pe.matmul(proj[:, h, :], wT[:, 0, k, h * P:(h + 1) * P], norm.xnT[:, k, :], start=k == 0, stop=k == KT - 1)
                    last.then_inc(q_done, 1)
                pe.wait_ge(ctx2_done, b * 2 + 2)
                pe.wait_ge(q_kept, b * 2 + 1)
                for k in range(KT):
                    last = pe.matmul(proj[:, 0, 0:D], ctx2[:, k].rearrange("p a j -> p (a j)"), wT[:, 2, k, :], start=k == 0, stop=k == KT - 1)
                last.then_inc(v_done, 1)

            def scores(b, t):
                if t == 0:
                    pe.wait_ge(q_kept, b * 2 + 2)
                    pe.wait_ge(kblk_done, b * 2 + 2)
                after(pe, capped, b * TB + t - 1)
                for h in range(KT):
                    last = pe.matmul(score[:, t % 2, h, :], qT[:, h, t * P:(t + 1) * P], kblk[:, h].rearrange("p h j -> p (h j)"),
                                     start=True, stop=True)
                last.then_inc(s_done, 1)

            def turn_probs(b, j, t):
                pe.wait_ge(prob_done, b * TB + t + 1)
                if t > 0:
                    pe.wait_ge(p_kept, b * TB + t)
                elif within(b + 1):
                    pe.wait_ge(norm.columns_done, b + 2)
                for i in range(PAIRS):
                    last = pe.transpose(turn[:, i // 4, (i % 4) * P:(i % 4 + 1) * P], prob[j][:, t, i * P:(i + 1) * P], g.ident[:, :])
                last.then_inc(p_turned, 1)

            def values(b, j):
                pe.wait_ge(p_kept, b * TB + TB)
                pe.wait_ge(v_kept, b + 2 if within(b + 1) else b + 1)
                for i in range(PAIRS):
                    r = 2 * HD * (i % 4)
                    last = pe.matmul(proj[r:r + 2 * HD, i // 4, :], vblk[j][:, i, :], probT[:, i, :], start=True, stop=True)
                last.then_inc(o_done, 1)

            def project_out(b):
                pe.wait_ge(o_kept, b + 1)
                for t in range(TB):
                    for k in range(KT):
                        last = pe.matmul(proj[:, t // 2, (t % 2) * D:(t % 2 + 1) * D], oT[:, k, t * P:(t + 1) * P], wT[:, 3, k, :],
                                         start=k == 0, stop=k == KT - 1)
                    if t % 2:
                        last.then_inc(w_done, 1)

            def body(b, j):
                back = not isinstance(b, int) or b >= 0
                for t in range(TB):
                    if within(b + 1):
                        scores(b + 1, t)
                    if back:
                        turn_probs(b, j, t)
                if within(b + 2):
                    norm.tensor(b + 2, free=[(p_kept, b * TB + TB)] if back else ())
                if back:
                    values(b, j)
                    project_out(b)
                if within(b + 2):
                    project(b + 2)

            project(0)
            body(-1, 1)
            over_pairs(pe, body)

        @block.scalar
        def _(act):
            for i in range(4):
                act.wait_ge(w_turned, i + 1)
                act.activation(wT[:, i].rearrange("p k e -> p (k e)"), score[:, i // 2, i % 2, :], ACT.Copy).then_inc(w_kept, 1)
            act.wait_ge(kt_done, 1)
            act.activation(kT[:, :, :], proj[:, :, :], ACT.Copy).then_inc(kt_kept, 1)
            norm.scalar(0)

            def keep_q(b):
                for h in range(KT):
                    act.wait_ge(q_done, b * 2 + h + 1)
                    after(act, s_done, b * TB)
                    act.activation(qT[:, h, :], proj[:, h, :], ACT.Copy, scale=HD ** -0.5).then_inc(q_kept, 1)

            def exponentials(b, j, t):
                act.wait_ge(less_max, b * TB + t + 1)
                act.activation(prob[j][:, t, :], prob[j][:, t, :], ACT.Exp).then_inc(exp_done, 1)

            def keep_turned(b, t):
                act.wait_ge(p_turned, b * TB + t + 1)
                after(act, o_done, b)
                act.activation(probT[:, :, t * P:(t + 1) * P], turn[:, :, :].rearrange("p a (i q) -> p (a i) q", i=4),
                               ACT.Copy).then_inc(p_kept, 1)

            def body(b, j):
                back = not isinstance(b, int) or b >= 0
                ahead = lambda t: exponentials(b + 1, 1 - j, t) if within(b + 1) else None
                if back:
                    keep_turned(b, 0)
                ahead(0)
                if back:
                    for t in range(1, TB):
                        keep_turned(b, t)
                ahead(1)
                if within(b + 2):
                    norm.scalar(b + 2, free=[(q_done, b * 2 + 4)])
                if back:
                    act.wait_ge(o_done, b + 1)
                    after(act, w_done, b * 2)
                    act.activation(oT[:, :, :], proj[:, :, :], ACT.Copy).then_inc(o_kept, 1)
                ahead(2)
                if within(b + 2):
                    keep_q(b + 2)
                ahead(3)

            keep_q(0)
            body(-1, 1)
            over_pairs(act, body)

        @block.vector
        def _(dve):
            norm.vector_stats(0)
            norm.vector_rows(0)
            dve.wait_ge(masks, 16)
            dve.tensor_scalar(cap[:, :, :], mask8[:, :, :], -BIG, BIG, ALU.mult, ALU.add).then_inc(caps, 1)
            dve.wait_ge(caps, 1)
            dve.scalar_tensor_tensor(out=cap[:, :, :], in0=mask8[:, :, :], scalar=NEG, in1=cap[:, :, :],
                                     op0=ALU.mult, op1=ALU.add).then_inc(caps, 1)
            dve.wait_ge(caps, 2)
            dve.wait_ge(ready, 6)

            def three(j, t):
                return prob[j][:, t].rearrange("p (h j) -> p h j", h=HEADS)

            def masked(b, j, t):
                dve.wait_ge(s_done, b * TB + t + 1)
                after(dve, p_turned, (b - 1) * TB)
                for h in range(KT):
                    step = dve.tensor_tensor(three(j, t)[:, h * HH:(h + 1) * HH], score[:, t % 2, h].rearrange("p (h j) -> p h j", h=HH),
                                             cap[:, bass.ds(b * TB + t, 1), :].broadcast_to([P, HH, SC]), ALU.min)
                step.then_inc(capped, 1)

            def less_maximum(b, j, t):
                dve.wait_ge(capped, b * TB + t + 1)
                dve.tensor_reduce(most[:, t], three(j, t), AX.X, ALU.max).then_inc(max_done, 1)
                dve.wait_ge(max_done, b * TB + t + 1)
                dve.tensor_tensor(three(j, t), three(j, t), most[:, t].unsqueeze(2).broadcast_to([P, HEADS, SC]),
                                  ALU.subtract).then_inc(less_max, 1)

            def shares(b, j, t):
                dve.wait_ge(exp_done, b * TB + t + 1)
                dve.tensor_reduce(total[:, t], three(j, t), AX.X, ALU.add).then_inc(sum_done, 1)
                dve.wait_ge(sum_done, b * TB + t + 1)
                after(dve, prob_done, (b - 1) * TB + t + 1)
                dve.reciprocal(share[:, t], total[:, t]).then_inc(share_done, 1)

            def keep_values(b, j):
                dve.wait_ge(v_done, b + 1)
                after(dve, o_done, b - 1)
                dve.tensor_tensor(vblk[j][:, :, :], proj[:, 0, 0:D].rearrange("p (i c) -> p i c", i=PAIRS),
                                  head_of_key[:, :].unsqueeze(1).broadcast_to([P, PAIRS, 2 * HD]), ALU.mult).then_inc(v_kept, 1)

            def add_to_x(b):
                for i in range(2):
                    dve.wait_ge(w_done, b * 2 + i + 1)
                    xt = g.x[:, bass.ds(b * TB + 2 * i, 2), :]
                    dve.tensor_tensor(xt, proj[:, i, :].rearrange("p (t d) -> p t d", t=2), xt, ALU.add).then_inc(x_done, 1)

            def body(b, j):
                back = not isinstance(b, int) or b >= 0
                for t in range(TB + 2):
                    if within(b + 1):
                        if t < TB:
                            masked(b + 1, 1 - j, t)
                        if 1 <= t <= TB:
                            less_maximum(b + 1, 1 - j, t - 1)
                        if t >= 2:
                            shares(b + 1, 1 - j, t - 2)
                    if t == 0 and within(b + 2):
                        norm.vector_stats(b + 2)
                    if t == 1 and within(b + 2):
                        norm.vector_rows(b + 2)
                    if t == TB and back:
                        add_to_x(b)
                if within(b + 2):
                    keep_values(b + 2, j)

            keep_values(0, 0)
            body(-1, 1)
            over_pairs(dve, body)


E = 8
SLOT_TILES = 72
UNROLL = 4
EXPERT_WORDS = SLOT_TILES // UNROLL + 1
FIELDS = UNROLL + 2


def route(nc, io, g, tag, gate_by_rows, gate_name, bias_name, tiny, scatter_rows, load_beside=None):
    with ExitStack() as ctx:
        sb = lambda name, shape, dt=F32: ctx.enter_context(nc.sbuf_tensor(f"{tag}_{name}", shape, dt))
        sem = lambda name: g.stage_semaphore(f"{tag}_{name}")
        turn = ctx.enter_context(nc.psum_tensor(f"{tag}_turn", [P, 2, BANK], F32))
        logit = ctx.enter_context(nc.psum_tensor(f"{tag}_logit", [P, 2, BANK], F32))
        count = ctx.enter_context(nc.psum_tensor(f"{tag}_count", [P, 2, NT, E], F32))
        norm = Norm(nc, ctx, g, tag, turn, depth=2)
        gate = sb("gate", [P, KT, E])
        gate_rows = sb("gate_rows", [E, D])
        gate_bias = sb("gate_bias", [P, E])
        mean_all, rstd_all = g.mean_all, g.rstd_all
        L, EX, PR = (sb(n, [P, NT, E]) for n in ("L", "EX", "PR"))
        CAND, REST, POS, BOTH = (sb(n, [P, NT, E]) for n in ("CAND", "REST", "POS", "BOTH"))
        CHOICE = sb("CHOICE", [P, 2, NT, E])
        R1, R2 = sb("R1", [P, NT]), sb("R2", [P, NT])
        TOP = sb("TOP", [P, 2, NT])
        POSF = sb("POSF", [P, NT, 2])
        rank = sb("rank", [P, E])
        rank_i = sb("rank_i", [P, E], I32)
        before = sb("before", [P, P])
        upto = sb("upto", [P, NT, E])
        tiles, tiles_i, tiles_end, tiles_start = sb("tiles", [P, E]), sb("tiles_i", [P, E], I32), sb("tiles_end", [P, E]), sb("tiles_start", [P, E])
        tile_no_i, tile_no = sb("tile_no_i", [1, SLOT_TILES], I32), sb("tile_no", [1, SLOT_TILES])
        past, expert_f = sb("past", [1, SLOT_TILES, E]), sb("expert_f", [1, UNROLL * EXPERT_WORDS + 2])
        word = sb("word", [1, EXPERT_WORDS])
        if scatter_rows:
            rows = [sb(f"rows{j}", [P, TB, D]) for j in range(2)]
            stat4 = [sb(f"stat4_{j}", [P, 2, TB]) for j in range(2)]
            slot4 = [sb(f"slot4_{j}", [P, TB, 2], I32) for j in range(2)]

        loaded, ready, gate_turned, gate_kept = sem("loaded"), sem("ready"), sem("gate_turned"), sem("gate_kept")
        l_done, l_kept, stats_kept = sem("l_done"), sem("l_kept"), sem("stats_kept")
        chain, shifted, exp_done, chosen, counted = sem("chain"), sem("shifted"), sem("exp_done"), sem("chosen"), sem("counted")
        placed, staged, rows_ready = sem("placed"), sem("staged"), sem("rows_ready")
        sorted_ = [[sem(f"sorted{j}_{t}") for t in range(TB)] for j in range(2)]
        block = ctx.enter_context(nc.Block())

        @block.sync
        def _(sp):
            if gate_by_rows:
                sp.dma_start(gate_rows[:, :], io[gate_name]).then_inc(loaded, 16)
            else:
                sp.dma_start(gate[:, :, :], io[gate_name].rearrange("(k p) e -> p k e", p=P)).then_inc(loaded, 16)
            if bias_name:
                sp.wait_ge(ready, 1)
                sp.dma_start(gate_bias[:, :], io[bias_name].partition_broadcast(P)).then_inc(loaded, 16)
            if load_beside:
                load_beside(sp)

        LOADS = 32 if bias_name else 16

        @block.gpsimd
        def _(pool):
            pool.memset(gate_bias[:, :], 0.0).then_inc(ready, 1)
            pool.memset(before[:, :], 1.0).then_inc(ready, 1)
            pool.iota(rank_i[:, :], [[-1, E]], base=E, channel_multiplier=0).then_inc(ready, 1)
            pool.iota(tile_no_i[:, :], [[1, SLOT_TILES]], base=0, channel_multiplier=0).then_inc(ready, 1)
            pool.wait_ge(ready, 4)
            pool.affine_select(out=before[:, :], in_=before[:, :], compare_op=ALU.is_gt, fill=0.0, base=0,
                               pattern=[[1, P]], channel_multiplier=-1).then_inc(ready, 1)

            def keep_stats(b, nxt):
                norm.gpsimd(b)
                pool.wait_ge(norm.rstd_done, b + 1)
                pool.tensor_copy(mean_all[:, bass.ds(b * TB, TB)], norm.mean[:, :]).then_inc(stats_kept, 1)
                pool.tensor_copy(rstd_all[:, bass.ds(b * TB, TB)], norm.rstd[:, :]).then_inc(stats_kept, 1)
            over_sequences(pool, keep_stats)

            def scatter(b, j):
                for t in range(TB):
                    wait_apart(pool, rows_ready, b * TB + t + 1, (g.zeroed, 16))
                    for c in range(2):
                        pool.indirect_dma_start(g.slots_x, bass.IndirectOffsetOnAxis(ap=slot4[j][:, t, c:c + 1], axis=0),
                                                rows[j][:, t, :], None).then_inc(sorted_[j][t], 16)
            if scatter_rows:
                pool.wait_ge(g.zeroed, 16)
                over_pairs(pool, scatter)
                for j in range(2):
                    for t in range(TB):
                        pool.wait_ge(sorted_[j][t], 16 * B)

        @block.tensor
        def _(pe):
            pe.wait_ge(loaded, LOADS)
            pe.wait_ge(ready, 5)
            if gate_by_rows:
                for k in range(KT):
                    last = pe.transpose(logit[:, 0, k * E:(k + 1) * E], gate_rows[:, k * P:(k + 1) * P], g.ident[0:E, 0:E])
                last.then_inc(gate_turned, 1)
                pe.wait_ge(gate_kept, 1)
            norm.tensor(0)

            def body(b, j):
                if within(b + 1):
                    norm.tensor(b + 1, buf=1 - j)
                pe.wait_ge(norm.columns_done, b + 1)
                after(pe, l_kept, b)
                for t in range(TB):
                    for k in range(KT):
                        last = pe.matmul(logit[:, 0, t * E:(t + 1) * E], norm.columns[j][:, k, t * P:(t + 1) * P], gate[:, k, :],
                                         start=k == 0, stop=k == KT - 1)
                last.then_inc(l_done, 1)
            over_pairs(pe, body)
            pe.wait_ge(chosen, 1)
            pe.matmul(count[:, 0].rearrange("p t e -> p (t e)"), before[:, :], BOTH[:, :, :].rearrange("p t e -> p (t e)"), start=True, stop=True)
            pe.matmul(count[:, 1].rearrange("p t e -> p (t e)"), g.ones[:, :], BOTH[:, :, :].rearrange("p t e -> p (t e)"),
                      start=True, stop=True).then_inc(counted, 1)

        @block.scalar
        def _(act):
            if gate_by_rows:
                act.wait_ge(gate_turned, 1)
                act.activation(gate[:, :, :], logit[:, 0, 0:KT * E].rearrange("p (k e) -> p k e", k=KT), ACT.Copy).then_inc(gate_kept, 1)
            norm.scalar(0)

            def body(b, j):
                if within(b + 1):
                    norm.scalar(b + 1, free=[(l_done, b)], buf=1 - j)
            over_pairs(act, body)
            act.wait_ge(shifted, 1)
            act.activation(EX[:, :, :], L[:, :, :], ACT.Exp).then_inc(exp_done, 1)

        @block.vector
        def _(dve):
            def make(b, j):
                after(dve, stats_kept, b * 2)
                norm.vector_stats(b)
                norm.vector_rows(b, buf=j)

            make(0, 0)
            make(1, 1)

            def body(b, j):
                if within(b + 2):
                    make(b + 2, j)
                dve.wait_ge(l_done, b + 1)
                dve.tensor_tensor(L[:, bass.ds(b * TB, TB), :], logit[:, 0, 0:TB * E].rearrange("p (t e) -> p t e", t=TB),
                                  gate_bias[:, :].unsqueeze(1).broadcast_to([P, TB, E]), ALU.add).then_inc(l_kept, 1)
            dve.wait_ge(loaded, LOADS)
            dve.wait_ge(ready, 5)
            over_pairs(dve, body)

            steps = [0]

            def link(ins):
                steps[0] += 1
                ins.then_inc(chain, 1)
                dve.wait_ge(chain, steps[0])

            def bc(a):
                return a.unsqueeze(2).broadcast_to([P, NT, E])

            def bt(a):
                return a.unsqueeze(1).broadcast_to([P, NT, E])

            dve.wait_ge(l_kept, B)
            link(dve.tensor_reduce(R1[:, :], L[:, :, :], AX.X, ALU.max))
            dve.tensor_tensor(L[:, :, :], L[:, :, :], bc(R1[:, :]), ALU.subtract).then_inc(shifted, 1)
            link(dve.tensor_copy(rank[:, :], rank_i[:, :]))
            link(dve.tensor_copy(tile_no[:, :], tile_no_i[:, :]))
            dve.wait_ge(exp_done, 1)
            link(dve.tensor_reduce(R1[:, :], EX[:, :, :], AX.X, ALU.add))
            link(dve.reciprocal(R2[:, :], R1[:, :]))
            link(dve.tensor_tensor(PR[:, :, :], EX[:, :, :], bc(R2[:, :]), ALU.mult))
            for c in range(2):
                left = PR if c == 0 else REST
                link(dve.tensor_reduce(TOP[:, c], left[:, :, :], AX.X, ALU.max))
                link(dve.tensor_tensor(CAND[:, :, :], left[:, :, :], bc(TOP[:, c]), ALU.is_ge))
                link(dve.tensor_tensor(CAND[:, :, :], CAND[:, :, :], bt(rank[:, :]), ALU.mult))
                link(dve.tensor_reduce(R1[:, :], CAND[:, :, :], AX.X, ALU.max))
                link(dve.tensor_tensor(CHOICE[:, c], CAND[:, :, :], bc(R1[:, :]), ALU.is_equal))
                if c == 0:
                    link(dve.scalar_tensor_tensor(out=REST[:, :, :], in0=CHOICE[:, 0], scalar=-2.0, in1=PR[:, :, :],
                                                  op0=ALU.mult, op1=ALU.add))
            dve.tensor_tensor(BOTH[:, :, :], CHOICE[:, 0], CHOICE[:, 1], ALU.add).then_inc(chosen, 1)
            link(dve.tensor_tensor(R1[:, :], TOP[:, 0], TOP[:, 1], ALU.add))
            link(dve.tensor_scalar(R1[:, :], R1[:, :], tiny, None, ALU.add))
            link(dve.reciprocal(R2[:, :], R1[:, :]))
            for c in range(2):
                link(dve.tensor_tensor(g.share[:, :, c], TOP[:, c], R2[:, :], ALU.mult))
            dve.wait_ge(counted, 1)
            for e in range(E):
                link(dve.tensor_tensor_scan(upto[:, :, e], g.ones[:, 0:NT], count[:, 1, :, e], 0.0, ALU.mult, ALU.add))
            link(dve.tensor_scalar(tiles[:, :], upto[:, NT - 1, :], float(P - 1), None, ALU.add))
            link(dve.tensor_copy(tiles_i[:, :], tiles[:, :]))
            link(dve.tensor_scalar(tiles_i[:, :], tiles_i[:, :], P.bit_length() - 1, None, ALU.logical_shift_right))
            link(dve.tensor_copy(tiles[:, :], tiles_i[:, :]))
            link(dve.tensor_tensor_scan(tiles_end[:, :], g.ones[:, 0:E], tiles[:, :], 0.0, ALU.mult, ALU.add))
            link(dve.tensor_tensor(tiles_start[:, :], tiles_end[:, :], tiles[:, :], ALU.subtract))
            link(dve.tensor_tensor(POS[:, :, :], upto[:, :, :], count[:, 1], ALU.subtract))
            link(dve.tensor_tensor(POS[:, :, :], POS[:, :, :], count[:, 0], ALU.add))
            link(dve.scalar_tensor_tensor(out=POS[:, :, :], in0=bt(tiles_start[:, :]), scalar=float(P), in1=POS[:, :, :],
                                          op0=ALU.mult, op1=ALU.add))
            for c in range(2):
                link(dve.tensor_tensor(CAND[:, :, :], CHOICE[:, c], POS[:, :, :], ALU.mult))
                link(dve.tensor_reduce(POSF[:, :, c], CAND[:, :, :], AX.X, ALU.add))
            link(dve.tensor_copy(g.slot[:, :, :], POSF[:, :, :]))
            link(dve.tensor_tensor(past[:, :, :], tile_no[:, :].unsqueeze(2).broadcast_to([1, SLOT_TILES, E]),
                                   tiles_end[0:1, :].unsqueeze(1).broadcast_to([1, SLOT_TILES, E]), ALU.is_ge))
            link(dve.memset(expert_f[:, :], 0.0))
            link(dve.tensor_reduce(expert_f[:, 2:2 + SLOT_TILES], past[:, :, :], AX.X, ALU.add))
            link(dve.tensor_scalar(expert_f[:, :], expert_f[:, :], float(E - 1), None, ALU.min))
            field = lambda n: expert_f[:, n:n + UNROLL * (EXPERT_WORDS - 1) + 1:UNROLL]
            link(dve.tensor_copy(word[:, :], field(FIELDS - 1)))
            for n in reversed(range(FIELDS - 1)):
                link(dve.scalar_tensor_tensor(out=word[:, :], in0=word[:, :], scalar=float(E), in1=field(n), op0=ALU.mult, op1=ALU.add))
            link(dve.tensor_copy(g.experts[:, :], word[:, :]))

            def rows_of(b, j):
                for t in range(TB):
                    after(dve, sorted_[j][t], (b - j) * 16)
                dve.tensor_copy(stat4[j][:, 0], mean_all[:, bass.ds(b * TB, TB)]).then_inc(staged, 1)
                dve.tensor_copy(stat4[j][:, 1], rstd_all[:, bass.ds(b * TB, TB)]).then_inc(staged, 1)
                dve.tensor_copy(slot4[j][:, :, :], g.slot[:, bass.ds(b * TB, TB), :]).then_inc(staged, 1)
                dve.wait_ge(staged, b * 3 + 3)
                for t in range(TB):
                    dve.tensor_scalar(rows[j][:, t, :], g.x[:, b * TB + t, :], stat4[j][:, 0, t:t + 1], stat4[j][:, 1, t:t + 1],
                                      ALU.subtract, ALU.mult).then_inc(rows_ready, 1)
            dve.wait_ge(stats_kept, 2 * B)
            if scatter_rows:
                over_pairs(dve, rows_of)


def combine(nc, g, tag, out=None, beside={}):
    with ExitStack() as ctx:
        sb = lambda name, shape, dt=F32: ctx.enter_context(nc.sbuf_tensor(f"{tag}_{name}", shape, dt))
        sem = lambda name: g.stage_semaphore(f"{tag}_{name}")
        slot4 = [sb(f"slot4_{j}", [P, TB, 2], I32) for j in range(2)]
        share4 = [sb(f"share4_{j}", [P, TB, 2]) for j in range(2)]
        rows = [sb(f"rows{j}", [P, TB, 2, D]) for j in range(2)]
        staged, used, half, stored = sem("staged"), sem("used"), sem("half"), sem("stored")
        fetched = [[sem(f"fetched{j}_{t}") for t in range(TB)] for j in range(2)]
        block = ctx.enter_context(nc.Block())

        @block.gpsimd
        def _(pool):
            if "gpsimd" in beside:
                beside["gpsimd"](pool)
            def body(b, j):
                for t in range(TB):
                    after(pool, fetched[j][t], (b - j) * 16)
                after(pool, used, (b - 1) * TB)
                pool.tensor_copy(slot4[j][:, :, :], g.slot[:, bass.ds(b * TB, TB), :]).then_inc(staged, 1)
                pool.tensor_copy(share4[j][:, :, :], g.share[:, bass.ds(b * TB, TB), :]).then_inc(staged, 1)
                wait_apart(pool, staged, b * 2 + 2, (staged, 2))
                for t in range(TB):
                    for c in range(2):
                        pool.indirect_dma_start(rows[j][:, t, c, :], None, g.slots_y,
                                                bass.IndirectOffsetOnAxis(ap=slot4[j][:, t, c:c + 1], axis=0)).then_inc(fetched[j][t], 16)
            over_pairs(pool, body)

        @block.scalar
        def _(act):
            if "scalar" in beside:
                beside["scalar"](act)

        @block.sync
        def _(sp):
            if "sync" in beside:
                beside["sync"](sp)
            def body(b, nxt):
                sp.wait_ge(used, b * TB + TB)
                sp.dma_start(out[b].rearrange("(t p) d -> p t d", p=P), g.x[:, bass.ds(b * TB, TB), :]).then_inc(stored, 16)
            if out is not None:
                over_sequences(sp, body)
                sp.wait_ge(stored, 16 * B)

        @block.vector
        def _(dve):
            if "vector" in beside:
                beside["vector"](dve)
            def body(b, j):
                dve.wait_ge(staged, b * 2 + 2)
                for c in range(2):
                    for t in range(TB):
                        if c == 0:
                            dve.wait_ge(fetched[j][t], (b - j) * 16 + 32)
                        else:
                            dve.wait_ge(half, b * TB + t + 1)
                        xt = g.x[:, b * TB + t, :]
                        dve.scalar_tensor_tensor(out=xt, in0=rows[j][:, t, c, :], scalar=share4[j][:, t, c:c + 1], in1=xt,
                                                 op0=ALU.mult, op1=ALU.add).then_inc((half, used)[c], 1)
            over_pairs(dve, body)


def over_tiles(eng, n, steps, own=0):
    def group(u, places=UNROLL):
        for j in range(places):
            steps(u * UNROLL + j, j, u, None)

    for first, last, kind in ((0, own, "own"), (own, n, "sorted")):
        if first < last:
            group(first // UNROLL)
            with eng.Fori(first // UNROLL + 1, last // UNROLL - 1) as u:
                for j in range(UNROLL):
                    steps(u * UNROLL + j, j, u, kind)
            group(last // UNROLL - 1)
    group(n // UNROLL, 2)


def load_experts(eng, g, u):
    word = g.experts[0:1, u:u + 1] if isinstance(u, int) else g.experts[0:1, bass.ds(u, 1)]
    value = eng.value_load(word, min_val=0, max_val=E ** FIELDS - 1)
    return [(value // E ** k) % E for k in range(FIELDS)]


def l0_experts(nc, io, g, w1, w2, loaded):
    F = 2 * D
    C = F // P
    N = SLOT_TILES
    with ExitStack() as ctx:
        sb = lambda name, shape, dt=F32: ctx.enter_context(nc.sbuf_tensor("e0_" + name, shape, dt))
        sem = lambda name: g.stage_semaphore("e0_" + name)
        ps = lambda name, shape: ctx.enter_context(nc.psum_tensor("e0_" + name, shape, F32))
        xt_ps, h_ps, ht_ps, y_ps = ps("xt_ps", [P, BANK]), ps("h_ps", [P, 2, BANK]), ps("ht_ps", [P, 2, BANK]), ps("y_ps", [P, 2, BANK])
        b1, b2 = sb("b1", [64, E, F], F32R), sb("b2", [64, E, D], F32R)
        b1_row, b2_row, ones_r = sb("b1_row", [1, E, F]), sb("b2_row", [1, E, D]), sb("ones_r", [64, P], F32R)
        xin, xT = sb("xin", [P, 2, D]), sb("xT", [P, 2, D])
        h, hT, y = sb("h", [P, 2, F]), sb("hT", [P, 2, F]), sb("y", [P, 2, D])

        b_loaded, b_ready, x_in = sem("b_loaded"), sem("b_ready"), [sem(f"x_in{j}") for j in range(2)]
        x_turned, x_kept, h_done, h_kept, h_turned, ht_kept = (sem(n) for n in ("x_turned", "x_kept", "h_done", "h_kept", "h_turned", "ht_kept"))
        y_done, y_kept, y_out = sem("y_done"), sem("y_kept"), [sem(f"y_out{j}") for j in range(2)]
        block = ctx.enter_context(nc.Block())
        rows_x = g.slots_x.rearrange("(i p) d -> i p d", p=P)
        rows_y = g.slots_y.rearrange("(i p) d -> i p d", p=P)

        @block.sync
        def _(sp):
            sp.dma_start(b1_row[:, :, :], io["L0_ffn_b1"].rearrange("(o e) f -> o e f", o=1)).then_inc(b_loaded, 16)
            sp.dma_start(b2_row[:, :, :], io["L0_ffn_b2"].rearrange("(o e) d -> o e d", o=1)).then_inc(b_loaded, 16)

            def fetch(i, j):
                after(sp, x_turned, i - 1)
                sp.dma_start(xin[:, j, :], rows_x[i]).then_inc(x_in[j], 16)

            fetch(0, 0)
            fetch(1, 1)

            def steps(i, place, u, kind):
                j = place % 2
                if kind or i + 2 < N:
                    fetch(i + 2, j)
                if kind or 2 <= i:
                    sp.wait_ge(y_kept, i - 1)
                    sp.dma_start(rows_y[i - 2], y[:, j, :]).then_inc(y_out[j], 16)
            over_tiles(sp, N, steps)
            for j in range(2):
                sp.wait_ge(y_out[j], 16 * N // 2)

        @block.tensor
        def _(pe):
            def turn_x(i, j):
                pe.wait_ge(x_in[j], (i - j) * 8 + 16)
                after(pe, x_kept, i)
                for k in range(KT):
                    last = pe.transpose(xt_ps[:, k * P:(k + 1) * P], xin[:, j, k * P:(k + 1) * P], g.ident[:, :])
                last.then_inc(x_turned, 1)

            turn_x(0, 0)
            pe.wait_ge(loaded, 16 * 2 * E)
            pe.wait_ge(b_ready, 7)

            experts = []

            def steps(i, place, u, kind):
                j = place % 2
                if place == 0:
                    experts[:] = load_experts(pe, g, u)
                if kind or i < N:
                    e = experts[place + 2]
                    pe.wait_ge(x_kept, i + 1)
                    after(pe, h_kept, i - 1)
                    for k in range(KT):
                        pe.matmul(h_ps[:, j, :], xT[:, j, k * P:(k + 1) * P], w1[:, e, k, :], start=k == 0, stop=False)
                    last = pe.matmul(h_ps[:, j, :], ones_r[:, :], b1[:, e, :], start=False, stop=True)
                    last.then_inc(h_done, 1)
                if kind or 1 <= i <= N:
                    pe.wait_ge(h_kept, i)
                    after(pe, ht_kept, i - 2)
                    for c in range(C):
                        last = pe.transpose(ht_ps[:, 1 - j, c * P:(c + 1) * P], h[:, 1 - j, c * P:(c + 1) * P], g.ident[:, :])
                    last.then_inc(h_turned, 1)
                if kind or i + 1 < N:
                    turn_x(i + 1, 1 - j)
                if kind or 2 <= i:
                    e = experts[place]
                    pe.wait_ge(ht_kept, i - 1)
                    after(pe, y_kept, i - 3)
                    for c in range(C):
                        pe.matmul(y_ps[:, j, 0:D], hT[:, j, c * P:(c + 1) * P], w2[:, e, c, :], start=c == 0, stop=False)
                    last = pe.matmul(y_ps[:, j, 0:D], ones_r[:, :], b2[:, e, :], start=False, stop=True)
                    last.then_inc(y_done, 1)
            over_tiles(pe, N, steps)

        @block.scalar
        def _(act):
            def steps(i, place, u, kind):
                j = place % 2
                if kind or 1 <= i <= N:
                    act.wait_ge(h_turned, i)
                    after(act, y_done, i - 2)
                    act.activation(hT[:, 1 - j, :], ht_ps[:, 1 - j, :], ACT.Relu).then_inc(ht_kept, 1)
            over_tiles(act, N, steps)

        @block.vector
        def _(dve):
            def keep_x(i, j):
                dve.wait_ge(x_turned, i + 1)
                after(dve, h_done, i - 1)
                dve.tensor_copy(xT[:, j, :], xt_ps[:, 0:D]).then_inc(x_kept, 1)

            dve.memset(b1[:, :, :].bitcast(F32), 0.0).then_inc(b_ready, 1)
            dve.memset(b2[:, :, :].bitcast(F32), 0.0).then_inc(b_ready, 1)
            dve.memset(ones_r[:, :].bitcast(F32), 1.0).then_inc(b_ready, 1)
            dve.wait_ge(b_loaded, 32)
            dve.wait_ge(b_ready, 3)
            dve.tensor_copy(b1[0:1], b1_row[:, :, :]).then_inc(b_ready, 1)
            dve.tensor_copy(b2[0:1], b2_row[:, :, :]).then_inc(b_ready, 1)
            dve.wait_ge(b_ready, 5)
            dve.tensor_tensor(b1[32:33], b1_row[:, :, :], b1[0:1].bitcast(F32), ALU.subtract).then_inc(b_ready, 1)
            dve.tensor_tensor(b2[32:33], b2_row[:, :, :], b2[0:1].bitcast(F32), ALU.subtract).then_inc(b_ready, 1)
            keep_x(0, 0)

            def steps(i, place, u, kind):
                j = place % 2
                if kind or i < N:
                    dve.wait_ge(h_done, i + 1)
                    after(dve, h_turned, i - 1)
                    dve.tensor_copy(h[:, j, :], h_ps[:, j, :]).then_inc(h_kept, 1)
                if kind or i + 1 < N:
                    keep_x(i + 1, 1 - j)
                if kind or 2 <= i:
                    dve.wait_ge(y_done, i - 1)
                    if kind or i >= 4:
                        dve.wait_ge(y_out[j], (i - j) * 8 - 16)
                    dve.tensor_copy(y[:, j, :], y_ps[:, j, 0:D]).then_inc(y_kept, 1)
            over_tiles(dve, N, steps)


def l0_ffn(nc, io, g):
    F = io["L0_ffn_w1"].shape[2]
    with nc.sbuf_tensor("e0_w1", [P, E, KT, F], F32) as w1, nc.sbuf_tensor("e0_w2", [P, E, F // P, D], F32) as w2:
        loaded = g.stage_semaphore("e0_loaded")

        def load(sp):
            for e in range(E):
                sp.dma_start(w1[:, e], io["L0_ffn_w1"][e].rearrange("(k p) f -> p k f", p=P)).then_inc(loaded, 16)
                sp.dma_start(w2[:, e], io["L0_ffn_w2"][e].rearrange("(c p) d -> p c d", p=P)).then_inc(loaded, 16)

        route(nc, io, g, "r0", False, "L0_ffn_router_w", "L0_ffn_router_b", 0.0, True, load)
        l0_experts(nc, io, g, w1, w2, loaded)


def l1_experts(nc, io, g):
    F = io["L1_ffn_sg"].shape[1]
    H = F // 2
    C = -(-F // P)
    OWN = NT
    N = OWN + SLOT_TILES
    NE = E + 1
    with ExitStack() as ctx:
        sb = lambda name, shape, dt=F32: ctx.enter_context(nc.sbuf_tensor("e1_" + name, shape, dt))
        sem = lambda name: g.stage_semaphore("e1_" + name)
        ps = lambda name, shape: ctx.enter_context(nc.psum_tensor("e1_" + name, shape, F32))
        up_ps, ht_ps, xt_ps, y_ps = ps("up_ps", [P, 4, BANK]), ps("ht_ps", [P, 2, BANK]), ps("xt_ps", [P, BANK]), ps("y_ps", [P, BANK])
        wgu, wd = sb("wgu", [P, NE, KT, 2, F]), sb("wd", [P, NE, C, D])
        rows = sb("rows", [P, UNROLL, D])
        stat4, slot4 = sb("stat4", [P, 2, UNROLL]), sb("slot4", [P, UNROLL, 2], I32)
        xin, xT = sb("xin", [P, 2, D]), sb("xT", [P, 2, D])
        act_g, h = sb("act_g", [P, H]), sb("h", [P, C * P])
        hT, y = sb("hT", [P, 2, C * P]), sb("y", [P, 2, D])

        ready, own_loaded, loaded, x_in = sem("ready"), sem("own_loaded"), sem("loaded"), [sem(f"x_in{j}") for j in range(2)]
        staged, rows_ready, placed = sem("staged"), sem("rows_ready"), [sem(f"placed{j}") for j in range(UNROLL)]
        x_turned, x_kept, up_done, gated, h_kept, h_turned, ht_kept = (
            sem(n) for n in ("x_turned", "x_kept", "up_done", "gated", "h_kept", "h_turned", "ht_kept"))
        y_done, y_kept, y_out = sem("y_done"), sem("y_kept"), [sem(f"y_out{j}") for j in range(2)]
        block = ctx.enter_context(nc.Block())
        rows_x = g.slots_x.rearrange("(i p) d -> i p d", p=P)
        rows_y = g.slots_y.rearrange("(i p) d -> i p d", p=P)

        def is_own(i, kind):
            return kind == "own" if kind else i < OWN

        @block.sync
        def _(sp):
            def load(e, wg, wu, w, done):
                sp.dma_start(wgu[:, e, :, 0, :], wg.rearrange("(k p) f -> p k f", p=P)).then_inc(done, 16)
                sp.dma_start(wgu[:, e, :, 1, :], wu.rearrange("(k p) f -> p k f", p=P)).then_inc(done, 16)
                sp.dma_start(wd[:, e, 0:C - 1, :], w[0:(C - 1) * P, :].rearrange("(c p) d -> p c d", p=P)).then_inc(done, 16)
                sp.dma_start(wd[0:F - (C - 1) * P, e, C - 1, :], w[(C - 1) * P:, :]).then_inc(done, 16)

            sp.wait_ge(ready, 2)
            load(E, io["L1_ffn_sg"], io["L1_ffn_su"], io["L1_ffn_sd"], own_loaded)
            sp.wait_ge(own_loaded, 16 * 4)
            for e in range(E):
                load(e, io["L1_ffn_wg"][e], io["L1_ffn_wu"][e], io["L1_ffn_wd"][e], loaded)

            def fetch(i, j):
                after(sp, x_turned, i - 1 + OWN)
                sp.dma_start(xin[:, j, :], rows_x[i]).then_inc(x_in[j], 16)

            for j in range(UNROLL):
                sp.wait_ge(placed[j], 32 * OWN // UNROLL)
            fetch(0, 0)
            fetch(1, 1)

            def steps(i, place, u, kind):
                j = place % 2
                if kind or i + 2 < SLOT_TILES:
                    fetch(i + 2, j)
                if kind or 2 <= i:
                    sp.wait_ge(y_kept, i - 1 + OWN)
                    sp.dma_start(rows_y[i - 2], y[:, j, :]).then_inc(y_out[j], 16)
            over_tiles(sp, SLOT_TILES, steps)
            for j in range(2):
                sp.wait_ge(y_out[j], 16 * SLOT_TILES // 2)

        @block.gpsimd
        def _(pool):
            pool.memset(wd[:, :, C - 1, :], 0.0).then_inc(ready, 1)
            pool.memset(h[:, F:], 0.0).then_inc(ready, 1)
            pool.wait_ge(g.zeroed, 16)

            def scatter(b, nxt):
                for t in range(UNROLL):
                    wait_apart(pool, rows_ready, b * UNROLL + t + 1, (g.zeroed, 16))
                    for c in range(2):
                        pool.indirect_dma_start(g.slots_x, bass.IndirectOffsetOnAxis(ap=slot4[:, t, c:c + 1], axis=0),
                                                rows[:, t, :], None).then_inc(placed[t], 16)
            over_sequences(pool, scatter)

        @block.tensor
        def _(pe):
            experts = []

            def turn_x(i, j, place, own):
                if own:
                    pe.wait_ge(rows_ready, i + 1)
                    source = rows[:, place]
                else:
                    pe.wait_ge(x_in[j], (i - OWN - j) * 8 + 16)
                    source = xin[:, j]
                after(pe, x_kept, i)
                for k in range(KT):
                    last = pe.transpose(xt_ps[:, k * P:(k + 1) * P], source[:, k * P:(k + 1) * P], g.ident[:, :])
                last.then_inc(x_turned, 1)

            turn_x(0, 0, 0, True)
            pe.wait_ge(own_loaded, 16 * 4)

            def steps(i, place, u, kind):
                j = place % 2
                if place == 0 and not is_own(i, kind):
                    experts[:] = load_experts(pe, g, u - OWN // UNROLL)
                if kind is None and i == OWN:
                    pe.wait_ge(loaded, 16 * 4 * E)
                if kind or i < N:
                    e = E if is_own(i, kind) else experts[place + 2]
                    pe.wait_ge(x_kept, i + 1)
                    for half in range(2):
                        after(pe, h_kept, 2 * i - 1 + half)
                        for u_ in range(2):
                            for k in range(KT):
                                last = pe.matmul(up_ps[:, 2 * half + u_, 0:H], xT[:, j, k * P:(k + 1) * P],
                                                 wgu[:, e, k, u_, half * H:(half + 1) * H], start=k == 0, stop=k == KT - 1)
                            last.then_inc(up_done, 1)
                if kind or 1 <= i <= N:
                    pe.wait_ge(h_kept, 2 * i)
                    after(pe, ht_kept, i - 1)
                    for c in range(C):
                        last = pe.transpose(ht_ps[:, c // 4, (c % 4) * P:(c % 4 + 1) * P], h[:, c * P:(c + 1) * P], g.ident[:, :])
                    last.then_inc(h_turned, 1)
                if kind or i + 1 < N:
                    turn_x(i + 1, 1 - j, (place + 1) % UNROLL, is_own(i + 1, kind))
                if kind or 2 <= i:
                    e = E if is_own(i - 2, kind) else experts[place]
                    pe.wait_ge(ht_kept, i - 1)
                    after(pe, y_kept, i - 2)
                    for c in range(C):
                        last = pe.matmul(y_ps[:, 0:D], hT[:, j, c * P:(c + 1) * P], wd[:, e, c, :], start=c == 0, stop=c == C - 1)
                    last.then_inc(y_done, 1)
            over_tiles(pe, N, steps, OWN)

        @block.scalar
        def _(act):
            def steps(i, place, u, kind):
                j = place % 2
                if kind or i < N:
                    for half in range(2):
                        act.wait_ge(up_done, 4 * i + 2 * half + 1)
                        after(act, h_kept, 2 * i + half)
                        act.activation(act_g[:, :], up_ps[:, 2 * half, 0:H], ACT.Silu).then_inc(gated, 1)
                if kind or 1 <= i <= N:
                    act.wait_ge(h_turned, i)
                    after(act, y_done, i - 2)
                    act.activation(hT[:, 1 - j, 0:4 * P], ht_ps[:, 0, :], ACT.Copy)
                    act.activation(hT[:, 1 - j, 4 * P:], ht_ps[:, 1, 0:(C - 4) * P], ACT.Copy).then_inc(ht_kept, 1)
            over_tiles(act, N, steps, OWN)

        @block.vector
        def _(dve):
            def keep_x(i, j):
                dve.wait_ge(x_turned, i + 1)
                after(dve, up_done, 4 * (i - 1))
                dve.tensor_copy(xT[:, j, :], xt_ps[:, 0:D]).then_inc(x_kept, 1)

            def make_rows(i, place, u):
                after(dve, placed[place], 32 * u)
                if place == 0:
                    for t in range(1, UNROLL):
                        after(dve, placed[t], 32 * u)
                    group = bass.ds(u * UNROLL, UNROLL)
                    dve.tensor_copy(stat4[:, 0], g.mean_all[:, group]).then_inc(staged, 1)
                    dve.tensor_copy(stat4[:, 1], g.rstd_all[:, group]).then_inc(staged, 1)
                    dve.tensor_copy(slot4[:, :, :], g.slot[:, group, :]).then_inc(staged, 1)
                    dve.wait_ge(staged, u * 3 + 3)
                after(dve, x_turned, i - UNROLL + 1)
                dve.tensor_scalar(rows[:, place, :], g.x[:, i, :], stat4[:, 0, place:place + 1], stat4[:, 1, place:place + 1],
                                  ALU.subtract, ALU.mult).then_inc(rows_ready, 1)

            make_rows(0, 0, 0)
            make_rows(1, 1, 0)
            keep_x(0, 0)

            def steps(i, place, u, kind):
                j = place % 2
                if is_own(i + 2, kind):
                    make_rows(i + 2, (place + 2) % UNROLL, u + (place + 2) // UNROLL)
                if kind or i < N:
                    for half in range(2):
                        dve.wait_ge(gated, 2 * i + half + 1)
                        dve.wait_ge(up_done, 4 * i + 2 * half + 2)
                        after(dve, h_turned, i)
                        dve.tensor_tensor(h[:, half * H:(half + 1) * H], act_g[:, :], up_ps[:, 2 * half + 1, 0:H],
                                          ALU.mult).then_inc(h_kept, 1)
                        if half == 0 and (kind or i + 1 < N):
                            keep_x(i + 1, 1 - j)
                if kind or 2 <= i:
                    dve.wait_ge(y_done, i - 1)
                    if is_own(i - 2, kind):
                        xt = g.x[:, i - 2, :]
                        dve.tensor_tensor(xt, y_ps[:, 0:D], xt, ALU.add).then_inc(y_kept, 1)
                    else:
                        if kind or i - OWN >= 4:
                            dve.wait_ge(y_out[j], (i - OWN - j) * 8 - 16)
                        dve.tensor_copy(y[:, j, :], y_ps[:, 0:D]).then_inc(y_kept, 1)
            over_tiles(dve, N, steps, OWN)


def l1_ffn(nc, io, g, out):
    route(nc, io, g, "r1", True, "L1_ffn_gate_w", None, 1e-20, False)
    l1_experts(nc, io, g)
    combine(nc, g, "m1", out)


def l1_attention(nc, io, g):
    HEADS, HD, GH = 16, 16, 4
    G = HEADS // GH
    AHEAD = 2
    UNITS = 3 * GH
    PARTS = 4 * HD
    ROW_J, ROW_I, ROW_M = PARTS, 96, 98
    NEG = -1e30
    Q_UNITS = (((3, 0),), ((2, 0), (0, 3 * P)), ((1, 0),))
    K_UNITS = (((0, 0),), ((1, 0), (3, 3 * P)), ((2, 0),))
    K_AT = {t: u * BANK + off for u, unit in enumerate(K_UNITS) for t, off in unit}
    HEAD_COLS = TB * (TB + 1) // 2 * P
    with ExitStack() as ctx:
        sb = lambda name, shape, dt=F32: ctx.enter_context(nc.sbuf_tensor("a1_" + name, shape, dt))
        sem = lambda name: g.stage_semaphore("a1_" + name)
        ps = lambda name, shape: ctx.enter_context(nc.psum_tensor("a1_" + name, shape, F32))
        work = ps("work", [P, 2, BANK])
        s_ps, st_ps = ps("s_ps", [P, 2, BANK]), ps("st_ps", [P, 2, BANK])
        o_ps, m_ps = ps("o_ps", [P, BANK]), ps("m_ps", [P, BANK])
        norm = Norm(nc, ctx, g, "a1", work)
        w = sb("w", [P, KT, 3 * D])
        w_qk = sb("w_qk", [P, KT, 2, KT, P])
        bias = sb("bias", [P, 2, KT])
        bv = sb("bv", [P, D])
        w_out, b_out = sb("w_out", [P, KT, D]), sb("b_out", [P, D])
        hi, lo = sb("hi", [P, 2, KT, S], F32R), sb("lo", [P, 2, KT, S], F32R)
        qs, ks = sb("qs", [P, HEADS, S], F32R), sb("ks", [P, HEADS, S], F32R)
        v = sb("v", [P, TB, HEADS, 2 * HD])
        slope, slope_hi, slope_lo = sb("slope", [1, HEADS]), sb("slope_hi", [1, HEADS], F32R), sb("slope_lo", [1, HEADS], F32R)
        slope2 = sb("slope2", [P, HEADS], F32R)
        count_i, count = sb("count_i", [P, S], I32), sb("count", [P, S])
        causal = sb("causal", [P, S])
        causalT = sb("causalT", [P, P], F32R)
        causalT_f = sb("causalT_f", [P, P])
        ident_r = sb("ident_r", [P, P], F32R)
        most = sb("most", [P, 2, GH, TB])
        m_hi, m_lo = sb("m_hi", [GH * TB, 2, P], F32R), sb("m_lo", [GH * TB, 2, P], F32R)
        prob = sb("prob", [P, GH, HEAD_COLS])
        o_raw = sb("o_raw", [P, S])
        rinv = sb("rinv", [P, TB, GH])
        o, oT = sb("o", [P, TB, D]), sb("oT", [P, KT, S])

        loaded, ready, consts = sem("loaded"), sem("ready"), sem("consts")
        slopes_placed = sem("slopes_placed")
        qk_done, qk_hi, qk_lo = sem("qk_done"), sem("qk_hi"), sem("qk_lo")
        v_done, v_kept = sem("v_done"), sem("v_kept")
        s_done, max_done, m_turned, m_high, m_low = sem("s_done"), sem("max_done"), sem("m_turned"), sem("m_high"), sem("m_low")
        st_done, exp_done = sem("st_done"), sem("exp_done")
        o_done, o_kept, o_turned, rinv_done, o_normed = sem("o_done"), sem("o_kept"), sem("o_turned"), sem("rinv_done"), sem("o_normed")
        heads_turned, heads_kept, x_biased = sem("heads_turned"), sem("heads_kept"), sem("x_biased")
        w_done, x_done = sem("w_done"), sem("x_done")
        spread = [sem(f"spread{i}") for i in range(KT)]
        m_placed = [sem(f"m_placed{i}") for i in range(G)]
        rows_set = sem("rows_set")
        SPREAD, PLACED = 16 * 8, 16 * 2
        CONSTS, READY, ROWS_SET = 10, 7, 7
        LOADS = 16 * (1 + 4 + 1 + 1 + 1 + 1)


        def load(sp):
            sp.dma_start(w[:, :, :], io["L1_attn_W_kqv"].rearrange("(k p) e -> p k e", p=P)).then_inc(loaded, 16)
            for i in range(2):
                for k in range(KT):
                    at = (1 - i) * D + k * P
                    sp.dma_start(bias[:, i, k:k + 1], io["L1_attn_b_kqv"][at:at + P].rearrange("(h d) -> d h", d=HD),
                                 allow_slow_non_contiguous=True).then_inc(loaded, 16)
            sp.dma_start(bv[:, :], io["L1_attn_b_kqv"][2 * D:3 * D].partition_broadcast(P)).then_inc(loaded, 16)
            sp.dma_start(w_out[:, :, :], io["L1_attn_W_proj"].rearrange("(k p) e -> p k e", p=P)).then_inc(loaded, 16)
            sp.dma_start(b_out[:, :], io["L1_attn_b_proj"].partition_broadcast(P)).then_inc(loaded, 16)
            sp.dma_start(slope[:, :], io["L1_attn_slopes"].rearrange("(o h) -> o h", o=1)).then_inc(loaded, 16)
            sp.wait_ge(consts, 2)
            for r in (ROW_J, ROW_I):
                sp.dma_start(slope2[r:r + 1, :].bitcast(F32), slope_hi[:, :].bitcast(F32)).then_inc(slopes_placed, 16)
                sp.dma_start(slope2[r + 1:r + 2, :].bitcast(F32), slope_lo[:, :].bitcast(F32)).then_inc(slopes_placed, 16)

        def set_masks(pool):
            pool.memset(v[:, :, :, HD:], 0.0).then_inc(ready, 1)
            pool.wait_ge(ready, 1)
            pool.memset(v[:, :, :, HD:HD + 1], 1.0).then_inc(ready, 1)
            pool.iota(count_i[:, :], [[1, S]], base=0, channel_multiplier=0).then_inc(ready, 1)
            pool.memset(causal[:, :], 0.0).then_inc(ready, 1)
            pool.memset(causalT_f[:, :], 0.0).then_inc(ready, 1)
            pool.wait_ge(ready, 5)
            pool.affine_select(out=causal[:, S - P:], in_=causal[:, S - P:], compare_op=ALU.is_ge, fill=NEG, base=0,
                               pattern=[[-1, P]], channel_multiplier=1).then_inc(ready, 1)
            pool.affine_select(out=causalT_f[:, :], in_=causalT_f[:, :], compare_op=ALU.is_ge, fill=NEG, base=0,
                               pattern=[[1, P]], channel_multiplier=-1).then_inc(ready, 1)

        def set_rows(act):
            zeros = g.zero_row[:, 0:1].unsqueeze(2).broadcast_to([P, HEADS, S])
            act.activation(qs[:, :, :], zeros, ACT.Copy).then_inc(rows_set, 1)
            act.activation(ks[:, :, :], zeros, ACT.Copy).then_inc(rows_set, 1)
            act.wait_ge(rows_set, 2)
            act.activation(ks[ROW_I:ROW_M + 2, :, :], g.ones[ROW_I:ROW_M + 2, 0:1].unsqueeze(2).broadcast_to([4, HEADS, S]),
                           ACT.Copy).then_inc(rows_set, 1)
            act.wait_ge(rows_set, 3)
            act.wait_ge(slopes_placed, 64)
            act.wait_ge(consts, CONSTS)
            by_head = lambda r: slope2[r:r + 2, :].bitcast(F32).unsqueeze(2).broadcast_to([2, HEADS, S])
            by_place = lambda r: count[r:r + 2, :].unsqueeze(1).broadcast_to([2, HEADS, S])
            act.activation(qs[ROW_J:ROW_J + 2, :, :], by_head(ROW_J), ACT.Copy).then_inc(rows_set, 1)
            act.activation(ks[ROW_J:ROW_J + 2, :, :], by_place(ROW_J), ACT.Copy).then_inc(rows_set, 1)
            act.activation(qs[ROW_I:ROW_I + 2, :, :], by_place(ROW_I), ACT.Copy, scale=-1.0).then_inc(rows_set, 1)
            act.activation(ks[ROW_I:ROW_I + 2, :, :], by_head(ROW_I), ACT.Copy).then_inc(rows_set, 1)
            act.wait_ge(rows_set, ROWS_SET)

        def set_weights(dve):
            dve.wait_ge(loaded, LOADS)
            dve.tensor_copy(slope_hi[:, :], slope[:, :]).then_inc(consts, 1)
            dve.wait_ge(consts, 1)
            dve.tensor_tensor(slope_lo[:, :], slope[:, :], slope_hi[:, :].bitcast(F32), ALU.subtract).then_inc(consts, 1)
            for half in range(KT):
                for i, scale in enumerate((HD ** -0.5, 1.0)):
                    at = (1 - i) * D + half * P
                    dve.tensor_scalar(w_qk[:, :, i, half, :].rearrange("p k (d h) -> p k d h", d=HD),
                                      w[:, :, at:at + P].rearrange("p k (h d) -> p k d h", d=HD), scale, None, ALU.mult).then_inc(consts, 1)
            dve.tensor_scalar(bias[:, 0, :], bias[:, 0, :], HD ** -0.5, None, ALU.mult).then_inc(consts, 1)
            dve.wait_ge(ready, READY)
            dve.tensor_copy(causalT[:, :], causalT_f[:, :]).then_inc(consts, 1)
            dve.tensor_copy(ident_r[:, :], g.ident[:, :]).then_inc(consts, 1)
            dve.tensor_copy(count[:, :], count_i[:, :]).then_inc(consts, 1)

        combine(nc, g, "m0", beside=dict(sync=load, gpsimd=set_masks, scalar=set_rows, vector=set_weights))
        block = ctx.enter_context(nc.Block())

        @block.sync
        def _(sp):
            def spread_half(b, half):
                sp.wait_ge(qk_lo, 4 * b + 2 * half + 2)
                heads = slice(half * HEADS // 2, (half + 1) * HEADS // 2)
                for part in range(4):
                    rows = slice(part * HD, (part + 1) * HD)
                    for dst, src in ((qs, (hi, lo)[part % 2][:, 0]), (ks, (hi, lo)[part // 2][:, 1])):
                        sp.dma_start(dst[rows, heads, :].bitcast(F32), src[:, half, :].bitcast(F32)).then_inc(spread[half], 16)

            spread_half(0, 0)

            def body(b, nxt):
                for gr in range(G):
                    n = b * G + gr
                    sp.wait_ge(m_low, n + 1)
                    for i, part in enumerate((m_hi, m_lo)):
                        sp.dma_start(qs[ROW_M + i:ROW_M + i + 1, gr * GH:(gr + 1) * GH, :].rearrange("o h (t q) -> o (h t) q", t=TB).bitcast(F32),
                                     part[:, gr % 2, :].bitcast(F32)).then_inc(m_placed[gr], 16)
                    if gr == 0:
                        spread_half(b, 1)
                    if gr == 2 and nxt is not None:
                        spread_half(nxt, 0)
            over_sequences(sp, body)

        @block.gpsimd
        def _(pool):
            norm.gpsimd(0)

            def body(b, nxt):
                if isinstance(b, int) and b == 0:
                    pool.wait_ge(loaded, LOADS)
                pool.wait_ge(norm.rows_done, b * TB + TB)
                xb = g.x[:, bass.ds(b * TB, TB), :]
                pool.tensor_tensor(xb, xb, b_out[:, :].unsqueeze(1).broadcast_to([P, TB, D]), ALU.add).then_inc(x_biased, 1)
                if nxt is not None:
                    norm.gpsimd(nxt)
            over_sequences(pool, body)

        @block.tensor
        def _(pe):
            def project_qk(b):
                pe.wait_ge(norm.columns_done, b + 1)
                for i in range(4):
                    if i >= 2:
                        pe.wait_ge(qk_lo, 4 * b + i - 1)
                    for k in range(KT):
                        last = pe.matmul(work[:, i % 2, :], w_qk[:, k, i % 2, i // 2], norm.xnT[:, k, :], start=k == 0, stop=k == KT - 1)
                    last.then_inc(qk_done, 1)

            def project_v(b):
                pe.wait_ge(qk_lo, 4 * b + 4)
                for t in range(TB):
                    for k in range(KT):
                        last = pe.matmul(work[:, t // 2, (t % 2) * D:(t % 2 + 1) * D], norm.xnT[:, k, t * P:(t + 1) * P],
                                         w[:, k, 2 * D:], start=k == 0, stop=k == KT - 1)
                    if t % 2:
                        last.then_inc(v_done, 1)

            def score_by_query(b, gr, units):
                n = b * G + gr
                if 0 in units:
                    pe.wait_ge(spread[gr // 2], SPREAD * (b + 1))
                for u in units:
                    head = gr * GH + u // 3
                    after(pe, max_done, UNITS * n + u - 1)
                    for t, off in Q_UNITS[u % 3]:
                        last = pe.matmul(s_ps[:, u % 2, off:off + (t + 1) * P], qs[0:ROW_M, head, t * P:(t + 1) * P],
                                         ks[0:ROW_M, head, 0:(t + 1) * P], start=True, stop=True)
                    last.then_inc(s_done, 1)

            def turn_maxima(b, gr):
                n = b * G + gr
                pe.wait_ge(max_done, UNITS * (n + 1))
                after(pe, o_normed, n - 1)
                pe.transpose(m_ps[0:GH * TB, 0:P], most[:, gr % 2].rearrange("p h t -> p (h t)"), g.ident[:, :]).then_inc(m_turned, 1)

            def score_by_key(b, gr, u):
                n = b * G + gr
                if u == 0:
                    pe.wait_ge(m_placed[gr], PLACED * (b + 1))
                head = gr * GH + u // 3
                after(pe, exp_done, UNITS * n + u - 1)
                for t, off in K_UNITS[u % 3]:
                    pe.matmul(st_ps[:, u % 2, off:off + S - t * P], ks[:, head, t * P:(t + 1) * P], qs[:, head, t * P:],
                              start=True, stop=False)
                    last = pe.matmul(st_ps[:, u % 2, off:off + P], ident_r[:, :], causalT[:, :], start=False, stop=True)
                last.then_inc(st_done, 1)

            def outputs(b, gr):
                n = b * G + gr
                pe.wait_ge(exp_done, UNITS * (n + 1))
                pe.wait_ge(v_kept, 2 * b + 2)
                after(pe, o_kept, n)
                for t in range(TB):
                    for h in range(GH):
                        r = 2 * HD * h
                        last = pe.matmul(o_ps[r:r + 2 * HD, t * P:], v[:, t, gr * GH + h, :],
                                         prob[:, h, K_AT[t]:K_AT[t] + S - t * P], start=t == 0, stop=t == TB - 1)
                last.then_inc(o_done, 1)

            def turn_outputs(b, gr):
                n = b * G + gr
                pe.wait_ge(o_kept, n + 1)
                after(pe, m_low, min(n + 2, B * G) if isinstance(n, int) else n + 2)
                after(pe, o_normed, n)
                for t in range(TB):
                    last = pe.transpose(m_ps[:, t * P:(t + 1) * P], o_raw[:, t * P:(t + 1) * P], g.ident[:, :])
                last.then_inc(o_turned, 1)

            def turn_heads(b, nxt):
                pe.wait_ge(o_normed, G * (b + 1))
                if nxt is not None:
                    pe.wait_ge(v_kept, 2 * b + 4)
                for k in range(KT):
                    for t in range(TB):
                        last = pe.transpose(work[:, k, t * P:(t + 1) * P], o[:, t, k * P:(k + 1) * P], g.ident[:, :])
                last.then_inc(heads_turned, 1)

            def project_out(b):
                pe.wait_ge(heads_kept, b + 1)
                for t in range(TB):
                    for k in range(KT):
                        last = pe.matmul(work[:, t // 2, (t % 2) * D:(t % 2 + 1) * D], oT[:, k, t * P:(t + 1) * P], w_out[:, k, :],
                                         start=k == 0, stop=k == KT - 1)
                    if t % 2:
                        last.then_inc(w_done, 1)

            pe.wait_ge(loaded, LOADS)
            pe.wait_ge(consts, CONSTS)
            pe.wait_ge(ready, READY)
            norm.tensor(0)
            project_qk(0)
            score_by_query(0, 0, range(UNITS))

            def body(b, nxt):
                first = isinstance(b, int) and b == 0
                for gr in range(G):
                    before = (b, gr - 1) if gr else (b - 1, G - 1)
                    following = (b, gr + 1) if gr < G - 1 else (nxt, 0)
                    turn_maxima(b, gr)
                    if following[0] is not None:
                        score_by_query(*following, range(AHEAD))
                    if gr == 1 and not first:
                        turn_heads(b - 1, b)
                    if gr or not first:
                        outputs(*before)
                    if gr == 0:
                        project_v(b)
                    if gr == 1:
                        if not first:
                            project_out(b - 1)
                        if nxt is not None:
                            norm.tensor(nxt, free=[(x_done, 2 * b), (v_kept, 2 * b + 2)])
                    if gr == 2 and nxt is not None:
                        project_qk(nxt)
                    if gr or not first:
                        turn_outputs(*before)
                    for u in range(UNITS):
                        score_by_key(b, gr, u)
                        if following[0] is not None and u + AHEAD < UNITS:
                            score_by_query(*following, [u + AHEAD])
            over_sequences(pe, body)
            outputs(B - 1, G - 1)
            turn_outputs(B - 1, G - 1)
            turn_heads(B - 1, None)
            project_out(B - 1)

        @block.scalar
        def _(act):
            def high_qk(b):
                for i in range(4):
                    act.wait_ge(qk_done, 4 * b + i + 1)
                    if i == 0:
                        for s in spread:
                            after(act, s, SPREAD * b)
                    act.activation(hi[:, i % 2, i // 2, :], work[:, i % 2, :], ACT.Identity,
                                   bias=bias[:, i % 2, i // 2:i // 2 + 1]).then_inc(qk_hi, 1)

            def high_maxima(b, gr):
                n = b * G + gr
                act.wait_ge(m_turned, n + 1)
                after(act, m_placed[(gr - 2) % G], PLACED * (b + (gr >= 2)))
                act.activation(m_hi[:, gr % 2, :], m_ps[0:GH * TB, 0:P], ACT.Copy, scale=-1.0).then_inc(m_high, 1)

            def exponentials(b, gr):
                n = b * G + gr
                after(act, o_done, n)
                for u in range(UNITS):
                    cols = sum((TB - t) * P for t, _ in K_UNITS[u % 3])
                    act.wait_ge(st_done, UNITS * n + u + 1)
                    act.activation(prob[:, u // 3, (u % 3) * BANK:(u % 3) * BANK + cols], st_ps[:, u % 2, 0:cols], ACT.Exp).then_inc(exp_done, 1)

            def keep_outputs(b, gr):
                n = b * G + gr
                act.wait_ge(o_done, n + 1)
                after(act, o_turned, n)
                act.activation(o_raw[:, :], o_ps[:, :], ACT.Copy).then_inc(o_kept, 1)

            def keep_heads(b):
                act.wait_ge(heads_turned, b + 1)
                after(act, w_done, 2 * b)
                act.activation(oT[:, :, :], work[:, :, :], ACT.Copy).then_inc(heads_kept, 1)

            act.wait_ge(loaded, LOADS)
            act.wait_ge(consts, CONSTS)
            norm.scalar(0)
            high_qk(0)

            def body(b, nxt):
                for gr in range(G):
                    first = isinstance(b, int) and b == 0
                    high_maxima(b, gr)
                    if gr == 1 and not first:
                        keep_heads(b - 1)
                    if gr:
                        keep_outputs(b, gr - 1)
                    elif not first:
                        keep_outputs(b - 1, G - 1)
                    if gr == 1 and nxt is not None:
                        norm.scalar(nxt, free=[(v_done, 2 * b + 2)])
                    if gr == 2 and nxt is not None:
                        high_qk(nxt)
                    exponentials(b, gr)
            over_sequences(act, body)
            keep_outputs(B - 1, G - 1)
            keep_heads(B - 1)

        @block.vector
        def _(dve):
            def low_qk(b):
                for i in range(4):
                    dve.wait_ge(qk_hi, 4 * b + i + 1)
                    part = hi[:, i % 2, i // 2, :].bitcast(F32)
                    dve.scalar_tensor_tensor(out=lo[:, i % 2, i // 2, :], in0=work[:, i % 2, :], scalar=bias[:, i % 2, i // 2:i // 2 + 1],
                                             in1=part, op0=ALU.add, op1=ALU.subtract).then_inc(qk_lo, 1)

            def maxima(b, gr, units=range(UNITS)):
                n = b * G + gr
                if 0 in units:
                    after(dve, m_turned, n - 1)
                for u in units:
                    wait_apart(dve, s_done, UNITS * n + u + 1, (ready, READY))
                    for t, off in Q_UNITS[u % 3]:
                        cols = (t + 1) * P
                        last = dve.tensor_tensor_reduce(s_ps[:, u % 2, off:off + cols], s_ps[:, u % 2, off:off + cols], causal[:, S - cols:], 1.0,
                                                        -3.0e38, ALU.add, ALU.max, most[:, gr % 2, u // 3, t:t + 1])
                    last.then_inc(max_done, 1)

            def low_maxima(b, gr):
                n = b * G + gr
                dve.wait_ge(m_high, n + 1)
                dve.scalar_tensor_tensor(out=m_lo[:, gr % 2, :], in0=m_ps[0:GH * TB, 0:P], scalar=-1.0,
                                         in1=m_hi[:, gr % 2, :].bitcast(F32), op0=ALU.mult, op1=ALU.subtract).then_inc(m_low, 1)

            def keep_values(b):
                for i in range(2):
                    dve.wait_ge(v_done, 2 * b + i + 1)
                    after(dve, o_done, G * b)
                    dve.tensor_tensor(v[:, 2 * i:2 * i + 2, :, 0:HD], work[:, i, :].rearrange("p (t h d) -> p t h d", t=2, h=HEADS),
                                      bv[:, :].rearrange("p (h d) -> p h d", h=HEADS).unsqueeze(1).broadcast_to([P, 2, HEADS, HD]),
                                      ALU.add).then_inc(v_kept, 1)

            def normalise(b, gr):
                n = b * G + gr
                four = m_ps[:, :].rearrange("p (t h d) -> p t h d", t=TB, h=GH)
                dve.wait_ge(o_turned, n + 1)
                dve.reciprocal(rinv[:, :, :], four[:, :, :, HD]).then_inc(rinv_done, 1)
                dve.wait_ge(rinv_done, n + 1)
                after(dve, heads_turned, b)
                dve.tensor_tensor(o[:, :, gr * GH * HD:(gr + 1) * GH * HD].rearrange("p t (h d) -> p t h d", h=GH), four[:, :, :, 0:HD],
                                  rinv[:, :, :].unsqueeze(3).broadcast_to([P, TB, GH, HD]), ALU.mult).then_inc(o_normed, 1)

            def add_to_x(b):
                for i in range(2):
                    dve.wait_ge(w_done, 2 * b + i + 1)
                    dve.wait_ge(x_biased, b + 1)
                    xt = g.x[:, bass.ds(b * TB + 2 * i, 2), :]
                    dve.tensor_tensor(xt, work[:, i, :].rearrange("p (t d) -> p t d", t=2), xt, ALU.add).then_inc(x_done, 1)

            norm.vector_stats(0)
            norm.vector_rows(0)
            low_qk(0)
            maxima(0, 0)

            def body(b, nxt):
                first = isinstance(b, int) and b == 0
                for gr in range(G):
                    before = (b, gr - 1) if gr else (b - 1, G - 1)
                    following = (b, gr + 1) if gr < G - 1 else (nxt, 0)
                    low_maxima(b, gr)
                    if following[0] is not None:
                        maxima(*following, range(AHEAD))
                    if gr == 0:
                        if nxt is not None:
                            norm.vector_stats(nxt)
                        keep_values(b)
                    if gr == 1 and nxt is not None:
                        norm.vector_rows(nxt)
                    if gr == 1 and not first:
                        add_to_x(b - 1)
                    if gr == 2 and nxt is not None:
                        low_qk(nxt)
                    if gr or not first:
                        normalise(*before)
                    if following[0] is not None:
                        maxima(*following, range(AHEAD, UNITS))
            over_sequences(dve, body)
            normalise(B - 1, G - 1)
            add_to_x(B - 1)


def l1_cross_attention(nc, io, g):
    with ExitStack() as ctx:
        sb = lambda name, shape, dt=F32: ctx.enter_context(nc.sbuf_tensor("c1_" + name, shape, dt))
        sem = lambda name: g.stage_semaphore("c1_" + name)
        ps = lambda name, shape: ctx.enter_context(nc.psum_tensor("c1_" + name, shape, F32))
        turn = ps("turn", [P, KT, S])
        sim_ps, at_ps, small = ps("sim_ps", [P, BANK]), ps("at_ps", [P, S]), ps("small", [P, BANK])
        out_ps = ps("out_ps", [P, 2, BANK])
        norm = Norm(nc, ctx, g, "c1", turn, depth=2)
        w = sb("w", [P, 4, KT, D])
        w_sim, b_sim = sb("w_sim", [P, 3, KT]), sb("b_sim", [P, 1])
        w2_wide = sb("w2_wide", [P, KT, P])
        key = sb("key", [P, KT, B * SC])
        key_bias = sb("key_bias", [P, B * SC])
        cw2 = sb("cw2", [P, B, D])
        c_rows = sb("c_rows", [P, D])
        sim = sb("sim", [P, TB, SC])
        least, total, share = (sb(n, [P, TB]) for n in ("least", "total", "share"))
        tile_least, all_least, shift = sb("tile_least", [P, 1]), sb("all_least", [1, 1]), sb("shift", [P, 1])
        att = sb("att", [P, TB, P])
        attT = sb("attT", [P, S])
        weight = sb("weight", [P, TB])
        weight_sum, weight_inv, hbar = sb("weight_sum", [P, 1]), sb("weight_inv", [P, 1]), sb("hbar", [P, KT])
        acT, prodT = sb("acT", [P, KT, S]), sb("prodT", [P, KT, S])
        w14 = sb("w14", [P, KT, D])

        loaded, ready, consts = sem("loaded"), sem("ready"), sem("consts")
        bias_done, bias_kept, cw2_done, cw2_kept, b_loaded = (sem(n) for n in ("bias_done", "bias_kept", "cw2_done", "cw2_kept", "b_loaded"))
        c_loaded = sem("c_loaded")
        sim_done, sim_kept, least_done, tile_done = sem("sim_done"), sem("sim_kept"), sem("least_done"), sem("tile_done")
        exp_done, total_done, share_done, att_done = sem("exp_done"), sem("total_done"), sem("share_done"), sem("att_done")
        tile_turned, all_done, all_spread, shift_done = sem("tile_turned"), sem("all_done"), sem("all_spread"), sem("shift_done")
        weight_done, hbar_done, hsum_done, hinv_done, hbar_kept, w14_done = (sem(n) for n in (
            "weight_done", "hbar_done", "hsum_done", "hinv_done", "hbar_kept", "w14_done"))
        att_turned, attT_kept, ac_done, ac_kept, prod_done = (sem(n) for n in (
            "att_turned", "attT_kept", "ac_done", "ac_kept", "prod_done"))
        out_done, x_done = sem("out_done"), sem("x_done")
        block = ctx.enter_context(nc.Block())
        ROW_AT, SHIFT_AT, SUM_AT, HBAR_AT = 0, P, P + 8, P + 16

        @block.sync
        def _(sp):
            sp.dma_start(w_sim[:, :, :], io["L1_xattn_w_sim"].rearrange("(f k p) -> p f k", f=3, p=P),
                         allow_slow_non_contiguous=True).then_inc(loaded, 16)
            sp.dma_start(b_sim[:, :], io["L1_xattn_b_sim"].partition_broadcast(P)).then_inc(loaded, 16)
            sp.dma_start(w[:, :, :, :], io["L1_xattn_W_qv"].rearrange("(f k p) e -> p f k e", f=4, p=P)).then_inc(loaded, 16)
            sp.wait_ge(ready, 3)
            sp.dma_start(cw2[SC:SC + 1, :, :], io["L1_xattn_b_qv"].rearrange("(o q d) -> o q d", o=1, q=1).broadcast_to([1, B, D])).then_inc(b_loaded, 16)

            def body(b, nxt):
                after(sp, ac_done, b)
                sp.dma_start(c_rows[0:SC, :], io["ctx_1024"][b]).then_inc(c_loaded, 16)
            over_sequences(sp, body)

        @block.gpsimd
        def _(pool):
            pool.memset(cw2[:, :, :], 0.0).then_inc(ready, 1)
            pool.memset(c_rows[:, :], 0.0).then_inc(ready, 1)
            pool.memset(att[:, :, SC:], 0.0).then_inc(ready, 1)
            pool.wait_ge(ready, 3)
            pool.memset(att[:, :, SC:SC + 1], 1.0).then_inc(ready, 1)

            def attend(b):
                pool.wait_ge(share_done, b + 1)
                pool.tensor_tensor(att[:, :, 0:SC], att[:, :, 0:SC], share[:, :].unsqueeze(2).broadcast_to([P, TB, SC]),
                                   ALU.mult).then_inc(att_done, 1)

            norm.gpsimd(0)
            norm.gpsimd(1)
            attend(0)

            def body(b, j):
                if within(b + 1):
                    attend(b + 1)
                if within(b + 2):
                    norm.gpsimd(b + 2)
            over_pairs(pool, body)

        @block.tensor
        def _(pe):
            pe.wait_ge(loaded, 48)
            pe.wait_ge(consts, 4)
            for k in range(KT):
                last = pe.matmul(turn[:, 0, :], w2_wide[:, k, :], g.ctxT[:, k, :], start=k == 0, stop=k == KT - 1)
            last.then_inc(bias_done, 1)
            for i in range(B):
                if i == 4:
                    pe.wait_ge(cw2_kept, 1)
                for k in range(KT):
                    last = pe.matmul(out_ps[0:SC, (i % 4) // 2, (i % 2) * D:(i % 2 + 1) * D], g.ctxT[:, k, i * SC:(i + 1) * SC], w[:, 1, k, :],
                                     start=k == 0, stop=k == KT - 1)
                if i % 4 == 3:
                    last.then_inc(cw2_done, 1)

            def similarity(b, j):
                pe.wait_ge(norm.columns_done, b + 1)
                after(pe, sim_kept, b)
                for t in range(TB):
                    for k in range(KT):
                        last = pe.matmul(sim_ps[:, t * SC:(t + 1) * SC], norm.columns[j][:, k, t * P:(t + 1) * P],
                                         key[:, k, bass.ds(b * SC, SC)], start=k == 0, stop=k == KT - 1)
                last.then_inc(sim_done, 1)

            def turn_least(b):
                pe.wait_ge(tile_done, b + 1)
                after(pe, hbar_kept, b)
                pe.matmul(small[0:1, ROW_AT:ROW_AT + P], tile_least[:, :], g.ident[:, :], start=True, stop=True).then_inc(tile_turned, 1)

            def spread_least(b):
                pe.wait_ge(all_done, b + 1)
                pe.matmul(small[:, SHIFT_AT:SHIFT_AT + 1], g.ones[0:1, :], all_least[:, :], start=True, stop=True).then_inc(all_spread, 1)

            def turn_attention(b):
                pe.wait_ge(att_done, b + 1)
                after(pe, attT_kept, b)
                for t in range(TB):
                    last = pe.transpose(at_ps[:, t * P:(t + 1) * P], att[:, t, :], g.ident[:, :])
                last.then_inc(att_turned, 1)

            def weighted_mean(b, j):
                pe.wait_ge(weight_done, b + 1)
                pe.matmul(small[:, SUM_AT:SUM_AT + TB], g.ones[:, :], weight[:, :], start=True, stop=True)
                for k in range(KT):
                    for t in range(TB):
                        last = pe.matmul(small[:, HBAR_AT + k:HBAR_AT + k + 1], norm.rows[j][:, t, k * P:(k + 1) * P], weight[:, t:t + 1],
                                         start=t == 0, stop=t == TB - 1)
                last.then_inc(hbar_done, 1)

            def attended(b):
                pe.wait_ge(attT_kept, b + 1)
                pe.wait_ge(c_loaded, (b + 1) * 16)
                for k in range(KT):
                    last = pe.matmul(turn[:, k, :], c_rows[:, k * P:(k + 1) * P], attT[:, :], start=True, stop=True)
                last.then_inc(ac_done, 1)

            def output(b, j, t):
                bank = out_ps[:, t // 2, (t % 2) * D:(t % 2 + 1) * D]
                if t % 2 == 0:
                    after(pe, x_done, b * 2 - 1 + t // 2)
                tile = slice(t * P, (t + 1) * P)
                pe.matmul(bank, attT[:, tile], cw2[:, b, :], start=True, stop=False)
                if t == 0:
                    pe.wait_ge(w14_done, (b + 1) * KT)
                for k in range(KT):
                    pe.matmul(bank, norm.columns[j][:, k, tile], w14[:, k, :], start=False, stop=False)
                if t == 0:
                    pe.wait_ge(prod_done, b + 1)
                for k in range(KT):
                    last = pe.matmul(bank, prodT[:, k, tile], w[:, 2, k, :], start=False, stop=k == KT - 1)
                if t % 2:
                    last.then_inc(out_done, 1)

            norm.tensor(0, free=[(bias_kept, 1)])
            similarity(0, 0)
            turn_least(0)
            spread_least(0)
            turn_attention(0)
            weighted_mean(0, 0)
            pe.wait_ge(cw2_kept, 2)
            pe.wait_ge(b_loaded, 16)

            def body(b, j):
                ahead = within(b + 1)
                attended(b)
                if ahead:
                    norm.tensor(b + 1, free=[(ac_kept, b + 1)], buf=1 - j)
                output(b, j, 0)
                if ahead:
                    similarity(b + 1, 1 - j)
                output(b, j, 1)
                if ahead:
                    turn_least(b + 1)
                output(b, j, 2)
                if ahead:
                    spread_least(b + 1)
                output(b, j, 3)
                if ahead:
                    turn_attention(b + 1)
                    weighted_mean(b + 1, 1 - j)
            over_pairs(pe, body)

        @block.scalar
        def _(act):
            act.wait_ge(ready, 4)
            for i in range(2):
                act.wait_ge(cw2_done, i + 1)
                act.activation(cw2[0:SC, 4 * i:4 * i + 4, :].rearrange("p (a c) d -> p a (c d)", a=2), out_ps[0:SC, :, :], ACT.Copy).then_inc(cw2_kept, 1)

            def exponentials(b):
                act.wait_ge(least_done, b + 1)
                after(act, att_turned, b)
                for t in range(TB):
                    act.activation(att[:, t, 0:SC], sim[:, t, :], ACT.Exp, bias=least[:, t:t + 1]).then_inc(exp_done, 1)

            def weights(b):
                act.wait_ge(shift_done, b + 1)
                after(act, hbar_done, b)
                act.activation(weight[:, :], least[:, :], ACT.Exp, bias=shift[:, 0:1], scale=-1.0).then_inc(weight_done, 1)

            def keep_attT(b):
                act.wait_ge(att_turned, b + 1)
                after(act, out_done, b * 2)
                act.activation(attT[:, :], at_ps[:, :], ACT.Copy).then_inc(attT_kept, 1)

            norm.scalar(0)
            exponentials(0)
            weights(0)
            keep_attT(0)

            def body(b, j):
                act.wait_ge(ac_done, b + 1)
                after(act, prod_done, b)
                act.activation(acT[:, :, :], turn[:, :, :], ACT.Copy).then_inc(ac_kept, 1)
                if within(b + 1):
                    norm.scalar(b + 1, free=[(out_done, b * 2)], buf=1 - j)
                    exponentials(b + 1)
                    weights(b + 1)
                    keep_attT(b + 1)
            over_pairs(act, body)

        @block.vector
        def _(dve):
            dve.wait_ge(loaded, 48)
            for k in range(KT):
                dve.tensor_scalar(w2_wide[:, k, :], g.ones[:, :], w_sim[:, 1, k:k + 1], None, ALU.mult).then_inc(consts, 1)
                dve.tensor_scalar(key[:, k, :], g.ctxT[:, k, :], w_sim[:, 2, k:k + 1], w_sim[:, 0, k:k + 1], ALU.mult, ALU.add).then_inc(consts, 1)
            norm.vector_stats(0)
            norm.vector_rows(0, buf=0)
            dve.wait_ge(bias_done, 1)
            dve.tensor_scalar(key_bias[:, :], turn[:, 0, :], b_sim[:, 0:1], None, ALU.add).then_inc(bias_kept, 1)
            dve.wait_ge(bias_kept, 1)
            norm.vector_stats(1)
            norm.vector_rows(1, buf=1)

            def maxima(b):
                dve.wait_ge(sim_done, b + 1)
                after(dve, exp_done, b * TB)
                dve.tensor_tensor(sim[:, :, :], sim_ps[:, 0:TB * SC].rearrange("p (t j) -> p t j", t=TB),
                                  key_bias[:, bass.ds(b * SC, SC)].unsqueeze(1).broadcast_to([P, TB, SC]), ALU.add).then_inc(sim_kept, 1)
                dve.wait_ge(sim_kept, b + 1)
                after(dve, weight_done, b)
                dve.tensor_reduce(least[:, :], sim[:, :, :], AX.X, ALU.max, negate=True).then_inc(least_done, 1)
                dve.wait_ge(least_done, b + 1)
                after(dve, tile_turned, b)
                dve.tensor_reduce(tile_least[:, :], least[:, :], AX.X, ALU.min).then_inc(tile_done, 1)

            def shares(b):
                dve.wait_ge(exp_done, (b + 1) * TB)
                dve.tensor_reduce(total[:, :], att[:, :, 0:SC], AX.X, ALU.add).then_inc(total_done, 1)
                dve.wait_ge(total_done, b + 1)
                after(dve, att_done, b)
                dve.reciprocal(share[:, :], total[:, :]).then_inc(share_done, 1)

            def shifts(b):
                dve.wait_ge(tile_turned, b + 1)
                after(dve, all_spread, b)
                dve.tensor_reduce(all_least[:, :], small[0:1, ROW_AT:ROW_AT + P], AX.X, ALU.min).then_inc(all_done, 1)
                dve.wait_ge(all_spread, b + 1)
                after(dve, weight_done, b)
                dve.tensor_copy(shift[:, :], small[:, SHIFT_AT:SHIFT_AT + 1]).then_inc(shift_done, 1)

            maxima(0)
            shares(0)
            shifts(0)

            def body(b, j):
                dve.wait_ge(hbar_done, b + 1)
                dve.tensor_reduce(weight_sum[:, :], small[:, SUM_AT:SUM_AT + TB], AX.X, ALU.add).then_inc(hsum_done, 1)
                dve.wait_ge(hsum_done, b + 1)
                dve.reciprocal(weight_inv[:, :], weight_sum[:, :]).then_inc(hinv_done, 1)
                dve.wait_ge(hinv_done, b + 1)
                dve.tensor_scalar(hbar[:, :], small[:, HBAR_AT:HBAR_AT + KT], weight_inv[:, 0:1], None, ALU.mult).then_inc(hbar_kept, 1)
                dve.wait_ge(hbar_kept, b + 1)
                after(dve, out_done, b * 2)
                for k in range(KT):
                    dve.scalar_tensor_tensor(out=w14[:, k, :], in0=w[:, 3, k, :], scalar=hbar[:, k:k + 1], in1=w[:, 0, k, :],
                                             op0=ALU.mult, op1=ALU.add).then_inc(w14_done, 1)
                dve.wait_ge(ac_kept, b + 1)
                dve.tensor_tensor(prodT[:, :, :], acT[:, :, :], norm.columns[j][:, :, :], ALU.mult).then_inc(prod_done, 1)
                if within(b + 1):
                    maxima(b + 1)
                    shares(b + 1)
                    shifts(b + 1)
                if within(b + 2):
                    norm.vector_stats(b + 2)
                    norm.vector_rows(b + 2, free=[(hbar_done, b + 1)], buf=j)
                for i in range(2):
                    dve.wait_ge(out_done, b * 2 + i + 1)
                    xt = g.x[:, bass.ds(b * TB + 2 * i, 2), :]
                    dve.tensor_tensor(xt, out_ps[:, i, :].rearrange("p (t d) -> p t d", t=2), xt, ALU.add).then_inc(x_done, 1)
            over_pairs(dve, body)


def build(nc, io, out):
    with ExitStack() as ctx:
        g = setup(nc, ctx, io)
        g.end_stage()
        with ExitStack() as attention:
            load_context(nc, attention, io, g)
            for stage in (l0_attention, l0_cross_attention, l0_ffn, l1_attention, l1_cross_attention):
                stage(nc, io, g)
                g.end_stage()
        l1_ffn(nc, io, g, out)


_INS = ['x', 'ctx_1024', 'mask_Bx1xSxS2_bk1', 'L0_attn_Wq', 'L0_attn_bq', 'L0_attn_Wk', 'L0_attn_bk', 'L0_attn_Wv',
        'L0_attn_bv', 'L0_xattn_Wq', 'L0_xattn_Wk', 'L0_xattn_Wv', 'L0_xattn_Wo', 'L0_ffn_router_w', 'L0_ffn_router_b',
        'L0_ffn_w1', 'L0_ffn_b1', 'L0_ffn_w2', 'L0_ffn_b2', 'L1_attn_W_kqv', 'L1_attn_b_kqv', 'L1_attn_W_proj',
        'L1_attn_b_proj', 'L1_attn_slopes', 'L1_xattn_w_sim', 'L1_xattn_b_sim', 'L1_xattn_W_qv', 'L1_xattn_b_qv',
        'L1_ffn_gate_w', 'L1_ffn_wg', 'L1_ffn_wu', 'L1_ffn_wd', 'L1_ffn_sg', 'L1_ffn_su', 'L1_ffn_sd']


def kernel(**inputs):
    import numpy as _np
    import concourse.bacc as _bacc
    from concourse import mybir as _mybir
    from concourse.bass_utils import run_bass_kernel_spmd as _run

    nc = _bacc.Bacc("TRN2", target_bir_lowering=False, num_devices=1)
    arrays, io = {}, {}
    for name in _INS:
        a = _np.ascontiguousarray(inputs[name])
        arrays[f"in_{name}"] = a
        io[name] = nc.dram_tensor(f"in_{name}", a.shape, _mybir.dt.from_np(a.dtype), kind="ExternalInput").ap()
    out = nc.dram_tensor("out", (8, 512, 256), _mybir.dt.float32, kind="ExternalOutput").ap()
    build(nc, io, out)
    r = _run(nc, [arrays], core_ids=[0])
    return r.results[0]["out"]
```
